# Optimizing a Trainium2 kernel written in Bass

```python
import numpy as np
import jax
import jax.numpy as jnp

def _softmax(x, axis=-1):
    return jax.nn.softmax(x, axis=axis)

def _gelu(x):
    return jax.nn.gelu(x, approximate=True)

def _silu(x):
    return jax.nn.silu(x)

def _sigmoid(x):
    return jax.nn.sigmoid(x)

def _layernorm(x, axis=-1, eps=1e-05):
    m = jnp.mean(x, axis=axis, keepdims=True)
    v = jnp.var(x, axis=axis, keepdims=True)
    return (x - m) / jnp.sqrt(v + eps)

def _scatter_add(tgt, idx, src, axis=0):
    return tgt.at[idx].add(src)

def _segment_sum(src, seg, n):
    return jax.ops.segment_sum(src, seg, n)
kernel_name = 'mk_prb_d4_jaxref_r8_dc145f'

def setup_inputs(seed: int=0):
    np.random.seed(seed)
    _w = jnp.asarray

    def _L0_attn_setup():
        import jax, jax.numpy as jnp
        import numpy as np
        EMB = 128
        HEADS = 16
        HD = EMB // HEADS
        B, N = (8, 128)
        key = jax.random.key(seed)
        ks = jax.random.split(key, 6)
        X = jax.random.normal(ks[0], (B, N, EMB), dtype=jnp.float32)
        s = 1.0 / np.sqrt(HD)
        Wq = jax.random.normal(ks[1], (HD, HD), dtype=jnp.float32) * s
        Wk = jax.random.normal(ks[2], (HD, HD), dtype=jnp.float32) * s
        Wv = jax.random.normal(ks[3], (HD, HD), dtype=jnp.float32) * s
        Wo = jax.random.normal(ks[4], (EMB, EMB), dtype=jnp.float32) * (1.0 / np.sqrt(EMB))
        bo = jnp.zeros((EMB,), dtype=jnp.float32)
        return {'X': X, 'Wq': Wq, 'Wk': Wk, 'Wv': Wv, 'Wo': Wo, 'bo': bo}
    _L0_attn_in = _L0_attn_setup()

    def _L0_ffn_setup():
        import jax, jax.numpy as jnp
        import numpy as np
        D_MODEL = 128
        MLP_DIM = 512
        N_EXPERTS = 8
        B, T = (4, 128)
        key = jax.random.key(seed)
        ks = jax.random.split(key, 7)
        scale_in = (1.0 / D_MODEL) ** 0.5
        scale_out = (1.0 / MLP_DIM) ** 0.5
        bound_g = (1.0 / D_MODEL) ** 0.5
        w_gate = jax.random.uniform(ks[0], (D_MODEL, N_EXPERTS), minval=-bound_g, maxval=bound_g, dtype=jnp.float32)
        b_gate = jax.random.uniform(ks[1], (N_EXPERTS,), minval=-bound_g, maxval=bound_g, dtype=jnp.float32)
        W1 = jax.random.uniform(ks[2], (N_EXPERTS, D_MODEL, MLP_DIM), minval=-scale_in, maxval=scale_in, dtype=jnp.float32)
        b1 = jnp.zeros((N_EXPERTS, MLP_DIM), dtype=jnp.float32)
        W2 = jax.random.uniform(ks[3], (N_EXPERTS, MLP_DIM, D_MODEL), minval=-scale_out, maxval=scale_out, dtype=jnp.float32)
        b2 = jnp.zeros((N_EXPERTS, D_MODEL), dtype=jnp.float32)
        x = jax.random.normal(ks[4], (B, T, D_MODEL), dtype=jnp.float32)
        return {'x': x, 'w_gate': w_gate, 'b_gate': b_gate, 'W1': W1, 'b1': b1, 'W2': W2, 'b2': b2}
    _L0_ffn_in = _L0_ffn_setup()

    def _L1_attn_setup():
        import jax, jax.numpy as jnp
        import numpy as np
        import math
        NUM_BUCKETS = 32
        MAX_DISTANCE = 128

        def _relative_position_bucket(relative_position):
            rp = jnp.maximum(-relative_position, 0)
            max_exact = NUM_BUCKETS // 2
            is_small = rp < max_exact
            rp_f = jnp.maximum(rp, 1).astype(jnp.float32)
            large = max_exact + (jnp.log(rp_f / max_exact) / math.log(MAX_DISTANCE / max_exact) * (NUM_BUCKETS - max_exact)).astype(jnp.int32)
            large = jnp.minimum(large, NUM_BUCKETS - 1)
            return jnp.where(is_small, rp, large)

        def _t5_rel_bias(bias_table, T):
            ctx = jnp.arange(T, dtype=jnp.int32)[:, None]
            mem = jnp.arange(T, dtype=jnp.int32)[None, :]
            buckets = _relative_position_bucket(mem - ctx)
            values = bias_table[buckets]
            return jnp.transpose(values, (2, 0, 1))[None]
        key = jax.random.key(seed)
        ks = jax.random.split(key, 6)
        B, T, C, H = (2, 256, 128, 16)
        x = jax.random.normal(ks[0], (B, T, C), dtype=jnp.float32)
        W_attn = jax.random.normal(ks[1], (C, 3 * C), dtype=jnp.float32) * 0.02
        b_attn = jnp.zeros((3 * C,), dtype=jnp.float32)
        W_proj = jax.random.normal(ks[2], (C, C), dtype=jnp.float32) * 0.02
        b_proj = jnp.zeros((C,), dtype=jnp.float32)
        bias_table = jax.random.normal(ks[3], (NUM_BUCKETS, H), dtype=jnp.float32) * 0.02
        return {'x': x, 'W_attn': W_attn, 'b_attn': b_attn, 'W_proj': W_proj, 'b_proj': b_proj, 'bias_table': bias_table}
    _L1_attn_in = _L1_attn_setup()

    def _L1_ffn_setup():
        import jax, jax.numpy as jnp
        import numpy as np
        D_MODEL = 128
        N_EXPERTS = 8
        TOP_K = 2
        key = jax.random.key(seed)
        ks = jax.random.split(key, 8)
        d, e = (D_MODEL, N_EXPERTS)
        s = 1.0 / np.sqrt(d)
        return {'x': jax.random.normal(ks[0], (4, 256, d), dtype=jnp.float32), 'W_gate': jax.random.uniform(ks[1], (d, e), jnp.float32, -s, s), 'b_gate': jax.random.uniform(ks[2], (e,), jnp.float32, -s, s), 'W1': jax.random.uniform(ks[3], (e, d, d), jnp.float32, -s, s), 'b1': jax.random.uniform(ks[4], (e, d), jnp.float32, -s, s), 'W2': jax.random.uniform(ks[5], (e, d, d), jnp.float32, -s, s), 'b2': jax.random.uniform(ks[6], (e, d), jnp.float32, -s, s)}
    _L1_ffn_in = _L1_ffn_setup()

    def _L2_attn_setup():
        import jax, jax.numpy as jnp
        import numpy as np
        B, T, C = (4, 512, 128)
        H = 16
        D = C // H
        W_SCALE = 0.02
        key = jax.random.key(seed)
        ks = jax.random.split(key, 9)
        inp = {'x': jax.random.normal(ks[0], (B, T, C), dtype=jnp.float32)}
        for i, nm in enumerate(['q', 'k', 'v', 'o']):
            inp[f'W{nm}'] = jax.random.normal(ks[1 + i], (C, C), dtype=jnp.float32) * W_SCALE
            inp[f'b{nm}'] = jnp.zeros((C,), dtype=jnp.float32)
        return inp
    _L2_attn_in = _L2_attn_setup()

    def _L2_ffn_setup():
        import jax, jax.numpy as jnp
        import numpy as np
        BLOCK = 16
        _GRID = jnp.array([0.0, 0.5, 1.0, 1.5, 2.0, 3.0, 4.0, 6.0], dtype=jnp.float32)
        _MID = jnp.array([0.25, 0.75, 1.25, 1.75, 2.5, 3.5, 5.0], dtype=jnp.float32)

        def fp4_quant_dequant(x):
            shape = x.shape
            xb = x.reshape(shape[:-1] + (shape[-1] // BLOCK, BLOCK))
            scale = jnp.max(jnp.abs(xb), axis=-1, keepdims=True) / 6.0
            scale = jnp.maximum(scale, jnp.float32(1e-12))
            xn = xb / scale
            idx = jnp.searchsorted(_MID, jnp.abs(xn))
            q = _GRID[idx] * jnp.sign(xn) * scale
            return q.reshape(shape)

        def fp4_linear(x, w):
            xq = fp4_quant_dequant(x)
            wq = fp4_quant_dequant(w)
            return jnp.einsum('bsk,nk->bsn', xq, wq)
        key = jax.random.key(seed)
        k1, k2, k3, k4 = jax.random.split(key, 4)
        H, I = (128, 352)
        x = jax.random.normal(k1, (4, 512, H), dtype=jnp.float32)
        w_gate = jax.random.normal(k2, (I, H), dtype=jnp.float32) * 0.02
        w_up = jax.random.normal(k3, (I, H), dtype=jnp.float32) * 0.02
        w_down = jax.random.normal(k4, (H, I), dtype=jnp.float32) * 0.02
        return {'x': x, 'w_gate': w_gate, 'w_up': w_up, 'w_down': w_down}
    _L2_ffn_in = _L2_ffn_setup()

    def _L3_attn_setup():
        import jax, jax.numpy as jnp
        import numpy as np
        DIM = 128
        G = 32
        QK = 128
        HID = 256
        NUM_BUCKETS = 32
        MAX_DIST = 128
        BIAS_SCALE = QK ** 0.5
        LN_EPS = 1e-05

        def t5_rel_bias(rel_table):
            pos = jnp.arange(G)
            rel = pos[None, :] - pos[:, None]
            n = jnp.maximum(-rel, 0)
            max_exact = NUM_BUCKETS // 2
            is_small = n < max_exact
            ln_ratio = np.log(MAX_DIST / max_exact)
            val_large = max_exact + (jnp.log(jnp.maximum(n, 1).astype(jnp.float32) / max_exact) / ln_ratio * (NUM_BUCKETS - max_exact)).astype(jnp.int32)
            val_large = jnp.minimum(val_large, NUM_BUCKETS - 1)
            bucket = jnp.where(is_small, n, val_large)
            return rel_table[bucket] * BIAS_SCALE
        key = jax.random.key(seed)
        ks = jax.random.split(key, 10)
        s = 0.02
        return {'x': jax.random.normal(ks[0], (4, 512, DIM), dtype=jnp.float32), 'ln_w': jnp.ones((DIM,), jnp.float32), 'ln_b': jnp.zeros((DIM,), jnp.float32), 'Wh': jax.random.normal(ks[1], (DIM, 2 * HID), jnp.float32) * s, 'bh': jnp.zeros((2 * HID,), jnp.float32), 'Wqk': jax.random.normal(ks[2], (DIM, QK), jnp.float32) * s, 'bqk': jnp.zeros((QK,), jnp.float32), 'qk_w': jax.random.normal(ks[3], (4, QK), jnp.float32) * s + 1.0, 'qk_b': jnp.zeros((4, QK), jnp.float32), 'rel_table': jax.random.normal(ks[4], (NUM_BUCKETS,), jnp.float32) * s, 'Wout': jax.random.normal(ks[5], (HID, DIM), jnp.float32) * s, 'bout': jnp.zeros((DIM,), jnp.float32)}
    _L3_attn_in = _L3_attn_setup()

    def _L3_ffn_setup():
        import jax, jax.numpy as jnp
        import numpy as np
        S, B, D, H, DH = (512, 8, 128, 16, 64)

        def _forward(x, Wg, Wq, bq, Wkv, bkv, Wo, bo, ln_g, ln_b):
            s_len, bsz, d_model = x.shape
            n_head, _, d_head = Wq.shape
            cap = s_len // n_head
            scale = 1.0 / d_head ** 0.5
            h = jnp.transpose(x, (1, 0, 2))
            t = h
            probs = jax.nn.softmax(h @ Wg, axis=-1)
            scores = jnp.transpose(probs, (0, 2, 1))
            _, idx = jax.lax.top_k(scores, cap)
            idx = jnp.sort(idx, axis=-1)
            hg = jnp.take_along_axis(h[:, None, :, :], idx[..., None], axis=2)
            hg = jnp.transpose(hg, (1, 0, 2, 3))
            q = jnp.einsum('hbcd,hde->hbce', hg, Wq) + bq[:, None, None, :]
            kv = jnp.einsum('hbcd,hde->hbce', hg, Wkv) + bkv[:, None, None, :]
            k, v = jnp.split(kv, 2, axis=-1)
            att = jnp.einsum('hbid,hbjd->hbij', q, k) * scale
            p = jax.nn.softmax(att, axis=1)
            av = jnp.einsum('hbij,hbjd->hbid', p, v)
            ao = jnp.einsum('hbid,hde->hbie', av, Wo) + bo
            tok = jnp.transpose(idx, (1, 0, 2))
            b_ids = jnp.arange(bsz)[None, :, None]
            outs = jnp.zeros_like(t).at[b_ids, tok].add(ao)
            y = t + outs
            mu = jnp.mean(y, axis=-1, keepdims=True)
            var = jnp.var(y, axis=-1, keepdims=True)
            yn = (y - mu) * jax.lax.rsqrt(var + 1e-05) * ln_g + ln_b
            return jnp.transpose(yn, (1, 0, 2))
        key = jax.random.key(seed)
        ks = jax.random.split(key, 6)
        s = 0.02
        return {'x': jax.random.normal(ks[0], (S, B, D), jnp.float32), 'attn_mask': jnp.zeros((S, S), jnp.bool_), 'Wg': jax.random.normal(ks[1], (D, H), jnp.float32) * s, 'Wq': jax.random.normal(ks[2], (H, D, DH), jnp.float32) * s, 'bq': jnp.zeros((H, DH), jnp.float32), 'Wkv': jax.random.normal(ks[3], (H, D, 2 * DH), jnp.float32) * s, 'bkv': jnp.zeros((H, 2 * DH), jnp.float32), 'Wo': jax.random.normal(ks[4], (H, DH, D), jnp.float32) * s, 'bo': jnp.zeros((D,), jnp.float32), 'ln_g': jnp.ones((D,), jnp.float32), 'ln_b': jnp.zeros((D,), jnp.float32)}
    _L3_ffn_in = _L3_ffn_setup()
    _d = {'L0_attn_X': _L0_attn_in['X'], 'L0_attn_Wq': _L0_attn_in['Wq'], 'L0_attn_Wk': _L0_attn_in['Wk'], 'L0_attn_Wv': _L0_attn_in['Wv'], 'L0_attn_Wo': _L0_attn_in['Wo'], 'L0_attn_bo': _L0_attn_in['bo'], 'L0_ffn_w_gate': _L0_ffn_in['w_gate'], 'L0_ffn_b_gate': _L0_ffn_in['b_gate'], 'L0_ffn_W1': _L0_ffn_in['W1'], 'L0_ffn_b1': _L0_ffn_in['b1'], 'L0_ffn_W2': _L0_ffn_in['W2'], 'L0_ffn_b2': _L0_ffn_in['b2'], 'L1_attn_W_attn': _L1_attn_in['W_attn'], 'L1_attn_b_attn': _L1_attn_in['b_attn'], 'L1_attn_W_proj': _L1_attn_in['W_proj'], 'L1_attn_b_proj': _L1_attn_in['b_proj'], 'L1_attn_bias_table': _L1_attn_in['bias_table'], 'L1_ffn_W_gate': _L1_ffn_in['W_gate'], 'L1_ffn_b_gate': _L1_ffn_in['b_gate'], 'L1_ffn_W1': _L1_ffn_in['W1'], 'L1_ffn_b1': _L1_ffn_in['b1'], 'L1_ffn_W2': _L1_ffn_in['W2'], 'L1_ffn_b2': _L1_ffn_in['b2'], 'L2_attn_Wq': _L2_attn_in['Wq'], 'L2_attn_bq': _L2_attn_in['bq'], 'L2_attn_Wk': _L2_attn_in['Wk'], 'L2_attn_bk': _L2_attn_in['bk'], 'L2_attn_Wv': _L2_attn_in['Wv'], 'L2_attn_bv': _L2_attn_in['bv'], 'L2_attn_Wo': _L2_attn_in['Wo'], 'L2_attn_bo': _L2_attn_in['bo'], 'L2_ffn_w_gate': _L2_ffn_in['w_gate'], 'L2_ffn_w_up': _L2_ffn_in['w_up'], 'L2_ffn_w_down': _L2_ffn_in['w_down'], 'L3_attn_ln_w': _L3_attn_in['ln_w'], 'L3_attn_ln_b': _L3_attn_in['ln_b'], 'L3_attn_Wh': _L3_attn_in['Wh'], 'L3_attn_bh': _L3_attn_in['bh'], 'L3_attn_Wqk': _L3_attn_in['Wqk'], 'L3_attn_bqk': _L3_attn_in['bqk'], 'L3_attn_qk_w': _L3_attn_in['qk_w'], 'L3_attn_qk_b': _L3_attn_in['qk_b'], 'L3_attn_rel_table': _L3_attn_in['rel_table'], 'L3_attn_Wout': _L3_attn_in['Wout'], 'L3_attn_bout': _L3_attn_in['bout'], 'L3_ffn_attn_mask': _L3_ffn_in['attn_mask'], 'L3_ffn_Wg': _L3_ffn_in['Wg'], 'L3_ffn_Wq': _L3_ffn_in['Wq'], 'L3_ffn_bq': _L3_ffn_in['bq'], 'L3_ffn_Wkv': _L3_ffn_in['Wkv'], 'L3_ffn_bkv': _L3_ffn_in['bkv'], 'L3_ffn_Wo': _L3_ffn_in['Wo'], 'L3_ffn_bo': _L3_ffn_in['bo'], 'L3_ffn_ln_g': _L3_ffn_in['ln_g'], 'L3_ffn_ln_b': _L3_ffn_in['ln_b']}
    _x0 = _d['L0_attn_X']
    _d['L0_attn_X'] = jax.random.normal(jax.random.fold_in(jax.random.key(seed), 1), (2, 1024, 128), dtype=_x0.dtype)
    del _x0
    return _d

def reference(L0_attn_X, L0_attn_Wq, L0_attn_Wk, L0_attn_Wv, L0_attn_Wo, L0_attn_bo, L0_ffn_w_gate, L0_ffn_b_gate, L0_ffn_W1, L0_ffn_b1, L0_ffn_W2, L0_ffn_b2, L1_attn_W_attn, L1_attn_b_attn, L1_attn_W_proj, L1_attn_b_proj, L1_attn_bias_table, L1_ffn_W_gate, L1_ffn_b_gate, L1_ffn_W1, L1_ffn_b1, L1_ffn_W2, L1_ffn_b2, L2_attn_Wq, L2_attn_bq, L2_attn_Wk, L2_attn_bk, L2_attn_Wv, L2_attn_bv, L2_attn_Wo, L2_attn_bo, L2_ffn_w_gate, L2_ffn_w_up, L2_ffn_w_down, L3_attn_ln_w, L3_attn_ln_b, L3_attn_Wh, L3_attn_bh, L3_attn_Wqk, L3_attn_bqk, L3_attn_qk_w, L3_attn_qk_b, L3_attn_rel_table, L3_attn_Wout, L3_attn_bout, L3_ffn_attn_mask, L3_ffn_Wg, L3_ffn_Wq, L3_ffn_bq, L3_ffn_Wkv, L3_ffn_bkv, L3_ffn_Wo, L3_ffn_bo, L3_ffn_ln_g, L3_ffn_ln_b):

    def _L0_attn_ref(X, Wq, Wk, Wv, Wo, bo):
        import jax, jax.numpy as jnp
        import numpy as np
        EMB = 128
        HEADS = 16
        HD = EMB // HEADS
        B, N = (8, 128)
        b, n, d = X.shape
        hd = Wq.shape[0]
        h = d // hd
        data = X.reshape(b, n, h, hd)
        q = jnp.einsum('bnhd,ed->bnhe', data, Wq)
        k = jnp.einsum('bnhd,ed->bnhe', data, Wk)
        v = jnp.einsum('bnhd,ed->bnhe', data, Wv)
        scores = jnp.einsum('bqhd,bkhd->bhqk', q, k) / d ** 0.5
        attn = jax.nn.softmax(scores, axis=-1)
        Y = jnp.einsum('bhqk,bkhd->bqhd', attn, v).reshape(b, n, d)
        return Y @ Wo.T + bo

    def _L0_ffn_ref(x, w_gate, b_gate, W1, b1, W2, b2):
        import jax, jax.numpy as jnp
        import numpy as np
        D_MODEL = 128
        MLP_DIM = 512
        N_EXPERTS = 8
        B, T = (4, 128)
        b, t, d = x.shape
        x_flat = x.reshape(b * t, d)
        logits = x_flat @ w_gate + b_gate
        probs = jax.nn.softmax(logits, axis=-1)
        route_p = jnp.max(probs, axis=-1)
        route_idx = jnp.argmax(probs, axis=-1)
        h = jnp.einsum('nd,edm->enm', x_flat, W1) + b1[:, None, :]
        h = jax.nn.relu(h)
        y = jnp.einsum('enm,emd->end', h, W2) + b2[:, None, :]
        n = b * t
        out = y[route_idx, jnp.arange(n)] * route_p[:, None]
        return out.reshape(b, t, d)

    def _L1_attn_ref(x, W_attn, b_attn, W_proj, b_proj, bias_table):
        import jax, jax.numpy as jnp
        import numpy as np
        import math
        NUM_BUCKETS = 32
        MAX_DISTANCE = 128

        def _relative_position_bucket(relative_position):
            rp = jnp.maximum(-relative_position, 0)
            max_exact = NUM_BUCKETS // 2
            is_small = rp < max_exact
            rp_f = jnp.maximum(rp, 1).astype(jnp.float32)
            large = max_exact + (jnp.log(rp_f / max_exact) / math.log(MAX_DISTANCE / max_exact) * (NUM_BUCKETS - max_exact)).astype(jnp.int32)
            large = jnp.minimum(large, NUM_BUCKETS - 1)
            return jnp.where(is_small, rp, large)

        def _t5_rel_bias(bias_table, T):
            ctx = jnp.arange(T, dtype=jnp.int32)[:, None]
            mem = jnp.arange(T, dtype=jnp.int32)[None, :]
            buckets = _relative_position_bucket(mem - ctx)
            values = bias_table[buckets]
            return jnp.transpose(values, (2, 0, 1))[None]
        B, T, C = x.shape
        H = bias_table.shape[1]
        D = C // H
        qkv = x @ W_attn + b_attn
        q, k, v = jnp.split(qkv, 3, axis=-1)
        q = q.reshape(B, T, H, D).transpose(0, 2, 1, 3)
        k = k.reshape(B, T, H, D).transpose(0, 2, 1, 3)
        v = v.reshape(B, T, H, D).transpose(0, 2, 1, 3)
        rel_bias = _t5_rel_bias(bias_table, T)
        att = jnp.einsum('bhtd,bhsd->bhts', q, k) * (1.0 / math.sqrt(D))
        att = att + rel_bias
        causal = jnp.tril(jnp.ones((T, T), dtype=bool))
        att = jnp.where(causal, att, -jnp.inf)
        att = jax.nn.softmax(att, axis=-1)
        y = jnp.einsum('bhts,bhsd->bhtd', att, v)
        y = y.transpose(0, 2, 1, 3).reshape(B, T, C)
        return y @ W_proj + b_proj

    def _L1_ffn_ref(x, W_gate, b_gate, W1, b1, W2, b2):
        import jax, jax.numpy as jnp
        import numpy as np
        D_MODEL = 128
        N_EXPERTS = 8
        TOP_K = 2
        B, T, d = x.shape
        xf = x.reshape(-1, d)
        scores = xf @ W_gate + b_gate
        topk_val, topk_idx = jax.lax.top_k(scores, TOP_K)
        onehot = jax.nn.one_hot(topk_idx, N_EXPERTS, dtype=xf.dtype)
        w = jnp.einsum('nk,nke->ne', topk_val, onehot)
        h = jax.nn.relu(jnp.einsum('nd,edh->neh', xf, W1) + b1)
        y = jnp.einsum('neh,ehd->ned', h, W2) + b2
        out = jnp.einsum('ned,ne->nd', y, w)
        return out.reshape(B, T, d)

    def _L2_attn_ref(x, Wq, bq, Wk, bk, Wv, bv, Wo, bo):
        import jax, jax.numpy as jnp
        import numpy as np
        B, T, C = (4, 512, 128)
        H = 16
        D = C // H
        W_SCALE = 0.02
        Bx, Tx, Cx = x.shape
        q = (x @ Wq.T + bq).reshape(Bx, Tx, H, D)
        k = (x @ Wk.T + bk).reshape(Bx, Tx, H, D)
        v = (x @ Wv.T + bv).reshape(Bx, Tx, H, D)
        q = jax.nn.elu(q) + 1.0
        k = jax.nn.elu(k) + 1.0
        kv = jnp.einsum('bthd,bthe->bhde', k, v)
        denom = jnp.einsum('bthd,bhd->bth', q, k.sum(axis=1))
        num = jnp.einsum('bthd,bhde->bthe', q, kv)
        out = num / jnp.clip(denom, 1e-06, None)[..., None]
        out = out.reshape(Bx, Tx, Cx)
        return out @ Wo.T + bo

    def _L2_ffn_ref(x, w_gate, w_up, w_down):
        import jax, jax.numpy as jnp
        import numpy as np
        BLOCK = 16
        _GRID = jnp.array([0.0, 0.5, 1.0, 1.5, 2.0, 3.0, 4.0, 6.0], dtype=jnp.float32)
        _MID = jnp.array([0.25, 0.75, 1.25, 1.75, 2.5, 3.5, 5.0], dtype=jnp.float32)

        def fp4_quant_dequant(x):
            shape = x.shape
            xb = x.reshape(shape[:-1] + (shape[-1] // BLOCK, BLOCK))
            scale = jnp.max(jnp.abs(xb), axis=-1, keepdims=True) / 6.0
            scale = jnp.maximum(scale, jnp.float32(1e-12))
            xn = xb / scale
            idx = jnp.searchsorted(_MID, jnp.abs(xn))
            q = _GRID[idx] * jnp.sign(xn) * scale
            return q.reshape(shape)

        def fp4_linear(x, w):
            xq = fp4_quant_dequant(x)
            wq = fp4_quant_dequant(w)
            return jnp.einsum('bsk,nk->bsn', xq, wq)
        gate = fp4_linear(x, w_gate)
        y = fp4_linear(x, w_up)
        h = jax.nn.silu(gate) * y
        return fp4_linear(h, w_down)

    def _L3_attn_ref(x, ln_w, ln_b, Wh, bh, Wqk, bqk, qk_w, qk_b, rel_table, Wout, bout):
        import jax, jax.numpy as jnp
        import numpy as np
        DIM = 128
        G = 32
        QK = 128
        HID = 256
        NUM_BUCKETS = 32
        MAX_DIST = 128
        BIAS_SCALE = QK ** 0.5
        LN_EPS = 1e-05

        def t5_rel_bias(rel_table):
            pos = jnp.arange(G)
            rel = pos[None, :] - pos[:, None]
            n = jnp.maximum(-rel, 0)
            max_exact = NUM_BUCKETS // 2
            is_small = n < max_exact
            ln_ratio = np.log(MAX_DIST / max_exact)
            val_large = max_exact + (jnp.log(jnp.maximum(n, 1).astype(jnp.float32) / max_exact) / ln_ratio * (NUM_BUCKETS - max_exact)).astype(jnp.int32)
            val_large = jnp.minimum(val_large, NUM_BUCKETS - 1)
            bucket = jnp.where(is_small, n, val_large)
            return rel_table[bucket] * BIAS_SCALE
        b, n, _ = x.shape
        g = G
        ng = n // g
        mu = jnp.mean(x, -1, keepdims=True)
        var = jnp.var(x, -1, keepdims=True)
        normed = (x - mu) * jax.lax.rsqrt(var + LN_EPS) * ln_w + ln_b
        hv = jax.nn.silu(normed @ Wh + bh)
        v, gate = jnp.split(hv, 2, axis=-1)
        qk = jax.nn.silu(normed @ Wqk + bqk)
        qk4 = qk[..., None, :] * qk_w + qk_b
        quad_q, lin_q, quad_k, lin_k = [qk4[..., h, :] for h in range(4)]
        grp = lambda t: t.reshape(b, ng, g, t.shape[-1])
        quad_q, quad_k, lin_q, lin_k, vg = map(grp, (quad_q, quad_k, lin_q, lin_k, v))
        sim = jnp.einsum('bgid,bgjd->bgij', quad_q, quad_k) / g
        sim = sim + t5_rel_bias(rel_table)
        attn = jnp.square(jax.nn.relu(sim))
        causal_mask = jnp.triu(jnp.ones((g, g), bool), 1)
        attn = jnp.where(causal_mask, 0.0, attn)
        quad_out = jnp.einsum('bgij,bgje->bgie', attn, vg)
        lin_kv = jnp.einsum('bgnd,bgne->bgde', lin_k, vg) / g
        lin_kv = jnp.cumsum(lin_kv, axis=1)
        lin_kv = jnp.pad(lin_kv, ((0, 0), (1, 0), (0, 0), (0, 0)))[:, :-1]
        lin_out = jnp.einsum('bgde,bgnd->bgne', lin_kv, lin_q)
        out = gate * (quad_out + lin_out).reshape(b, n, HID)
        return out @ Wout + bout + x

    def _L3_ffn_ref(x, attn_mask, Wg, Wq, bq, Wkv, bkv, Wo, bo, ln_g, ln_b):
        import jax, jax.numpy as jnp
        import numpy as np
        S, B, D, H, DH = (512, 8, 128, 16, 64)

        def _forward(x, Wg, Wq, bq, Wkv, bkv, Wo, bo, ln_g, ln_b):
            s_len, bsz, d_model = x.shape
            n_head, _, d_head = Wq.shape
            cap = s_len // n_head
            scale = 1.0 / d_head ** 0.5
            h = jnp.transpose(x, (1, 0, 2))
            t = h
            probs = jax.nn.softmax(h @ Wg, axis=-1)
            scores = jnp.transpose(probs, (0, 2, 1))
            _, idx = jax.lax.top_k(scores, cap)
            idx = jnp.sort(idx, axis=-1)
            hg = jnp.take_along_axis(h[:, None, :, :], idx[..., None], axis=2)
            hg = jnp.transpose(hg, (1, 0, 2, 3))
            q = jnp.einsum('hbcd,hde->hbce', hg, Wq) + bq[:, None, None, :]
            kv = jnp.einsum('hbcd,hde->hbce', hg, Wkv) + bkv[:, None, None, :]
            k, v = jnp.split(kv, 2, axis=-1)
            att = jnp.einsum('hbid,hbjd->hbij', q, k) * scale
            p = jax.nn.softmax(att, axis=1)
            av = jnp.einsum('hbij,hbjd->hbid', p, v)
            ao = jnp.einsum('hbid,hde->hbie', av, Wo) + bo
            tok = jnp.transpose(idx, (1, 0, 2))
            b_ids = jnp.arange(bsz)[None, :, None]
            outs = jnp.zeros_like(t).at[b_ids, tok].add(ao)
            y = t + outs
            mu = jnp.mean(y, axis=-1, keepdims=True)
            var = jnp.var(y, axis=-1, keepdims=True)
            yn = (y - mu) * jax.lax.rsqrt(var + 1e-05) * ln_g + ln_b
            return jnp.transpose(yn, (1, 0, 2))
        return _forward(x, Wg, Wq, bq, Wkv, bkv, Wo, bo, ln_g, ln_b)
    x = L0_attn_X
    xn = _layernorm(x, axis=-1)
    x = x + _L0_attn_ref(xn, L0_attn_Wq, L0_attn_Wk, L0_attn_Wv, L0_attn_Wo, L0_attn_bo) + _L0_ffn_ref(xn, L0_ffn_w_gate, L0_ffn_b_gate, L0_ffn_W1, L0_ffn_b1, L0_ffn_W2, L0_ffn_b2)
    xn = _layernorm(x, axis=-1)
    x = x + _L1_attn_ref(xn, L1_attn_W_attn, L1_attn_b_attn, L1_attn_W_proj, L1_attn_b_proj, L1_attn_bias_table) + _L1_ffn_ref(xn, L1_ffn_W_gate, L1_ffn_b_gate, L1_ffn_W1, L1_ffn_b1, L1_ffn_W2, L1_ffn_b2)
    xn = _layernorm(x, axis=-1)
    x = x + _L2_attn_ref(xn, L2_attn_Wq, L2_attn_bq, L2_attn_Wk, L2_attn_bk, L2_attn_Wv, L2_attn_bv, L2_attn_Wo, L2_attn_bo) + _L2_ffn_ref(xn, L2_ffn_w_gate, L2_ffn_w_up, L2_ffn_w_down)
    xn = _layernorm(x, axis=-1)
    x = x + _L3_attn_ref(xn, L3_attn_ln_w, L3_attn_ln_b, L3_attn_Wh, L3_attn_bh, L3_attn_Wqk, L3_attn_bqk, L3_attn_qk_w, L3_attn_qk_b, L3_attn_rel_table, L3_attn_Wout, L3_attn_bout) + _L3_ffn_ref(xn, L3_ffn_attn_mask, L3_ffn_Wg, L3_ffn_Wq, L3_ffn_bq, L3_ffn_Wkv, L3_ffn_bkv, L3_ffn_Wo, L3_ffn_bo, L3_ffn_ln_g, L3_ffn_ln_b)
    return x

_drawn_inputs = setup_inputs


def setup_inputs(seed=0):
    import zlib

    import numpy as np

    out = dict(_drawn_inputs(seed))
    spreads = {'L0_attn_bo': (0.0, 0.1),
     'L0_ffn_b1': (0.0, 0.1),
     'L0_ffn_b2': (0.0, 0.1),
     'L1_attn_b_attn': (0.0, 0.1),
     'L1_attn_b_proj': (0.0, 0.1),
     'L2_attn_bq': (0.0, 0.1),
     'L2_attn_bk': (0.0, 0.1),
     'L2_attn_bv': (0.0, 0.1),
     'L2_attn_bo': (0.0, 0.1),
     'L3_attn_ln_w': (1.0, 0.2),
     'L3_attn_ln_b': (0.0, 0.1),
     'L3_attn_bh': (0.0, 0.1),
     'L3_attn_bqk': (0.0, 0.1),
     'L3_attn_qk_b': (0.0, 0.1),
     'L3_attn_bout': (0.0, 0.1),
     'L3_ffn_bq': (0.0, 0.1),
     'L3_ffn_bkv': (0.0, 0.1),
     'L3_ffn_bo': (0.0, 0.1),
     'L3_ffn_ln_g': (1.0, 0.2),
     'L3_ffn_ln_b': (0.0, 0.1)}
    factors = {}
    for name, (base, spread) in spreads.items():
        noise = np.random.default_rng([zlib.crc32(name.encode()), seed]).standard_normal(out[name].shape)
        drawn = base * np.exp(spread * noise) if base else spread * noise
        out[name] = jnp.asarray(drawn.astype(out[name].dtype))
    for name, factor in factors.items():
        out[name] = (out[name] * factor).astype(out[name].dtype)
    return out
```

```python
from contextlib import ExitStack

import numpy as np

import concourse.bass as bass
from concourse import mybir

F32 = mybir.dt.float32
BF16 = mybir.dt.bfloat16
I32 = mybir.dt.int32
ALU = mybir.AluOpType
ACT = mybir.ActivationFunctionType
AX = mybir.AxisListType

P = 128
BATCH = 2
SEQ = 1024
TOK = BATCH * SEQ
NT = TOK // P
BT = SEQ // P
HEADS = 16
HD = P // HEADS
PARTS = 3
PAIRS = ((0, 0), (0, 1), (1, 0), (1, 1), (0, 2), (2, 0))
NP_ = len(PAIRS)
ROWS = HD * NP_
SROWS = ROWS + 2
VW = 32
QUAD = 4
NQUAD = BATCH * HEADS // QUAD
LN_EPS = 1e-5
NEG = -1e30
BUCKETS = 32
NEAR = 2 * P
EXPERTS = 8


class Order:

    def __init__(self, nc, ctx, eng, name):
        self.eng, self.sem, self.n, self.base = eng, nc.alloc_semaphore(name), 0, None

    def done(self, ins):
        self.n += 1
        ins.then_inc(self.sem, 1)

    def settle(self):
        if self.base is None:
            self.eng.wait_ge(self.sem, self.n)
        else:
            self.eng.wait_ge(self.sem, self.base + self.n)

    def step(self, ins):
        self.done(ins)
        self.settle()

    def enter(self, index, per_turn):
        self.start, self.turn, self.base = self.n, per_turn, index * per_turn

    def leave(self, turns):
        assert self.n - self.start == self.turn, (self.n - self.start, self.turn)
        self.n, self.base = self.start + self.turn * turns, None


def rows_bcast(ap, parts):
    return ap.rearrange("(a n) -> a n", a=1).to_broadcast([parts, ap.shape[0]])


def column(ap):
    return ap.rearrange("(n a) -> n a", a=1)


def norm_phase(nc, S, name):
    with nc.cleanup_on_exit(), ExitStack() as ctx:
        sb = lambda n, s, d=F32: ctx.enter_context(nc.sbuf_tensor(f"{name}_{n}", s, d))
        sem = lambda n: nc.alloc_semaphore(f"{name}_{n}")
        stats = sb("stats", [P, NT, 6])
        mv = sb("mv", [P, NT, 2])
        std = sb("std", [P, NT])
        rstd = sb("rstd", [P, NT])
        eps = sb("eps", [P, 1])
        tp = ctx.enter_context(nc.psum_tensor(f"{name}_tp", [P, 4, 4, P], F32))
        var_ready, std_ready, xn_ready, turned, copied = (
            sem(n) for n in ("var_ready", "std_ready", "xn_ready", "turned", "copied"))
        block = ctx.enter_context(nc.Block())

        @block.vector
        def _(dve):
            own = Order(nc, ctx, dve, f"{name}_dve")
            own.done(nc.vector.memset(eps[:], LN_EPS))
            for t in range(NT):
                own.done(nc.vector.bn_stats(stats[:, t, :], S.x[:, t, :]))
            own.settle()
            for t in range(NT):
                last = nc.vector.bn_aggr(mv[:, t, :], stats[:, t, :])
            last.then_inc(var_ready, 1)
            dve.wait_ge(std_ready, 1)
            own.step(nc.vector.reciprocal(rstd[:], std[:]))
            for t in range(NT):
                nc.vector.tensor_scalar(S.xn[:, t, :], S.x[:, t, :], mv[:, t, 0:1], rstd[:, t:t + 1],
                                        ALU.subtract, ALU.mult).then_inc(xn_ready, 1)

        @block.scalar
        def _(act):
            act.wait_ge(var_ready, 1)
            nc.scalar.activation(std[:], mv[:, :, 1], ACT.Sqrt, bias=eps[:]).then_inc(std_ready, 1)
            for g in range(NT // 4):
                act.wait_ge(turned, g + 1)
                nc.scalar.copy(S.xnT[:, g * 512:(g + 1) * 512],
                               tp[:, g].rearrange("p a b -> p (a b)")).then_inc(copied, 1)
            act.wait_ge(copied, NT // 4)

        @block.tensor
        def _(pe):
            for g in range(NT // 4):
                pe.wait_ge(xn_ready, 4 * g + 4)
                for t in range(4 * g, 4 * g + 4):
                    last = nc.tensor.transpose(tp[:, g, t % 4, :], S.xn[:, t, :], S.ident[:])
                last.then_inc(turned, 1)


def split_phase(nc, S, name, layer):
    with nc.cleanup_on_exit(), ExitStack() as ctx:
        sb = lambda n, s, d=F32: ctx.enter_context(nc.sbuf_tensor(f"{name}_{n}", s, d))
        sem = lambda n: nc.alloc_semaphore(f"{name}_{n}")
        full = sb("full", [P, 2, SEQ])
        rest = sb("rest", [P, 2, SEQ])
        parts = sb("parts", [P, 2, PARTS, SEQ], BF16)
        v = sb("v", [P, BATCH, HEADS, BT, VW])
        ps = ctx.enter_context(nc.psum_tensor(f"{name}_ps", [P, 2, 2, 512], F32))
        pv = ctx.enter_context(nc.psum_tensor(f"{name}_pv", [P, 2, 512], F32))
        scores_in, evac, split, v_ready, v_done, vsplit, v_filled = (
            sem(n) for n in ("proj", "evac", "split", "v_proj", "v_evac", "v_stored", "v_filled"))
        stored = [sem(f"stored{s}") for s in range(2)]
        scale = 1.0 / np.sqrt(P) if layer == 0 else 1.0 / np.sqrt(HD)
        jobs = [(b, side) for b in range(BATCH) for side in range(2)]
        block = ctx.enter_context(nc.Block())

        @block.tensor
        def _(pe):
            for i, (b, side) in enumerate(jobs):
                if i >= 2:
                    pe.wait_ge(evac, i - 1)
                for h in range(2):
                    last = nc.tensor.matmul(ps[:, i % 2, h, :], S.wqk[layer][side],
                                            S.xnT[:, b * SEQ + h * 512: b * SEQ + h * 512 + 512],
                                            start=True, stop=True)
                last.then_inc(scores_in, 1)
            for t in range(NT):
                if t >= 2:
                    pe.wait_ge(v_done, t - 1)
                nc.tensor.matmul(pv[:, t % 2, 0:P], S.xnT[:, t * P:(t + 1) * P], S.wv[layer],
                                 start=True, stop=True).then_inc(v_ready, 1)

        @block.scalar
        def _(act):
            own = Order(nc, ctx, act, f"{name}_act")
            for i, (b, side) in enumerate(jobs):
                act.wait_ge(scores_in, i + 1)
                if i >= 2:
                    act.wait_ge(split, i - 1)
                src = ps[:, i % 2].rearrange("p a b -> p (a b)")
                dst = full[:, i % 2, :]
                k = scale if side == 0 else 1.0
                if layer == 0:
                    nc.scalar.activation(dst, src, ACT.Copy, scale=k).then_inc(evac, 1)
                else:
                    nc.scalar.activation(dst, src, ACT.Identity, bias=S.bqk[:, side:side + 1],
                                         scale=k).then_inc(evac, 1)

        @block.vector
        def _(dve):
            own = Order(nc, ctx, dve, f"{name}_dve")
            for i, (b, side) in enumerate(jobs):
                s = i % 2
                dve.wait_ge(evac, i + 1)
                if i >= 2:
                    dve.wait_ge(stored[s], 16 * NP_ * (i // 2))
                f, r = full[:, s, :], rest[:, s, :]
                own.step(nc.vector.tensor_copy(parts[:, s, 0, :], f))
                own.step(nc.vector.tensor_tensor(r, f, parts[:, s, 0, :], ALU.subtract))
                own.step(nc.vector.tensor_copy(parts[:, s, 1, :], r))
                nc.vector.tensor_tensor(parts[:, s, 2, :], r, parts[:, s, 1, :],
                                        ALU.subtract).then_inc(split, 1)
            dve.wait_ge(v_filled, 2)
            for t in range(NT):
                dve.wait_ge(v_ready, t + 1)
                dst = v[:, t // BT, :, t % BT, 0:HD]
                src = pv[:, t % 2, 0:P].rearrange("p (h d) -> p h d", h=HEADS)
                if layer == 0:
                    nc.vector.tensor_copy(dst, src).then_inc(v_done, 1)
                else:
                    nc.vector.tensor_tensor(dst, src, S.bv[:].rearrange("p (h d) -> p h d", h=HEADS),
                                            ALU.add).then_inc(v_done, 1)

        @block.gpsimd
        def _(pool):
            nc.gpsimd.memset(v[:], 0.0).then_inc(v_filled, 1)
            pool.wait_ge(v_filled, 1)
            nc.gpsimd.memset(v[:, :, :, :, HD:HD + 1], 1.0).then_inc(v_filled, 1)

        @block.sync
        def _(sp):
            for i, (b, side) in enumerate(jobs):
                sp.wait_ge(split, i + 1)
                for n, pair in enumerate(PAIRS):
                    sp.dma_start(S.stack[b, :, n, side, :], parts[:, i % 2, pair[side], :]
                                 ).then_inc(stored[i % 2], 16)
            sp.wait_ge(v_done, NT)
            for b in range(BATCH):
                sp.dma_start(S.vstack[b].rearrange("h p c -> p h c"),
                             v[:, b].rearrange("p h t c -> p h (t c)")).then_inc(vsplit, 16)
            for s in range(2):
                sp.wait_ge(stored[s], 16 * NP_ * (len(jobs) // 2))
            sp.wait_ge(vsplit, 16 * BATCH)


def attention_phase(nc, S, name, causal):
    units = [(qt, h) for qt in range(BT) for h in range(2) if not causal or 512 * h < (qt + 1) * P]
    NM = len(units)
    USES = NM + 1
    PER_KT = [NM // BT + (kt < NM % BT) for kt in range(BT)]
    NPROB = 4
    HEAD_END = BT + NPROB
    A_DMA, B_DMA = (32, 48) if causal else (16, 32)
    with nc.cleanup_on_exit(), ExitStack() as ctx:
        sb = lambda n, s, d=F32: ctx.enter_context(nc.sbuf_tensor(f"{name}_{n}", s, d))
        sem = lambda n: nc.alloc_semaphore(f"{name}_{n}")
        slot_a = sb("slot_a", [ROWS, QUAD, 2, SEQ], BF16)
        slot_b = sb("slot_b", [SROWS, QUAD, 2, SEQ], BF16)
        slot_v = sb("slot_v", [P, QUAD, BT, VW])
        ones_row = sb("ones_row", [2, SEQ], BF16)
        if causal:
            bias_a = sb("bias_a", [P, QUAD, NEAR], BF16)
            bias_b = sb("bias_b", [P, QUAD, PARTS, NEAR], BF16)
        probs = sb("probs", [P, NPROB, SEQ])
        halfmax = sb("halfmax", [P, 2, BT, 2])
        negmax = sb("negmax", [P, 2, BT])
        mparts = sb("mparts", [BT, QUAD, 2, P], BF16)
        mbank = ctx.enter_context(nc.psum_tensor(f"{name}_mbank", [P, 2, 512], F32))
        ebank = ctx.enter_context(nc.psum_tensor(f"{name}_ebank", [P, 2, SEQ], F32))
        acc = ctx.enter_context(nc.psum_tensor(f"{name}_acc", [P, SEQ], F32))
        a_loaded = [sem(f"a_loaded{j}") for j in range(QUAD)]
        b_loaded = [sem(f"b_loaded{j}") for j in range(QUAD)]
        rows_loaded = [sem(f"rows_loaded{j}") for j in range(QUAD)]
        ones_set, ones_loaded, m_full, m_empty, max_ready, part_ready, e_full, p_full, p_empty, acc_empty = (
            sem(n) for n in ("ones_set", "ones_loaded", "m_full", "m_empty", "max_ready", "part_ready",
                             "e_full", "p_full", "p_empty", "acc_empty"))
        block = ctx.enter_context(nc.Block())

        @block.sync
        def _(sp):
            def load_a(n, j):
                sp.dma_start(slot_a[:, j].rearrange("p s t -> p (s t)"),
                             S.stack_heads[bass.ds(n, 1)].rearrange("o r c -> (o r) c")
                             ).then_inc(a_loaded[j], 16)
                if causal:
                    sp.dma_start(bias_a[:, j, :], S.hankel(n, 0)).then_inc(a_loaded[j], 16)

            def load_b(n, j):
                sp.dma_start(slot_b[0:ROWS, j].rearrange("p s t -> p (s t)"),
                             S.stack_heads[bass.ds(n, 1)].rearrange("o r c -> (o r) c")
                             ).then_inc(b_loaded[j], 16)
                sp.dma_start(slot_v[:, j].rearrange("p t c -> p (t c)"),
                             S.v_heads[bass.ds(n, 1)].rearrange("o p c -> (o p) c")
                             ).then_inc(b_loaded[j], 16)
                if causal:
                    sp.dma_start(bias_b[:, j], S.hankel(n, None)).then_inc(b_loaded[j], 16)

            def load_rows(n, j):
                sp.wait_ge(m_empty, n * USES + (NM + 3))
                for i in range(2):
                    sp.dma_start(slot_b[ROWS + i:ROWS + i + 1, j, 0, :],
                                 mparts[:, j, i, :]).then_inc(rows_loaded[j], 16)

            for j in range(QUAD):
                load_a(j, j)
            sp.wait_ge(ones_set, 1)
            for j in range(QUAD):
                sp.dma_start(slot_b[ROWS:SROWS, j, 1, :], ones_row[:]).then_inc(ones_loaded, 16)
                load_b(j, j)
            for j in range(QUAD):
                sp.wait_ge(m_full, j * USES + NM)
                load_a(QUAD + j, j)
                load_rows(j, j)

            def turn(u, more):
                for j in range(QUAD):
                    sp.wait_ge(p_empty, (u * QUAD + j) * BT + HEAD_END)
                    load_b(u * QUAD + (QUAD + j), j)
                    if more:
                        sp.wait_ge(m_full, (u * QUAD + (QUAD + j)) * USES + NM)
                        load_a(u * QUAD + (2 * QUAD + j), j)
                    load_rows(u * QUAD + (QUAD + j), j)

            with sp.Fori(0, NQUAD - 2) as u:
                turn(u, True)
            turn(NQUAD - 2, False)

        @block.tensor
        def _(pe):
            def a_unit(n, quad, j, m):
                qt, h = units[m]
                bank = (j * USES + m) % 2
                if m == 0:
                    pe.wait_ge(a_loaded[j], (quad + 1) * A_DMA)
                pe.wait_ge(m_empty, n * USES + (m + 1))
                width = min(512, (qt + 1) * P - 512 * h) if causal else 512
                near = [kt for kt in (qt - 1, qt) if causal and 4 * h <= kt < 4 * h + 4]
                last = nc.tensor.matmul(mbank[:, bank, 0:width], slot_a[:, j, 0, qt * P:(qt + 1) * P],
                                        slot_a[:, j, 1, 512 * h:512 * h + width], start=True, stop=not near)
                for kt in near:
                    c = kt * P - 512 * h
                    last = nc.tensor.matmul(mbank[:, bank, c:c + P],
                                            bias_a[:, j, (qt - kt) * P:(qt - kt + 1) * P], S.anti[:],
                                            start=False, stop=kt == near[-1])
                last.then_inc(m_full, 1)

            def turn_max(n, j):
                pe.wait_ge(max_ready, n + 1)
                pe.wait_ge(m_empty, n * USES + (NM + 1))
                nc.tensor.transpose(mbank[0:BT, (j * USES + NM) % 2, 0:P], negmax[:, j % 2, :],
                                    S.ident[:]).then_inc(m_full, 1)

            def scores(n, quad, j, kt):
                if kt == 0:
                    pe.wait_ge(b_loaded[j], (quad + 1) * B_DMA)
                    pe.wait_ge(rows_loaded[j], (quad + 1) * 32)
                pe.wait_ge(p_full, n * BT + (kt + 1))
                k = slot_b[:, j, 1, kt * P:(kt + 1) * P]
                first = kt * P if causal else 0
                for h in range(2):
                    lo, hi = max(first, 512 * h), 512 * (h + 1)
                    if lo >= hi:
                        continue
                    near = [qt for qt in (kt, kt + 1) if causal and 4 * h <= qt < 4 * h + 4]
                    last = nc.tensor.matmul(ebank[:, kt % 2, lo:hi], k, slot_b[:, j, 0, lo:hi],
                                            start=True, stop=not near)
                    for qt in near:
                        for part in range(PARTS):
                            last = nc.tensor.matmul(
                                ebank[:, kt % 2, qt * P:(qt + 1) * P], S.anti[:],
                                bias_b[:, j, part, (qt - kt) * P:(qt - kt + 1) * P],
                                start=False, stop=qt == near[-1] and part == PARTS - 1)
                last.then_inc(e_full, 1)

            def values(n, j, kt):
                if kt == 0:
                    pe.wait_ge(acc_empty, n + 1)
                pe.wait_ge(p_full, n * BT + (kt + 3))
                first = kt * P if causal else 0
                for h in range(2):
                    lo, hi = max(first, 512 * h), 512 * (h + 1)
                    if lo < hi:
                        stop = kt == (4 * h + 3 if causal else BT - 1)
                        last = nc.tensor.matmul(acc[32 * j:32 * (j + 1), lo:hi], slot_v[:, j, kt, :],
                                                probs[:, kt % NPROB, lo:hi], start=kt == 0, stop=stop)
                last.then_inc(p_empty, 1)

            pe.sem_inc(p_empty, NPROB)
            for j in range(QUAD):
                for m in range(NM):
                    a_unit(j, 0, j, m)
                turn_max(j, j)
            pe.wait_ge(ones_loaded, 16 * QUAD)

            def turn(u, with_a):
                for j in range(QUAD):
                    n = u * QUAD + j
                    m = 0
                    for kt in range(BT):
                        for _ in range(PER_KT[kt] if with_a else 0):
                            a_unit(u * QUAD + (QUAD + j), u + 1, j, m)
                            m += 1
                        scores(n, u, j, kt)
                        if kt:
                            values(n, j, kt - 1)
                        elif j:
                            values(u * QUAD + (j - 1), j - 1, BT - 1)
                    if with_a:
                        turn_max(u * QUAD + (QUAD + j), j)
                values(u * QUAD + (QUAD - 1), QUAD - 1, BT - 1)

            with pe.Fori(0, NQUAD - 1) as u:
                turn(u, True)
            turn(NQUAD - 1, False)

        @block.scalar
        def _(act):
            act.sem_inc(p_full, 2)
            act.sem_inc(acc_empty, QUAD)

            def copy_out(u, j):
                act.wait_ge(p_empty, (u * QUAD + j) * BT + HEAD_END)
                nc.scalar.copy(S.oT[32 * j:32 * (j + 1), bass.ds(u, 1), :].rearrange("p o q -> p (o q)"),
                               acc[32 * j:32 * (j + 1), :]).then_inc(acc_empty, 1)

            with act.Fori(0, NQUAD) as u:
                for j in range(QUAD):
                    for kt in range(BT):
                        g = u * (QUAD * BT) + (j * BT + kt + 1)
                        act.wait_ge(e_full, g)
                        act.wait_ge(p_empty, g)
                        first = kt * P if causal else 0
                        nc.scalar.activation(probs[:, kt % NPROB, first:SEQ], ebank[:, kt % 2, first:SEQ],
                                             ACT.Exp).then_inc(p_full, 1)
                        if kt == 2 and j:
                            copy_out(u, j - 1)
                copy_out(u, QUAD - 1)

        @block.vector
        def _(dve):
            dve.sem_inc(m_empty, 2)
            nc.vector.memset(halfmax[:], NEG)
            nc.vector.memset(ones_row[:], 1.0).then_inc(ones_set, 1)
            dve.wait_ge(ones_set, 1)

            def reduce(n, j, m):
                qt, h = units[m]
                width = min(512, (qt + 1) * P - 512 * h) if causal else 512
                dve.wait_ge(m_full, n * USES + (m + 1))
                nc.vector.reduce_max(halfmax[:, j % 2, qt, h:h + 1], mbank[:, (j * USES + m) % 2, 0:width],
                                     AX.X).then_inc(m_empty, 1)

            def combine(n, j):
                dve.wait_ge(m_empty, n * USES + (NM + 2))
                nc.vector.tensor_reduce(negmax[:, j % 2, :], halfmax[:, j % 2], AX.X, ALU.max,
                                        negate=True).then_inc(max_ready, 1)

            def split(n, quad, j):
                dve.wait_ge(m_full, n * USES + (NM + 1))
                if quad is not None:
                    dve.wait_ge(rows_loaded[j], (quad + 1) * 32)
                src = mbank[0:BT, (j * USES + NM) % 2, 0:P]
                nc.vector.tensor_copy(mparts[:, j, 0, :], src).then_inc(part_ready, 1)
                dve.wait_ge(part_ready, n + 1)
                nc.vector.tensor_tensor(mparts[:, j, 1, :], src, mparts[:, j, 0, :],
                                        ALU.subtract).then_inc(m_empty, 1)

            for j in range(QUAD):
                for m in range(NM):
                    reduce(j, j, m)
                combine(j, j)
                split(j, None, j)

            with dve.Fori(0, NQUAD - 1) as u:
                for j in range(QUAD):
                    nxt = u * QUAD + (QUAD + j)
                    for m in range(NM):
                        reduce(nxt, j, m)
                    combine(nxt, j)
                    split(nxt, u, j)
def project_phase(nc, S, name, w, bias, linear=None):
    BQ = HEADS // QUAD
    with nc.cleanup_on_exit(), ExitStack() as ctx:
        sb = lambda n, s, d=F32: ctx.enter_context(nc.sbuf_tensor(f"{name}_{n}", s, d))
        sem = lambda n: nc.alloc_semaphore(f"{name}_{n}")
        y = sb("y", [P, 2, P])
        yT = sb("yT", [P, 2, P])
        rden = sb("rden", [P, 2, HEADS])
        den = sb("den", [P, 2, HEADS])
        xb = sb("xb", [P, NT, P])
        op = ctx.enter_context(nc.psum_tensor(f"{name}_op", [P, 2, 512], F32))
        tp = ctx.enter_context(nc.psum_tensor(f"{name}_tp", [P, 2, 512], F32))
        pr = ctx.enter_context(nc.psum_tensor(f"{name}_pr", [P, 2, 512], F32))
        o_turned, r_ready, y_ready, y_turned, copied, product, added, biased, den_ready = (
            sem(n) for n in ("o_turned", "r_ready", "y_ready", "y_turned", "copied", "product", "added", "biased",
                             "den_ready"))
        block = ctx.enter_context(nc.Block())

        @block.tensor
        def _(pe):
            for i in range(NT + 2):
                if i < NT:
                    if i >= 2:
                        pe.wait_ge(y_ready, i - 1)
                    if linear:
                        last = nc.tensor.matmul(op[:, i % 2, 0:P + HEADS], linear[0][:, i * P:(i + 1) * P],
                                                linear[1][:, i // BT, :], start=True, stop=True)
                    for q in range(0 if linear else BQ):
                        last = nc.tensor.transpose(
                            op[:, i % 2, q * P:(q + 1) * P],
                            S.oT[:, i // BT * BQ + q, i % BT * P:(i % BT + 1) * P], S.ident[:])
                    last.then_inc(o_turned, 1)
                t = i - 1
                if 0 <= t < NT:
                    pe.wait_ge(y_ready, t + 1)
                    if t >= 2:
                        pe.wait_ge(copied, t - 1)
                    nc.tensor.transpose(tp[:, t % 2, 0:P], y[:, t % 2, :], S.ident[:]).then_inc(y_turned, 1)
                t = i - 2
                if t >= 0:
                    pe.wait_ge(copied, t + 1)
                    if t >= 2:
                        pe.wait_ge(added, t - 1)
                    nc.tensor.matmul(pr[:, t % 2, 0:P], yT[:, t % 2, :], w, start=True, stop=True
                                     ).then_inc(product, 1)

        @block.vector
        def _(dve):
            nc.vector.tensor_tensor(xb[:], S.x[:], bias.unsqueeze(1).to_broadcast([P, NT, P]),
                                    ALU.add).then_inc(biased, 1)
            dve.wait_ge(biased, 1)
            for i in range(NT + 2):
                if i < NT:
                    dve.wait_ge(o_turned, i + 1)
                    if linear:
                        o = op[:, i % 2, 0:P].rearrange("p (h d) -> p h d", d=HD)
                        nc.vector.tensor_scalar(den[:, i % 2, :], op[:, i % 2, P:P + HEADS], 1e-6, None,
                                                ALU.max).then_inc(den_ready, 1)
                        dve.wait_ge(den_ready, i + 1)
                        sums = den[:, i % 2, :]
                    else:
                        o = op[:, i % 2, :].rearrange("p (h c) -> p h c", c=32)
                        sums = o[:, :, HD]
                    nc.vector.reciprocal(rden[:, i % 2, :], sums).then_inc(r_ready, 1)
                    dve.wait_ge(r_ready, i + 1)
                    if i >= 2:
                        dve.wait_ge(y_turned, i - 1)
                    nc.vector.tensor_tensor(y[:, i % 2, :].rearrange("p (h d) -> p h d", d=HD), o[:, :, 0:HD],
                                            rden[:, i % 2, :].unsqueeze(2).to_broadcast([P, HEADS, HD]),
                                            ALU.mult).then_inc(y_ready, 1)
                t = i - 2
                if t >= 0:
                    dve.wait_ge(product, t + 1)
                    nc.vector.tensor_tensor(S.x[:, t, :], pr[:, t % 2, 0:P], xb[:, t, :],
                                            ALU.add).then_inc(added, 1)

        @block.scalar
        def _(act):
            for t in range(NT):
                act.wait_ge(y_turned, t + 1)
                if t >= 2:
                    act.wait_ge(product, t - 1)
                nc.scalar.copy(yT[:, t % 2, :], tp[:, t % 2, 0:P]).then_inc(copied, 1)
            act.wait_ge(copied, NT)
def moe_phase(nc, S, name, top, w_gate, gate_bias, w1, b1, w2, b2):
    MC = w2.shape[2]
    CH = 512
    HB = 4
    E = EXPERTS
    with nc.cleanup_on_exit(), ExitStack() as ctx:
        sb = lambda n, s, d=F32: ctx.enter_context(nc.sbuf_tensor(f"{name}_{n}", s, d))
        sem = lambda n: nc.alloc_semaphore(f"{name}_{n}")
        logit, expo, tie, pick, left, pick2, w = (
            sb(n, [P, NT, E]) for n in ("logit", "expo", "tie", "pick", "left", "pick2", "w"))
        mx = sb("mx", [P, 8, NT])
        wT = sb("wT", [P, P])
        wE = sb("wE", [E, TOK])
        wb = sb("wb", [P, 4, CH])
        hid = sb("hid", [P, 2, MC, CH])
        prod = sb("prod", [P, 2, CH])
        total = sb("total", [P, TOK])
        gp = ctx.enter_context(nc.psum_tensor(f"{name}_gp", [P, 512], F32))
        hp = ctx.enter_context(nc.psum_tensor(f"{name}_hp", [P, HB, 512], F32))
        yp = ctx.enter_context(nc.psum_tensor(f"{name}_yp", [P, 2, 512], F32))
        wb_loaded = [sem(f"wb_loaded{i}") for i in range(4)]
        gated, shifted, exped, w_ready, w_turned, wT_ready, w_stored, wE_loaded, b2_full, h_full, h_done, y_full, y_empty, summed, summed_start, turned, added = (
            sem(n) for n in ("gated", "shifted", "exped", "w_ready", "w_turned", "wT_ready", "w_stored",
                             "wE_loaded", "b2_full", "h_full", "h_done", "y_full", "y_empty", "summed",
                             "summed_start", "turned", "added"))
        block = ctx.enter_context(nc.Block())

        @block.tensor
        def _(pe):
            for t in range(NT):
                last = nc.tensor.matmul(gp[:, t * E:(t + 1) * E], S.xnT[:, t * P:(t + 1) * P], w_gate,
                                        start=True, stop=True)
            last.then_inc(gated, 1)
            pe.sem_inc(y_full, 2)

            def hidden(c, e):
                for m in range(MC):
                    k = e * MC + m
                    pe.wait_ge(h_done, c * (E * MC) + (k + 1))
                    nc.tensor.matmul(hp[:, k % HB, :], w1[:, e, m * P:(m + 1) * P],
                                     S.xnT[:, bass.ds(c * CH, CH)], start=True, stop=True).then_inc(h_full, 1)

            def output(c, e):
                pe.wait_ge(h_done, c * (E * MC) + (e + 1) * MC + HB)
                pe.wait_ge(y_empty, c * E + (e + 1))
                for m in range(MC):
                    last = nc.tensor.matmul(yp[:, e % 2, :], w2[:, e, m, :], hid[:, e % 2, m, :],
                                            start=m == 0, stop=m == MC - 1)
                last.then_inc(y_full, 1)

            pe.wait_ge(w_ready, 1)
            nc.tensor.transpose(yp[:, 0, 0:P], w[:].rearrange("p t e -> p (t e)"), S.ident[:]
                                ).then_inc(w_turned, 1)
            pe.wait_ge(wT_ready, 1)
            with pe.Fori(0, TOK // CH) as c:
                hidden(c, 0)
                for e in range(E):
                    if e + 1 < E:
                        hidden(c, e + 1)
                    output(c, e)
            pe.wait_ge(wE_loaded, 16)
            pe.wait_ge(h_done, TOK // CH * E * MC + HB)
            pe.wait_ge(summed, E * (TOK // CH))
            for t in range(NT):
                if t >= HB:
                    pe.wait_ge(added, t - HB + 1)
                nc.tensor.matmul(hp[:, t % HB, 0:P], wE[:, t * P:(t + 1) * P], b2, start=True, stop=False)
                nc.tensor.matmul(hp[:, t % HB, 0:P], total[:, t * P:(t + 1) * P], S.ident[:],
                                 start=False, stop=True).then_inc(turned, 1)

        @block.scalar
        def _(act):
            if top == 1:
                act.wait_ge(shifted, 1)
                nc.scalar.activation(expo[:], logit[:], ACT.Exp).then_inc(exped, 1)
            act.sem_inc(h_done, HB)
            with act.Fori(0, TOK // CH) as c:
                for e in range(E):
                    act.wait_ge(y_full, c * E + (e + 1))
                    for m in range(MC):
                        k = e * MC + m
                        act.wait_ge(h_full, c * (E * MC) + (k + 1))
                        nc.scalar.activation(hid[:, e % 2, m, :], hp[:, k % HB, :], ACT.Relu,
                                             bias=b1[:, k:k + 1]).then_inc(h_done, 1)

        @block.sync
        def _(sp):
            sp.wait_ge(wT_ready, 1)
            sp.dma_start(S.w_dram.rearrange("e (t p) -> t e p", p=P), wT[:]).then_inc(w_stored, 16)
            sp.wait_ge(w_stored, 16)
            sp.dma_start(wE[:], S.w_dram).then_inc(wE_loaded, 16)

            def load_wb(c, e):
                sp.dma_start(wb[:, e % 4, :], S.w_dram[e:e + 1, bass.ds(c * CH, CH)].to_broadcast([P, CH])
                             ).then_inc(wb_loaded[e % 4], 16)

            for e in range(4):
                load_wb(0, e)

            def turn(c, more):
                for e in range(E):
                    if e < 4 or more:
                        sp.wait_ge(y_empty, c * E + (e + 3))
                        load_wb(c + (e + 4) // E, (e + 4) % E)

            with sp.Fori(0, TOK // CH - 1) as c:
                turn(c, True)
            turn(TOK // CH - 1, False)

        @block.vector
        def _(dve):
            own = Order(nc, ctx, dve, f"{name}_dve")
            logit3 = logit[:]

            def row_max(i, src):
                own.step(nc.vector.tensor_reduce(mx[:, i, :], src[:], AX.X, ALU.max))
                return mx[:, i, :].unsqueeze(2).to_broadcast([P, NT, E])

            def best(i, src, out):
                m = row_max(i, src)
                own.step(nc.vector.tensor_tensor(tie[:], src[:], m, ALU.is_ge))
                own.step(nc.vector.tensor_tensor(tie[:], tie[:], S.falling[:].unsqueeze(1).to_broadcast([P, NT, E]),
                                                 ALU.mult))
                m = row_max(i + 1, tie)
                own.step(nc.vector.tensor_tensor(out[:], tie[:], m, ALU.is_equal))

            dve.wait_ge(gated, 1)
            own.step(nc.vector.tensor_tensor(logit3, gp[:, 0:NT * E].rearrange("p (t e) -> p t e", e=E),
                                             gate_bias.unsqueeze(1).to_broadcast([P, NT, E]), ALU.add))
            if top == 1:
                m = row_max(0, logit)
                nc.vector.tensor_tensor(logit3, logit3, m, ALU.subtract).then_inc(shifted, 1)
                dve.wait_ge(exped, 1)
                best(1, expo, pick)
                own.step(nc.vector.tensor_reduce(mx[:, 3, :], expo[:], AX.X, ALU.add))
                own.step(nc.vector.reciprocal(mx[:, 4, :], mx[:, 3, :]))
                own.step(nc.vector.tensor_tensor(left[:], expo[:],
                                                 mx[:, 4, :].unsqueeze(2).to_broadcast([P, NT, E]), ALU.mult))
                nc.vector.tensor_tensor(w[:], left[:], pick[:], ALU.mult).then_inc(w_ready, 1)
            else:
                best(0, logit, pick)
                own.step(nc.vector.scalar_tensor_tensor(left[:], pick[:], -3e38, logit3, ALU.mult, ALU.add))
                best(2, left, pick2)
                own.step(nc.vector.tensor_tensor(pick[:], pick[:], pick2[:], ALU.add))
                nc.vector.tensor_tensor(w[:], logit3, pick[:], ALU.mult).then_inc(w_ready, 1)
            dve.wait_ge(w_turned, 1)
            nc.vector.tensor_copy(wT[:], yp[:, 0, 0:P]).then_inc(wT_ready, 1)
            nc.vector.memset(total[:], 0.0).then_inc(summed_start, 1)
            dve.wait_ge(summed_start, 1)
            dve.sem_inc(y_empty, 2)
            with dve.Fori(0, TOK // CH) as c:
                for e in range(E):
                    dve.wait_ge(y_full, c * E + (e + 3))
                    dve.wait_ge(wb_loaded[e % 4], c * 32 + (16 + 16 * (e // 4)))
                    nc.vector.tensor_tensor(prod[:, e % 2, :], yp[:, e % 2, :], wb[:, e % 4, :],
                                            ALU.mult).then_inc(y_empty, 1)
                    dve.wait_ge(y_empty, c * E + (e + 3))
                    if e:
                        dve.wait_ge(summed, c * E + e)
                    part = total[:, bass.ds(c * CH, CH)]
                    nc.vector.tensor_tensor(part, part, prod[:, e % 2, :], ALU.add).then_inc(summed, 1)
            for t in range(NT):
                dve.wait_ge(turned, t + 1)
                nc.vector.tensor_tensor(S.x[:, t, :], hp[:, t % HB, 0:P], S.x[:, t, :], ALU.add).then_inc(added, 1)
def linear_phase(nc, S, name, qT, state):
    with nc.cleanup_on_exit(), ExitStack() as ctx:
        sb = lambda n, s, d=F32: ctx.enter_context(nc.sbuf_tensor(f"{name}_{n}", s, d))
        sem = lambda n: nc.alloc_semaphore(f"{name}_{n}")
        z = sb("z", [P, 2, 512])
        low = sb("low", [P, 2, 512])
        expo = sb("expo", [P, 2, 512])
        k = sb("k", [P, NT, P])
        v = sb("v", [P, NT, P + 1])
        ps = ctx.enter_context(nc.psum_tensor(f"{name}_ps", [P, 2, 512], F32))
        pv = ctx.enter_context(nc.psum_tensor(f"{name}_pv", [P, 2, 512], F32))
        kv = ctx.enter_context(nc.psum_tensor(f"{name}_kv", [P, 2, 512], F32))
        proj, z_ready, low_ready, exp_ready, act_ready, v_proj, v_ready, kv_ready = (
            sem(n) for n in ("proj", "z_ready", "low_ready", "exp_ready", "act_ready", "v_proj", "v_ready",
                             "kv_ready"))
        G = NT // 4
        block = ctx.enter_context(nc.Block())

        @block.tensor
        def _(pe):
            for i in range(2 * G):
                if i >= 2:
                    pe.wait_ge(z_ready, i - 1)
                g = i % G
                if i < G:
                    last = nc.tensor.matmul(ps[:, i % 2, :], S.wot[:, 1, :], S.xnT[:, g * 512:(g + 1) * 512],
                                            start=True, stop=True)
                else:
                    for t in range(4):
                        last = nc.tensor.matmul(ps[:, i % 2, t * P:(t + 1) * P],
                                                S.xnT[:, (4 * g + t) * P:(4 * g + t + 1) * P], S.wot[:, 2, :],
                                                start=True, stop=True)
                last.then_inc(proj, 1)
            for g in range(G):
                if g >= 2:
                    pe.wait_ge(v_ready, g)
                for t in range(4):
                    last = nc.tensor.matmul(pv[:, g % 2, t * P:(t + 1) * P],
                                            S.xnT[:, (4 * g + t) * P:(4 * g + t + 1) * P], S.wot[:, 3, :],
                                            start=True, stop=True)
                last.then_inc(v_proj, 1)
            pe.wait_ge(act_ready, 2 * G)
            pe.wait_ge(v_ready, G + 1)
            for b in range(BATCH):
                for t in range(BT):
                    last = nc.tensor.matmul(kv[:, b, 0:P + 1], k[:, b * BT + t, :], v[:, b * BT + t, :],
                                            start=t == 0, stop=t == BT - 1)
                last.then_inc(kv_ready, 1)

        @block.scalar
        def _(act):
            for i in range(2 * G):
                act.wait_ge(low_ready, i + 1)
                if i >= 2:
                    act.wait_ge(act_ready, i - 1)
                nc.scalar.activation(expo[:, i % 2, :], low[:, i % 2, :], ACT.Exp).then_inc(exp_ready, 1)

        @block.vector
        def _(dve):
            own = Order(nc, ctx, dve, f"{name}_dve")
            nc.vector.memset(v[:, :, P:P + 1], 1.0).then_inc(v_ready, 1)

            def front(i):
                dve.wait_ge(proj, i + 1)
                if i >= 2:
                    dve.wait_ge(act_ready, i - 1)
                    dve.wait_ge(exp_ready, i - 1)
                if i < G:
                    nc.vector.tensor_scalar(z[:, i % 2, :], ps[:, i % 2, :], S.b2col[:, 0:1], None,
                                            ALU.add).then_inc(z_ready, 1)
                else:
                    nc.vector.tensor_tensor(z[:, i % 2, :].rearrange("p (t c) -> p t c", c=P),
                                            ps[:, i % 2, :].rearrange("p (t c) -> p t c", c=P),
                                            S.b_row[:, 3, :].unsqueeze(1).to_broadcast([P, 4, P]),
                                            ALU.add).then_inc(z_ready, 1)
                dve.wait_ge(z_ready, i + 1)
                nc.vector.tensor_scalar(low[:, i % 2, :], z[:, i % 2, :], 0.0, None, ALU.min).then_inc(low_ready, 1)

            def back(i):
                dve.wait_ge(exp_ready, i + 1)
                g = i % G
                dst = (qT[:, g * 512:(g + 1) * 512] if i < G
                       else k[:, 4 * g:4 * g + 4, :].rearrange("p t c -> p (t c)"))
                nc.vector.scalar_tensor_tensor(dst, z[:, i % 2, :], 0.0, expo[:, i % 2, :], ALU.max,
                                               ALU.add).then_inc(act_ready, 1)

            for i in range(2 * G):
                front(i)
                if i:
                    back(i - 1)
            back(2 * G - 1)
            for g in range(G):
                dve.wait_ge(v_proj, g + 1)
                nc.vector.tensor_tensor(v[:, 4 * g:4 * g + 4, 0:P],
                                        pv[:, g % 2, :].rearrange("p (t c) -> p t c", c=P),
                                        S.b_row[:, 4, :].unsqueeze(1).to_broadcast([P, 4, P]),
                                        ALU.add).then_inc(v_ready, 1)
            for b in range(BATCH):
                dve.wait_ge(kv_ready, b + 1)
                own.done(nc.vector.tensor_tensor(state[:, b, 0:P], kv[:, b, 0:P], S.same_head[:], ALU.mult))
                own.done(nc.vector.tensor_tensor(state[:, b, P:P + HEADS], S.head_of[:],
                                                 kv[:, b, P:P + 1].to_broadcast([P, HEADS]), ALU.mult))
            own.settle()


FP4 = 16


def fp4_steps(nc, own, src, out, blocks, tmp):
    V = nc.vector
    n = blocks * FP4
    s3 = src.rearrange("p (b k) -> p b k", k=FP4)
    u, acc, cmp_, half, inv, big = (tmp[i] for i in ("u", "acc", "cmp", "half", "inv", "big"))
    u, acc, cmp_ = u[:, 0:n], acc[:, 0:n], cmp_[:, 0:n]
    half, inv, big = half[:, 0:blocks], inv[:, 0:blocks], big[:, 0:blocks]
    own.step(V.tensor_reduce(big, s3, AX.X, ALU.max, apply_absolute_value=True))
    own.step(V.tensor_scalar(big, big, 1.0 / 6.0, 1e-12, ALU.mult, ALU.max))
    own.done(V.reciprocal(inv, big))
    own.step(V.tensor_scalar(half, big, 0.5, None, ALU.mult))
    own.step(V.tensor_tensor(u.rearrange("p (b k) -> p b k", k=FP4), s3,
                             inv.unsqueeze(2).to_broadcast([P, blocks, FP4]), ALU.mult))
    own.step(V.tensor_scalar(u.bitcast(I32), u.bitcast(I32), 0x7FFFFFFF, None, ALU.bitwise_and))
    own.done(V.tensor_scalar(cmp_, u, 1.75, None, ALU.is_gt))
    own.step(V.tensor_scalar(acc, u, 5.0, 2.0, ALU.is_gt, ALU.mult))
    own.step(V.scalar_tensor_tensor(acc, u, 3.5, acc, ALU.is_gt, ALU.add))
    own.step(V.scalar_tensor_tensor(acc, u, 2.5, acc, ALU.is_gt, ALU.add))
    own.step(V.scalar_tensor_tensor(acc, acc, 2.0, cmp_, ALU.mult, ALU.add))
    for mid in (1.25, 0.75, 0.25):
        own.step(V.scalar_tensor_tensor(acc, u, mid, acc, ALU.is_gt, ALU.add))
    own.step(V.tensor_tensor(u.rearrange("p (b k) -> p b k", k=FP4), acc.rearrange("p (b k) -> p b k", k=FP4),
                             half.unsqueeze(2).to_broadcast([P, blocks, FP4]), ALU.mult))
    return V.scalar_tensor_tensor(out.bitcast(I32), src.bitcast(I32), SIGN, u.bitcast(I32),
                                  ALU.bitwise_and, ALU.bitwise_or)


SIGN = -2 ** 31


def fp4_phase(nc, S, name):
    F = 352
    FC = [(0, P), (P, P), (2 * P, F - 2 * P)]
    WB = (6 * P + F) // FP4
    G = 2
    NG = NT // G
    with nc.cleanup_on_exit(), ExitStack() as ctx:
        sb = lambda n, s, d=F32: ctx.enter_context(nc.sbuf_tensor(f"{name}_{n}", s, d))
        sem = lambda n: nc.alloc_semaphore(f"{name}_{n}")
        wq = sb("wq", [P, 6 * P + F])
        wgu = sb("wgu", [P, 2, 3 * P])
        wd = sb("wd", [P, 3, P])
        xq = sb("xq", [P, NT * P])
        xqT = sb("xqT", [P, TOK])
        sil = sb("sil", [P, 2, F])
        h = sb("h", [P, 2, G * F])
        hq = sb("hq", [P, 2, G * F])
        hT = sb("hT", [P, 2, 3, P])
        tmp = {n: sb(n, [P, NT * P]) for n in ("u", "acc", "cmp")}
        tmp.update({n: sb(n, [P, NT * P // FP4]) for n in ("half", "inv", "big")})
        ps = ctx.enter_context(nc.psum_tensor(f"{name}_ps", [P, 2, 2, 512], F32))
        tp = ctx.enter_context(nc.psum_tensor(f"{name}_tp", [P, 2, 512], F32))
        po = ctx.enter_context(nc.psum_tensor(f"{name}_po", [P, 2, 512], F32))
        wq_ready, x_ready, turned, copied, gu, siluted, h_ready, hq_ready, h_turned, h_copied, down, added = (
            sem(n) for n in ("wq_ready", "x_ready", "turned", "copied", "gate_up", "silu", "h_ready",
                             "hq_ready", "h_turned", "h_copied", "down", "added"))
        block = ctx.enter_context(nc.Block())

        @block.tensor
        def _(pe):
            pe.wait_ge(wq_ready, 1)
            for i in range(2):
                for j in range(3):
                    last = nc.tensor.transpose(tp[:, i, j * P:(j + 1) * P], wq[:, (3 * i + j) * P:(3 * i + j + 1) * P],
                                               S.ident[:])
                last.then_inc(turned, 1)
            pe.wait_ge(copied, 1)
            for j, (at, w) in enumerate(FC):
                last = nc.tensor.transpose(tp[0:w, 0, j * P:(j + 1) * P], wq[:, 6 * P + at:6 * P + at + w], S.ident[:])
            last.then_inc(turned, 1)
            pe.wait_ge(x_ready, 1)
            for i in range(NT // 4):
                pe.wait_ge(copied, i + 2)
                for t in range(4):
                    last = nc.tensor.transpose(tp[:, (i + 1) % 2, t * P:(t + 1) * P],
                                               xq[:, (4 * i + t) * P:(4 * i + t + 1) * P], S.ident[:])
                last.then_inc(turned, 1)
            pe.wait_ge(copied, 3 + NT // 4)
            for i in range(NT + 2 * G):
                if i < NT:
                    if i >= 2:
                        pe.wait_ge(h_ready, i - 1)
                    for side in range(2):
                        last = nc.tensor.matmul(ps[:, i % 2, side, 0:F], xqT[:, i * P:(i + 1) * P],
                                                wgu[:, side, 0:F], start=True, stop=True)
                    last.then_inc(gu, 1)
                t = i - 2 * G
                if t >= 0:
                    pe.wait_ge(hq_ready, t // G + 1)
                    if t >= 2:
                        pe.wait_ge(h_copied, t - 1)
                    for j, (at, w) in enumerate(FC):
                        o = (t % G) * F + at
                        last = nc.tensor.transpose(tp[0:w, t % 2, j * P:(j + 1) * P],
                                                   hq[:, t // G % 2, o:o + w], S.ident[:])
                    last.then_inc(h_turned, 1)
                    pe.wait_ge(h_copied, t + 1)
                    if t >= 2:
                        pe.wait_ge(added, t - 1)
                    for j, (at, w) in enumerate(FC):
                        last = nc.tensor.matmul(po[:, t % 2, 0:P], hT[0:w, t % 2, j, :], wd[0:w, j, :],
                                                start=j == 0, stop=j == 2)
                    last.then_inc(down, 1)

        @block.scalar
        def _(act):
            for i in range(2):
                act.wait_ge(turned, i + 1)
                nc.scalar.copy(wgu[:, i, :], tp[:, i, 0:3 * P]).then_inc(copied, 1)
            act.wait_ge(turned, 3)
            nc.scalar.copy(wd[0:FC[2][1], :, :].rearrange("p j c -> p (j c)"), tp[0:FC[2][1], 0, 0:3 * P])
            nc.scalar.copy(wd[FC[2][1]:P, 0:2, :].rearrange("p j c -> p (j c)"),
                           tp[FC[2][1]:P, 0, 0:2 * P]).then_inc(copied, 1)
            for i in range(NT // 4):
                act.wait_ge(turned, 4 + i)
                nc.scalar.copy(xqT[:, i * 512:(i + 1) * 512], tp[:, (i + 1) % 2, :]).then_inc(copied, 1)
            for i in range(NT + 2 * G):
                if i < NT:
                    act.wait_ge(gu, i + 1)
                    if i >= 2:
                        act.wait_ge(h_ready, i - 1)
                    nc.scalar.activation(sil[:, i % 2, :], ps[:, i % 2, 0, 0:F], ACT.Silu).then_inc(siluted, 1)
                t = i - 2 * G
                if t >= 0:
                    act.wait_ge(h_turned, t + 1)
                    if t >= 2:
                        act.wait_ge(down, t - 1)
                    nc.scalar.copy(hT[0:FC[2][1], t % 2, :, :].rearrange("p j c -> p (j c)"),
                                   tp[0:FC[2][1], t % 2, 0:3 * P])
                    nc.scalar.copy(hT[FC[2][1]:P, t % 2, 0:2, :].rearrange("p j c -> p (j c)"),
                                   tp[FC[2][1]:P, t % 2, 0:2 * P]).then_inc(h_copied, 1)
            act.wait_ge(h_copied, NT)

        @block.vector
        def _(dve):
            own = Order(nc, ctx, dve, f"{name}_dve")
            fp4_steps(nc, own, S.wfp[:], wq[:], WB, tmp).then_inc(wq_ready, 1)
            dve.wait_ge(wq_ready, 1)
            fp4_steps(nc, own, S.xn[:].rearrange("p t c -> p (t c)"), xq[:], NT * P // FP4, tmp).then_inc(x_ready, 1)
            dve.wait_ge(x_ready, 1)

            def add(t):
                dve.wait_ge(down, t + 1)
                nc.vector.tensor_tensor(S.x[:, t, :], po[:, t % 2, 0:P], S.x[:, t, :], ALU.add).then_inc(added, 1)

            for g in range(NG):
                for t in range(G * g, G * g + G):
                    dve.wait_ge(siluted, t + 1)
                    if g >= 2:
                        dve.wait_ge(hq_ready, g - 1)
                    nc.vector.tensor_tensor(h[:, g % 2, (t % G) * F:(t % G + 1) * F], sil[:, t % 2, :],
                                            ps[:, t % 2, 1, 0:F], ALU.mult).then_inc(h_ready, 1)
                dve.wait_ge(h_ready, G * (g + 1))
                if g >= 2:
                    dve.wait_ge(h_turned, G * (g - 1))
                fp4_steps(nc, own, h[:, g % 2, :], hq[:, g % 2, :], G * F // FP4, tmp).then_inc(hq_ready, 1)
                dve.wait_ge(hq_ready, g + 1)
                if g >= 2:
                    for t in range(G * (g - 2), G * (g - 1)):
                        add(t)
            for t in range(G * (NG - 2), NT):
                add(t)
GROUP = 32
HIDDEN = 2 * P


def renorm_phase(nc, S, name):
    with nc.cleanup_on_exit(), ExitStack() as ctx:
        sb = lambda n, s, d=F32: ctx.enter_context(nc.sbuf_tensor(f"{name}_{n}", s, d))
        sem = lambda n: nc.alloc_semaphore(f"{name}_{n}")
        stats = sb("stats", [P, NT, 6])
        mv = sb("mv", [P, NT, 2])
        std = sb("std", [P, NT])
        rstd = sb("rstd", [P, NT])
        eps = sb("eps", [P, 1])
        z = sb("z", [P, NT, P])
        zw = sb("zw", [P, NT, P])
        zg = sb("zg", [P, NT, P])
        tp = ctx.enter_context(nc.psum_tensor(f"{name}_tp", [P, 4, 4, P], F32))
        var_ready, std_ready, z_ready, zw_ready, side, turned, copied = (
            sem(n) for n in ("var_ready", "std_ready", "z_ready", "zw_ready", "side", "turned", "copied"))
        block = ctx.enter_context(nc.Block())
        row = lambda i: S.row3[:, i, :].unsqueeze(1).to_broadcast([P, 4, P])

        @block.vector
        def _(dve):
            own = Order(nc, ctx, dve, f"{name}_dve")
            own.done(nc.vector.memset(eps[:], LN_EPS))
            for t in range(NT):
                own.done(nc.vector.bn_stats(stats[:, t, :], S.xn[:, t, :]))
            own.settle()
            for t in range(NT):
                last = nc.vector.bn_aggr(mv[:, t, :], stats[:, t, :])
            last.then_inc(var_ready, 1)
            dve.wait_ge(std_ready, 1)
            own.step(nc.vector.reciprocal(rstd[:], std[:]))
            for t in range(NT):
                nc.vector.tensor_scalar(z[:, t, :], S.xn[:, t, :], mv[:, t, 0:1], rstd[:, t:t + 1],
                                        ALU.subtract, ALU.mult).then_inc(z_ready, 1)
            for g in range(NT // 4):
                s = slice(4 * g, 4 * g + 4)
                dve.wait_ge(z_ready, 4 * g + 4)
                own.step(nc.vector.tensor_tensor(zw[:, s], z[:, s], row(0), ALU.mult))
                nc.vector.tensor_tensor(zw[:, s], zw[:, s], row(1), ALU.add).then_inc(zw_ready, 1)
            for g in range(NT // 4):
                s = slice(4 * g, 4 * g + 4)
                dve.wait_ge(side, 3 * g + 3)
                own.step(nc.vector.tensor_tensor(S.x[:, s], S.x[:, s], S.xn[:, s], ALU.add))
                own.step(nc.vector.tensor_tensor(S.x[:, s], S.x[:, s], zg[:, s], ALU.add))

        @block.gpsimd
        def _(pool):
            for g in range(NT // 4):
                s = slice(4 * g, 4 * g + 4)
                pool.wait_ge(z_ready, 4 * g + 4)
                for i, op in ((2, ALU.mult), (3, ALU.add), (4, ALU.add)):
                    src = z[:, s] if i == 2 else zg[:, s]
                    nc.gpsimd.tensor_tensor(zg[:, s], src, row(i), op).then_inc(side, 1)
                    pool.wait_ge(side, 3 * g + i - 1)

        @block.scalar
        def _(act):
            act.wait_ge(var_ready, 1)
            nc.scalar.activation(std[:], mv[:, :, 1], ACT.Sqrt, bias=eps[:]).then_inc(std_ready, 1)
            for g in range(NT // 4):
                act.wait_ge(turned, g + 1)
                nc.scalar.copy(S.xnT[:, g * 512:(g + 1) * 512],
                               tp[:, g].rearrange("p a b -> p (a b)")).then_inc(copied, 1)
            act.wait_ge(copied, NT // 4)

        @block.tensor
        def _(pe):
            for g in range(NT // 4):
                pe.wait_ge(zw_ready, g + 1)
                for t in range(4):
                    last = nc.tensor.transpose(tp[:, g, t, :], zw[:, 4 * g + t, :], S.ident[:])
                last.then_inc(turned, 1)


def gau_phase(nc, S, name):
    with nc.cleanup_on_exit(), ExitStack() as ctx:
        sb = lambda n, s, d=F32: ctx.enter_context(nc.sbuf_tensor(f"{name}_{n}", s, d))
        sem = lambda n: nc.alloc_semaphore(f"{name}_{n}")
        pre = sb("pre", [P, 2, 512])
        hv = sb("hv", [P, NT, 4 * P])
        qk = sb("qk", [P, 2, 512])
        quad_q, lin_q, quad_k, lin_k = (sb(n, [P, TOK]) for n in ("quad_q", "lin_q", "quad_k", "lin_k"))
        lin_kt = sb("lin_kt", [P, NT, P])
        sim = sb("sim", [P, 2, P])
        sq = sb("sq", [P, 2, P])
        lin = sb("lin", [P, 2, P])
        amat = sb("amat", [P, 2, P])
        state = sb("state", [P, 2, HIDDEN])
        gated = sb("gated", [P, 2, HIDDEN])
        gT = sb("gT", [P, 2, HIDDEN])
        biasT = sb("biasT", [P, P])
        b_rev = sb("b_rev", [P, P])
        row = sb("row", [1, 2 * P])
        ps = ctx.enter_context(nc.psum_tensor(f"{name}_ps", [P, 2, 512], F32))
        pa = ctx.enter_context(nc.psum_tensor(f"{name}_pa", [P, 2, 512], F32))
        pst = ctx.enter_context(nc.psum_tensor(f"{name}_pst", [P, 512], F32))
        po = ctx.enter_context(nc.psum_tensor(f"{name}_po", [P, 512], F32))
        pg = ctx.enter_context(nc.psum_tensor(f"{name}_pg", [P, 2, 512], F32))
        (row_full, row_ready, row_stored, rev_loaded, rev_full, bias_ready, h_full, pre_ready, hv_ready, qk_full, qk_ready,
         aff_ready, kt_full, kt_ready, a_full, parts_ready, a_ready, st_full, st_ready, o_full, gated_ready, g_full,
         gT_ready, p_full, added) = (
            sem(n) for n in ("row_full", "row_ready", "row_stored", "rev_loaded", "rev_full", "bias_ready", "h_full",
                             "pre_ready", "hv_ready", "qk_full", "qk_ready", "aff_ready", "kt_full", "kt_ready",
                             "a_full", "parts_ready", "a_ready", "st_full", "st_ready", "o_full", "gated_ready",
                             "g_full", "gT_ready", "p_full", "added"))
        G = NT // 4
        affine = ((quad_q, 0), (lin_q, 1), (quad_k, 2), (lin_k, 3))
        block = ctx.enter_context(nc.Block())

        @block.sync
        def _(sp):
            sp.wait_ge(row_ready, 1)
            sp.dma_start(S.row3_dram, row[:]).then_inc(row_stored, 16)
            sp.wait_ge(row_stored, 16)
            sp.dma_start(b_rev[:], bass.AP(S.row3_dram.tensor, 0, [[1, P], [1, P]])).then_inc(rev_loaded, 16)

        @block.tensor
        def _(pe):
            nc.tensor.matmul(po[0:1, 0:2 * P], S.rel3[:], S.table3[:], start=True, stop=True).then_inc(row_full, 1)
            for g in range(G):
                if g >= 2:
                    pe.wait_ge(qk_ready, g - 1)
                nc.tensor.matmul(pg[:, g % 2, :], S.wqk3[:], S.xnT[:, g * 512:(g + 1) * 512], start=True,
                                 stop=True).then_inc(qk_full, 1)
            for t in range(NT):
                if t >= 2:
                    pe.wait_ge(pre_ready, t - 1)
                nc.tensor.matmul(ps[:, t % 2, :], S.xnT[:, t * P:(t + 1) * P], S.wh3[:], start=True,
                                 stop=True).then_inc(h_full, 1)
            pe.wait_ge(rev_loaded, 16)
            pe.wait_ge(row_ready, 1)
            nc.tensor.matmul(po[:, 0:P], S.anti32[:], b_rev[:], start=True, stop=True).then_inc(rev_full, 1)
            pe.wait_ge(aff_ready, 4 * G)
            pe.wait_ge(qk_ready, G)
            for g in range(G):
                if g >= 2:
                    pe.wait_ge(kt_ready, g - 1)
                for t in range(4):
                    last = nc.tensor.transpose(pg[:, g % 2, t * P:(t + 1) * P],
                                               lin_k[:, (4 * g + t) * P:(4 * g + t + 1) * P], S.ident[:])
                last.then_inc(kt_full, 1)
            pe.wait_ge(kt_ready, G)
            pe.wait_ge(hv_ready, NT)

            def square(t):
                if t >= 2:
                    pe.wait_ge(a_ready, t - 1)
                c = slice(t * P, (t + 1) * P)
                nc.tensor.matmul(pa[:, t % 2, 0:P], quad_k[:, c], quad_q[:, c], start=True, stop=True)
                nc.tensor.matmul(pa[:, t % 2, P:2 * P], lin_k[:, c], lin_q[:, c], start=True,
                                 stop=True).then_inc(a_full, 1)

            def out(t):
                b0 = t % BT == 0
                if t % BT < BT - 1:
                    if not b0 or t:
                        pe.wait_ge(st_ready, t - t // BT)
                    nc.tensor.matmul(pst[:, 0:HIDDEN], lin_kt[:, t, :], hv[:, t, 0:HIDDEN], start=b0,
                                     stop=t % BT == BT - 2, skip_group_check=True).then_inc(st_full, 1)
                pe.wait_ge(a_ready, t + 1)
                if t:
                    pe.wait_ge(gated_ready, t)
                nc.tensor.matmul(po[:, 0:HIDDEN], amat[:, t % 2, :], hv[:, t, 0:HIDDEN], start=True, stop=b0
                                 ) if not b0 else nc.tensor.matmul(
                    po[:, 0:HIDDEN], amat[:, t % 2, :], hv[:, t, 0:HIDDEN], start=True, stop=True
                    ).then_inc(o_full, 1)
                if not b0:
                    n = t - t // BT
                    pe.wait_ge(st_ready, n)
                    nc.tensor.matmul(po[:, 0:HIDDEN], lin_q[:, t * P:(t + 1) * P], state[:, (n - 1) % 2, :],
                                     start=False, stop=True).then_inc(o_full, 1)

            def project(t):
                pe.wait_ge(gated_ready, t + 1)
                if t >= 2:
                    pe.wait_ge(gT_ready, t - 1)
                    pe.wait_ge(added, t - 1)
                for j in range(2):
                    last = nc.tensor.transpose(pg[:, t % 2, j * P:(j + 1) * P], gated[:, t % 2, j * P:(j + 1) * P],
                                               S.ident[:])
                last.then_inc(g_full, 1)
                pe.wait_ge(gT_ready, t + 1)
                for j in range(2):
                    last = nc.tensor.matmul(pg[:, t % 2, HIDDEN:HIDDEN + P], gT[:, t % 2, j * P:(j + 1) * P],
                                            S.wo3[:, j, :], start=j == 0, stop=j == 1)
                last.then_inc(p_full, 1)

            square(0)
            for t in range(NT + 1):
                if t + 1 < NT:
                    square(t + 1)
                if t < NT:
                    out(t)
                if t:
                    project(t - 1)

        @block.scalar
        def _(act):
            for g in range(G):
                act.wait_ge(qk_full, g + 1)
                if g >= 2:
                    act.wait_ge(aff_ready, 4 * (g - 1))
                nc.scalar.activation(qk[:, g % 2, :], pg[:, g % 2, :], ACT.Silu, bias=S.col3[:, 0:1]
                                     ).then_inc(qk_ready, 1)
            for t in range(NT):
                act.wait_ge(pre_ready, t + 1)
                nc.scalar.activation(hv[:, t, :], pre[:, t % 2, :], ACT.Silu).then_inc(hv_ready, 1)
            for g in range(G):
                act.wait_ge(kt_full, g + 1)
                nc.scalar.copy(lin_kt[:, 4 * g:4 * g + 4, :].rearrange("p t c -> p (t c)"), pg[:, g % 2, :]
                               ).then_inc(kt_ready, 1)
            for t in range(NT + 1):
                if t < NT and t % BT < BT - 1:
                    n = t - t // BT
                    act.wait_ge(st_full, n + 1)
                    if n >= 2:
                        act.wait_ge(o_full, t)
                    nc.scalar.copy(state[:, n % 2, :], pst[:, 0:HIDDEN]).then_inc(st_ready, 1)
                if t:
                    act.wait_ge(g_full, t)
                    if t >= 3:
                        act.wait_ge(p_full, t - 2)
                    nc.scalar.copy(gT[:, (t - 1) % 2, :], pg[:, (t - 1) % 2, 0:HIDDEN]).then_inc(gT_ready, 1)

        @block.vector
        def _(dve):
            own = Order(nc, ctx, dve, f"{name}_dve")
            dve.wait_ge(row_full, 1)
            nc.vector.tensor_copy(row[:], po[0:1, 0:2 * P]).then_inc(row_ready, 1)
            for g in range(G):
                dve.wait_ge(qk_ready, g + 1)
                for dst, i in affine:
                    nc.vector.tensor_scalar(dst[:, g * 512:(g + 1) * 512], qk[:, g % 2, :], S.aff3[:, i:i + 1],
                                            S.aff3[:, 4 + i:5 + i], ALU.mult, ALU.add).then_inc(aff_ready, 1)
            for t in range(NT):
                dve.wait_ge(h_full, t + 1)
                if t >= 2:
                    dve.wait_ge(hv_ready, t - 1)
                nc.vector.tensor_tensor(pre[:, t % 2, :], ps[:, t % 2, :], S.bh3[:], ALU.add).then_inc(pre_ready, 1)
            dve.wait_ge(rev_full, 1)
            own.step(nc.vector.tensor_tensor(biasT[:], po[:, 0:P], S.quad_mask[:, 0, :], ALU.mult))
            nc.vector.tensor_tensor(biasT[:], biasT[:], S.quad_mask[:, 1, :], ALU.add).then_inc(bias_ready, 1)
            dve.wait_ge(bias_ready, 1)

            def weights(t):
                s = t % 2
                dve.wait_ge(a_full, t + 1)
                own.done(nc.vector.tensor_tensor(sim[:, s, :], pa[:, s, 0:P], biasT[:], ALU.add))
                own.step(nc.vector.tensor_tensor(lin[:, s, :], pa[:, s, P:2 * P], S.lin_mask[:], ALU.mult))
                own.step(nc.vector.scalar_tensor_tensor(sq[:, s, :], sim[:, s, :], 0.0, sim[:, s, :], ALU.max,
                                                        ALU.mult))
                if t >= 2:
                    dve.wait_ge(o_full, t - 1)
                nc.vector.tensor_tensor(amat[:, s, :], sq[:, s, :], lin[:, s, :], ALU.add).then_inc(a_ready, 1)

            def add(t):
                dve.wait_ge(p_full, t + 1)
                nc.vector.tensor_tensor(S.x[:, t, :], pg[:, t % 2, HIDDEN:HIDDEN + P], S.x[:, t, :],
                                        ALU.add).then_inc(added, 1)

            weights(0)
            for t in range(NT + 1):
                if t + 1 < NT:
                    weights(t + 1)
                if t < NT:
                    dve.wait_ge(o_full, t + 1)
                    if t >= 2:
                        dve.wait_ge(g_full, t - 1)
                    nc.vector.tensor_tensor(gated[:, t % 2, :], po[:, 0:HIDDEN], hv[:, t, HIDDEN:2 * HIDDEN],
                                            ALU.mult).then_inc(gated_ready, 1)
                if t:
                    add(t - 1)
def buckets():
    dist = np.arange(-(P - 1), NEAR + 1)
    bucket = bucket_of(dist)
    table = np.zeros((BUCKETS + 1, len(dist)), np.float32)
    table[bucket, np.arange(len(dist))] = 1.0
    table[BUCKETS - 1] -= 1.0
    table[:, dist < 0] = 0.0
    table[BUCKETS, dist < 0] = NEG
    return table


def bucket_of(dist):
    half = BUCKETS // 2
    far = half + (np.log(np.maximum(dist, 1).astype(np.float32) / np.float32(half)) / np.float32(np.log(8.0))
                  * half).astype(np.int32)
    return np.where(dist < half, np.maximum(dist, 0), np.minimum(far, BUCKETS - 1))


def buckets3():
    table = np.zeros((BUCKETS, 2 * P), np.float32)
    dist = np.arange(2 * P) - (P - 1)
    table[bucket_of(dist), np.arange(2 * P)] = np.float32(np.sqrt(P))
    return table


def group_masks():
    i = np.arange(P)
    same = (i[:, None] // GROUP == i[None, :] // GROUP) & (i[:, None] <= i[None, :])
    earlier = i[:, None] // GROUP < i[None, :] // GROUP
    quad = np.stack([same.astype(np.float32), np.where(same, 0.0, NEG).astype(np.float32)], axis=1)
    return np.ascontiguousarray(quad), earlier.astype(np.float32)


class Store:
    pass


def setup_phase(nc, S, I):
    with nc.cleanup_on_exit(), ExitStack() as ctx:
        sb = lambda n, s, d=F32: ctx.enter_context(nc.sbuf_tensor(f"setup_{n}", s, d))
        sem = lambda n: nc.alloc_semaphore(f"setup_{n}")
        small = sb("small", [P, 3, P])
        wo = sb("wo", [P, 5, P])
        b1 = sb("b1", [5 * EXPERTS, P])
        aff_rows = sb("aff_rows", [8, P])
        table = sb("table", [BUCKETS + 1, P + NEAR])
        rel = sb("rel", [BUCKETS + 1, HEADS])
        brow = sb("brow", [HEADS, P + NEAR])
        brow2 = sb("brow2", [HEADS, P + NEAR])
        bparts = sb("bparts", [HEADS, PARTS, P + NEAR], BF16)
        ps = ctx.enter_context(nc.psum_tensor("setup_ps", [P, 8, 512], F32))
        consts, first, blocks, rest, zeroed, turned, copied, stored, rel_ready = (
            sem(n) for n in ("consts", "first", "blocks", "rest", "zeroed", "turned", "copied", "stored", "rel"))
        block = ctx.enter_context(nc.Block())
        W = P + NEAR
        small_names = ("L0_attn_Wq", "L0_attn_Wk", "L0_attn_Wv")
        square = ("L0_attn_Wo", "L2_attn_Wq", "L2_attn_Wk", "L2_attn_Wv", "L2_attn_Wo")
        loads = [
            (S.wa1[:], I["L1_attn_W_attn"]),
            (S.wp1[:], I["L1_attn_W_proj"]),
            (S.b_row[:, 0, :], rows_bcast(I["L0_attn_bo"], P)),
            (S.b_row[:, 1, :], rows_bcast(I["L1_attn_b_proj"], P)),
            (S.b_row[:, 2, :], rows_bcast(I["L1_attn_b_attn"][2 * P:3 * P], P)),
            (S.bqk_raw[:, 0:1], column(I["L1_attn_b_attn"][0:P])),
            (S.bqk_raw[:, 1:2], column(I["L1_attn_b_attn"][P:2 * P])),
            (S.gate_w[:, 0, :], I["L0_ffn_w_gate"]),
            (S.gate_w[:, 1, :], I["L1_ffn_W_gate"]),
            (S.gate_b[:, 0, :], rows_bcast(I["L0_ffn_b_gate"], P)),
            (S.gate_b[:, 1, :], rows_bcast(I["L1_ffn_b_gate"], P)),
            (S.w1_0[:], I["L0_ffn_W1"].rearrange("e c m -> c e m")),
            (S.w2_0[:], I["L0_ffn_W2"].rearrange("e (m p) d -> p e m d", p=P)),
            (S.w1_1[:], I["L1_ffn_W1"].rearrange("e c m -> c e m")),
            (S.w2_1[:, :, 0, :], I["L1_ffn_W2"].rearrange("e c m -> c e m")),
            (S.b2_0[:], I["L0_ffn_b2"]),
            (S.b2_1[:], I["L1_ffn_b2"]),
            (b1[0:4 * EXPERTS, :], I["L0_ffn_b1"].rearrange("e (m p) -> (e m) p", p=P)),
            (b1[4 * EXPERTS:5 * EXPERTS, :], I["L1_ffn_b1"]),
            (S.same_head[:], I["same_head"]),
            (S.quad_mask[:], I["quad_mask"]),
            (S.lin_mask[:], I["lin_mask"]),
            (S.table3[:], I["buckets3"]),
            (S.rel3[:], column(I["L3_attn_rel_table"])),
            (S.wh3[:], I["L3_attn_Wh"]),
            (S.wqk3[:], I["L3_attn_Wqk"]),
            (S.wo3[:], I["L3_attn_Wout"].rearrange("(j p) c -> p j c", p=P)),
            (S.bh3[:], rows_bcast(I["L3_attn_bh"], P)),
            (S.col3[:], column(I["L3_attn_bqk"])),
            (S.row3[:, 0, :], rows_bcast(I["L3_attn_ln_w"], P)),
            (S.row3[:, 1, :], rows_bcast(I["L3_attn_ln_b"], P)),
            (S.row3[:, 2, :], rows_bcast(I["L3_ffn_ln_g"], P)),
            (S.row3[:, 3, :], rows_bcast(I["L3_ffn_ln_b"], P)),
            (S.row3[:, 4, :], rows_bcast(I["L3_attn_bout"], P)),
            (aff_rows[0:4, :], I["L3_attn_qk_w"]),
            (aff_rows[4:8, :], I["L3_attn_qk_b"]),
            (S.head_of[:], I["head_of"]),
            (S.b2col[:, 0:1], column(I["L2_attn_bq"])),
            (S.b_row[:, 3, :], rows_bcast(I["L2_attn_bk"], P)),
            (S.b_row[:, 4, :], rows_bcast(I["L2_attn_bv"], P)),
            (S.b_row[:, 5, :], rows_bcast(I["L2_attn_bo"], P)),
            (S.wfp[:, 6 * P:6 * P + 352], I["L2_ffn_w_down"]),
        ] + [(wo[:, i, :], I[n]) for i, n in enumerate(square)]
        for i, n in enumerate(("L2_ffn_w_gate", "L2_ffn_w_up")):
            loads += [(S.wfp[:, (3 * i + j) * P:(3 * i + j + 1) * P], I[n][j * P:(j + 1) * P]) for j in range(2)]
            loads.append((S.wfp[0:352 - 2 * P, (3 * i + 2) * P:(3 * i + 3) * P], I[n][2 * P:352]))

        @block.sync
        def _(sp):
            sp.dma_start(S.ident[:], I["ident"]).then_inc(consts, 16)
            sp.dma_start(S.anti32[:], I["anti"]).then_inc(consts, 16)
            sp.dma_start(table[:], I["buckets"]).then_inc(consts, 16)
            sp.dma_start(rel[0:BUCKETS, :], I["L1_attn_bias_table"]).then_inc(consts, 16)
            sp.dma_start(S.x[:], I["L0_attn_X"].rearrange("b (t p) c -> p (b t) c", p=P)).then_inc(first, 16)
            for dst, src in loads:
                sp.dma_start(dst, src).then_inc(rest, 16)
            sp.wait_ge(consts, 64)
            sp.wait_ge(first, 16)
            sp.wait_ge(rest, 16 * len(loads))
            sp.wait_ge(rel_ready, 6)
            for copy in range(BATCH):
                sp.dma_start(S.trow.ap()[copy * HEADS:(copy + 1) * HEADS], bparts[:]).then_inc(stored, 16)
            sp.wait_ge(stored, 16 * BATCH)

        @block.gpsimd
        def _(pool):
            pool.wait_ge(zeroed, 1)
            for i, n in enumerate(small_names):
                for h in range(HEADS):
                    pool.dma_start(small[h * HD:(h + 1) * HD, i, h * HD:(h + 1) * HD], I[n]).then_inc(blocks, 16)
            pool.wait_ge(blocks, 16 * 3 * HEADS)

        @block.vector
        def _(dve):
            nc.vector.memset(small[:], 0.0).then_inc(zeroed, 1)
            for i in range(2):
                nc.vector.memset(S.wfp[352 - 2 * P:P, (3 * i + 2) * P:(3 * i + 3) * P], 0.0)
            nc.vector.memset(rel[BUCKETS:BUCKETS + 1, :], 1.0).then_inc(rel_ready, 1)
            dve.wait_ge(consts, 64)
            nc.vector.tensor_copy(S.anti[:], S.anti32[:])
            dve.wait_ge(rest, 16 * len(loads))
            nc.vector.tensor_scalar(S.bqk[:, 0:1], S.bqk_raw[:, 0:1], 1.0 / np.sqrt(HD), None, ALU.mult)
            nc.vector.tensor_copy(S.bqk[:, 1:2], S.bqk_raw[:, 1:2])
            dve.wait_ge(turned, 1)
            nc.vector.tensor_copy(brow[:], ps[0:HEADS, 0, 0:W]).then_inc(rel_ready, 1)
            dve.wait_ge(rel_ready, 2)
            nc.vector.tensor_copy(bparts[:, 0, :], brow[:]).then_inc(rel_ready, 1)
            dve.wait_ge(rel_ready, 3)
            nc.vector.tensor_tensor(brow2[:], brow[:], bparts[:, 0, :], ALU.subtract).then_inc(rel_ready, 1)
            dve.wait_ge(rel_ready, 4)
            nc.vector.tensor_copy(bparts[:, 1, :], brow2[:]).then_inc(rel_ready, 1)
            dve.wait_ge(rel_ready, 5)
            nc.vector.tensor_tensor(bparts[:, 2, :], brow2[:], bparts[:, 1, :], ALU.subtract).then_inc(rel_ready, 1)
            dve.wait_ge(turned, 2)
            nc.vector.tensor_copy(S.wt0[:], ps[:, 1:4, 0:P])
            nc.vector.tensor_copy(S.wot[:], ps[:, 4:8, 0:P]).then_inc(copied, 1)
            dve.wait_ge(turned, 3)
            for e in range(EXPERTS):
                nc.vector.memset(S.falling[:, e:e + 1], float(EXPERTS - e))
            for at, scale in ((0, 1.0), (2, 1.0 / GROUP), (4, 1.0), (6, 1.0 / GROUP)):
                nc.vector.tensor_scalar(S.aff3[:, at:at + 2], ps[:, 0, 2 * P + at:2 * P + at + 2], scale, None,
                                        ALU.mult)
            nc.vector.tensor_copy(S.b1[:], ps[:, 0, P:P + 5 * EXPERTS])
            nc.vector.tensor_copy(S.wot4[:], ps[:, 0, 0:P]).then_inc(copied, 1)
            dve.wait_ge(copied, 2)

        @block.tensor
        def _(pe):
            pe.wait_ge(consts, 64)
            pe.wait_ge(rel_ready, 1)
            nc.tensor.matmul(ps[0:HEADS, 0, 0:W], rel[:], table[:], start=True, stop=True).then_inc(turned, 1)
            pe.wait_ge(blocks, 16 * 3 * HEADS)
            pe.wait_ge(rest, 16 * len(loads))
            for i in range(3):
                nc.tensor.transpose(ps[:, 1 + i, 0:P], small[:, i, :], S.ident[:])
            for i in range(4):
                last = nc.tensor.transpose(ps[:, 4 + i, 0:P], wo[:, i, :], S.ident[:])
            last.then_inc(turned, 1)
            pe.wait_ge(rel_ready, 2)
            nc.tensor.transpose(ps[:, 0, 0:P], wo[:, 4, :], S.ident[:])
            nc.tensor.transpose(ps[:, 0, 2 * P:2 * P + 8], aff_rows[:], S.ident[0:8, 0:8])
            nc.tensor.transpose(ps[:, 0, P:P + 5 * EXPERTS], b1[:], S.ident[0:5 * EXPERTS, 0:5 * EXPERTS]
                                ).then_inc(turned, 1)


def network(nc, I, out, layers=(0, 1, 2, 3)):
    with ExitStack() as ctx:
        sb = lambda n, s, d=F32: ctx.enter_context(nc.sbuf_tensor(n, s, d))
        S = Store()
        S.x = sb("x", [P, NT, P])
        S.xn = sb("xn", [P, NT, P])
        S.xnT = sb("xnT", [P, TOK])
        S.ident = sb("ident", [P, P])
        S.anti32 = sb("anti32", [P, P])
        S.anti = sb("anti", [P, P], BF16)
        S.b_row = sb("b_row", [P, 6, P])
        S.b2col = sb("b2col", [P, 1])
        S.same_head = sb("same_head", [P, P])
        S.head_of = sb("head_of", [P, HEADS])
        S.wfp = sb("wfp", [P, 6 * P + 352])
        S.bqk_raw = sb("bqk_raw", [P, 2])
        S.bqk = sb("bqk", [P, 2])
        S.wt0 = sb("wt0", [P, 3, P])
        S.wot = sb("wot", [P, 4, P])
        S.wot4 = sb("wot4", [P, P])
        S.gate_w = sb("gate_w", [P, 2, EXPERTS])
        S.gate_b = sb("gate_b", [P, 2, EXPERTS])
        S.falling = sb("falling", [P, EXPERTS])
        S.b1 = sb("b1", [P, 5 * EXPERTS])
        S.b2_0 = sb("b2_0", [EXPERTS, P])
        S.b2_1 = sb("b2_1", [EXPERTS, P])
        S.w_dram = nc.dram_tensor("w_rows", (EXPERTS, TOK), F32).ap()
        S.quad_mask = sb("quad_mask", [P, 2, P])
        S.lin_mask = sb("lin_mask", [P, P])
        S.table3 = sb("table3", [BUCKETS, 2 * P])
        S.rel3 = sb("rel3", [BUCKETS, 1])
        S.wh3 = sb("wh3", [P, 4 * P])
        S.wqk3 = sb("wqk3", [P, P])
        S.wo3 = sb("wo3", [P, 2, P])
        S.bh3 = sb("bh3", [P, 4 * P])
        S.col3 = sb("col3", [P, 1])
        S.row3 = sb("row3", [P, 5, P])
        S.aff3 = sb("aff3", [P, 8])
        S.row3_dram = nc.dram_tensor("row3_dram", (1, 2 * P), F32).ap()
        S.bv = S.b_row[:, 2, :]
        stack = nc.dram_tensor("stack", (BATCH, P, NP_, 2, SEQ), BF16)
        vstack = nc.dram_tensor("vstack", (BATCH, HEADS, P, BT * VW), F32)
        S.trow = nc.dram_tensor("trow", (BATCH * HEADS, PARTS, P + NEAR), BF16)
        S.stack, S.vstack = stack.ap(), vstack.ap()
        S.stack_heads = S.stack.rearrange("b (h d) n s t -> (b h) (d n) (s t)", h=HEADS)
        S.v_heads = S.vstack.rearrange("b h p c -> (b h) p c")

        def hankel(n, part):
            at = S.trow.ap()[bass.ds(n, 1)].offset
            W = P + NEAR
            if part is None:
                return bass.AP(S.trow, at, [[1, P], [W, PARTS], [1, NEAR]])
            return bass.AP(S.trow, at, [[1, P], [1, NEAR]])

        S.hankel = hankel
        first_half = ctx.enter_context(ExitStack())
        early = lambda n, s, d=F32: first_half.enter_context(nc.sbuf_tensor(n, s, d))
        S.oT = early("oT", [P, NQUAD, SEQ])
        S.wa1 = early("wa1", [P, 3 * P])
        S.wp1 = early("wp1", [P, P])
        S.w1_0 = early("w1_0", [P, EXPERTS, 4 * P])
        S.w2_0 = early("w2_0", [P, EXPERTS, 4, P])
        S.w1_1 = early("w1_1", [P, EXPERTS, P])
        S.w2_1 = early("w2_1", [P, EXPERTS, 1, P])
        S.wqk = [[S.wt0[:, 0, :], S.wt0[:, 1, :]], [S.wa1[:, 0:P], S.wa1[:, P:2 * P]]]
        S.wv = [S.wt0[:, 2, :], S.wa1[:, 2 * P:3 * P]]
        setup_phase(nc, S, I)
        if 0 in layers:
            norm_phase(nc, S, "n0")
            split_phase(nc, S, "s0", 0)
            attention_phase(nc, S, "a0", False)
            project_phase(nc, S, "p0", S.wot[:, 0, :], S.b_row[:, 0, :])
            moe_phase(nc, S, "m0", 1, S.gate_w[:, 0, :], S.gate_b[:, 0, :], S.w1_0, S.b1[:, 0:4 * EXPERTS],
                      S.w2_0, S.b2_0[:])
        if 1 in layers:
            norm_phase(nc, S, "n1")
            split_phase(nc, S, "s1", 1)
            attention_phase(nc, S, "a1", True)
            project_phase(nc, S, "p1", S.wp1[:], S.b_row[:, 1, :])
            moe_phase(nc, S, "m1", 2, S.gate_w[:, 1, :], S.gate_b[:, 1, :], S.w1_1,
                      S.b1[:, 4 * EXPERTS:5 * EXPERTS], S.w2_1, S.b2_1[:])
        first_half.close()
        if 2 in layers:
            norm_phase(nc, S, "n2")
            with nc.sbuf_tensor("q2T", [P, TOK], F32) as qT, nc.sbuf_tensor("state", [P, BATCH, P + HEADS], F32) as st:
                linear_phase(nc, S, "l2", qT, st)
                project_phase(nc, S, "p2", S.wot4[:], S.b_row[:, 5, :], linear=(qT, st))
            fp4_phase(nc, S, "f2")
        if 3 in layers:
            norm_phase(nc, S, "n3")
            renorm_phase(nc, S, "r3")
            gau_phase(nc, S, "g3")
        with nc.semaphore("written") as written, nc.Block() as block:
            @block.sync
            def _(sp):
                sp.dma_start(out.rearrange("b (t p) c -> p (b t) c", p=P), S.x[:]).then_inc(written, 16)
                sp.wait_ge(written, 16)


LAYERS = (0, 1, 2, 3)


def kernel(**inputs):
    import concourse.bacc as bacc
    from concourse.bass_utils import run_bass_kernel_spmd

    nc = bacc.Bacc("TRN2", target_bir_lowering=False, num_devices=1)
    arrays, args = {}, {}
    given = dict(inputs)
    given.pop("L3_ffn_attn_mask")
    given["ident"] = np.eye(P, dtype=np.float32)
    given["anti"] = np.ascontiguousarray(np.eye(P, dtype=np.float32)[::-1])
    given["buckets"] = buckets()
    given["buckets3"] = buckets3()
    given["quad_mask"], given["lin_mask"] = group_masks()
    given["head_of"] = np.ascontiguousarray(np.repeat(np.eye(HEADS, dtype=np.float32), HD, axis=0))
    given["same_head"] = np.ascontiguousarray(np.kron(np.eye(HEADS), np.ones((HD, HD))).astype(np.float32))
    for name, value in given.items():
        a = np.ascontiguousarray(value)
        arrays[f"in_{name}"] = a
        args[name] = nc.dram_tensor(f"in_{name}", a.shape, mybir.dt.from_np(a.dtype), kind="ExternalInput").ap()
    out = nc.dram_tensor("out_x", (BATCH, SEQ, P), F32, kind="ExternalOutput").ap()
    network(nc, args, out, LAYERS)
    r = run_bass_kernel_spmd(nc, [arrays], core_ids=[0])
    return r.results[0]["out_x"]
```

```python
from contextlib import ExitStack

import numpy as np

import concourse.bass as bass
from concourse import mybir

F32 = mybir.dt.float32
BF16 = mybir.dt.bfloat16
I32 = mybir.dt.int32
ALU = mybir.AluOpType
ACT = mybir.ActivationFunctionType
AX = mybir.AxisListType

P = 128
BATCH = 2
SEQ = 1024
TOK = BATCH * SEQ
NT = TOK // P
BT = SEQ // P
HEADS = 16
HD = P // HEADS
PARTS = 3
PAIRS = ((0, 0), (0, 1), (1, 0), (1, 1), (0, 2), (2, 0))
NP_ = len(PAIRS)
ROWS = HD * NP_
SROWS = ROWS + 2
VW = 32
QUAD = 4
NQUAD = BATCH * HEADS // QUAD
LN_EPS = 1e-5
NEG = -1e30
BUCKETS = 32
NEAR = 2 * P
EXPERTS = 8


class Order:

    def __init__(self, nc, ctx, eng, name):
        self.eng, self.sem, self.n, self.base = eng, nc.alloc_semaphore(name), 0, None

    def done(self, ins):
        self.n += 1
        ins.then_inc(self.sem, 1)

    def settle(self):
        if self.base is None:
            self.eng.wait_ge(self.sem, self.n)
        else:
            self.eng.wait_ge(self.sem, self.base + self.n)

    def step(self, ins):
        self.done(ins)
        self.settle()

    def enter(self, index, per_turn):
        self.start, self.turn, self.base = self.n, per_turn, index * per_turn

    def leave(self, turns):
        assert self.n - self.start == self.turn, (self.n - self.start, self.turn)
        self.n, self.base = self.start + self.turn * turns, None


def rows_bcast(ap, parts):
    return ap.rearrange("(a n) -> a n", a=1).to_broadcast([parts, ap.shape[0]])


def column(ap):
    return ap.rearrange("(n a) -> n a", a=1)


def norm_phase(nc, S, name):
    with nc.cleanup_on_exit(), ExitStack() as ctx:
        sb = lambda n, s, d=F32: ctx.enter_context(nc.sbuf_tensor(f"{name}_{n}", s, d))
        sem = lambda n: nc.alloc_semaphore(f"{name}_{n}")
        stats = sb("stats", [P, NT, 6])
        mv = sb("mv", [P, NT, 2])
        std = sb("std", [P, NT])
        rstd = sb("rstd", [P, NT])
        eps = sb("eps", [P, 1])
        tp = ctx.enter_context(nc.psum_tensor(f"{name}_tp", [P, 4, 4, P], F32))
        var_ready, std_ready, xn_ready, turned, copied = (
            sem(n) for n in ("var_ready", "std_ready", "xn_ready", "turned", "copied"))
        block = ctx.enter_context(nc.Block())

        @block.vector
        def _(dve):
            own = Order(nc, ctx, dve, f"{name}_dve")
            own.done(nc.vector.memset(eps[:], LN_EPS))
            for t in range(NT):
                own.done(nc.vector.bn_stats(stats[:, t, :], S.x[:, t, :]))
            own.settle()
            for t in range(NT):
                last = nc.vector.bn_aggr(mv[:, t, :], stats[:, t, :])
            last.then_inc(var_ready, 1)
            dve.wait_ge(std_ready, 1)
            own.step(nc.vector.reciprocal(rstd[:], std[:]))
            for t in range(NT):
                nc.vector.tensor_scalar(S.xn[:, t, :], S.x[:, t, :], mv[:, t, 0:1], rstd[:, t:t + 1],
                                        ALU.subtract, ALU.mult).then_inc(xn_ready, 1)

        @block.scalar
        def _(act):
            act.wait_ge(var_ready, 1)
            nc.scalar.activation(std[:], mv[:, :, 1], ACT.Sqrt, bias=eps[:]).then_inc(std_ready, 1)
            for g in range(NT // 4):
                act.wait_ge(turned, g + 1)
                nc.scalar.copy(S.xnT[:, g * 512:(g + 1) * 512],
                               tp[:, g].rearrange("p a b -> p (a b)")).then_inc(copied, 1)
            act.wait_ge(copied, NT // 4)

        @block.tensor
        def _(pe):
            for g in range(NT // 4):
                pe.wait_ge(xn_ready, 4 * g + 4)
                for t in range(4 * g, 4 * g + 4):
                    last = nc.tensor.transpose(tp[:, g, t % 4, :], S.xn[:, t, :], S.ident[:])
                last.then_inc(turned, 1)


def split_phase(nc, S, name, layer):
    with nc.cleanup_on_exit(), ExitStack() as ctx:
        sb = lambda n, s, d=F32: ctx.enter_context(nc.sbuf_tensor(f"{name}_{n}", s, d))
        sem = lambda n: nc.alloc_semaphore(f"{name}_{n}")
        full = sb("full", [P, 2, SEQ])
        rest = sb("rest", [P, 2, SEQ])
        parts = sb("parts", [P, 2, PARTS, SEQ], BF16)
        v = S.oT[:].rearrange("p q s -> p (q s)").rearrange("p (b h t c) -> p b h t c", b=BATCH, h=HEADS, t=BT)
        ps = ctx.enter_context(nc.psum_tensor(f"{name}_ps", [P, 2, 2, 512], F32))
        pv = ctx.enter_context(nc.psum_tensor(f"{name}_pv", [P, 2, 512], F32))
        scores_in, evac, split, v_ready, v_done, vsplit, v_filled = (
            sem(n) for n in ("proj", "evac", "split", "v_proj", "v_evac", "v_stored", "v_filled"))
        stored = [sem(f"stored{s}") for s in range(2)]
        scale = 1.0 / np.sqrt(P) if layer == 0 else 1.0 / np.sqrt(HD)
        jobs = [(b, side) for b in range(BATCH) for side in range(2)]
        block = ctx.enter_context(nc.Block())

        @block.tensor
        def _(pe):
            for i, (b, side) in enumerate(jobs):
                if i >= 2:
                    pe.wait_ge(evac, i - 1)
                for h in range(2):
                    last = nc.tensor.matmul(ps[:, i % 2, h, :], S.wqk[layer][side],
                                            S.xnT[:, b * SEQ + h * 512: b * SEQ + h * 512 + 512],
                                            start=True, stop=True)
                last.then_inc(scores_in, 1)
            for t in range(NT):
                if t >= 2:
                    pe.wait_ge(v_done, t - 1)
                nc.tensor.matmul(pv[:, t % 2, 0:P], S.xnT[:, t * P:(t + 1) * P], S.wv[layer],
                                 start=True, stop=True).then_inc(v_ready, 1)

        @block.scalar
        def _(act):
            own = Order(nc, ctx, act, f"{name}_act")
            for i, (b, side) in enumerate(jobs):
                act.wait_ge(scores_in, i + 1)
                if i >= 2:
                    act.wait_ge(split, i - 1)
                src = ps[:, i % 2].rearrange("p a b -> p (a b)")
                dst = full[:, i % 2, :]
                k = scale if side == 0 else 1.0
                if layer == 0:
                    nc.scalar.activation(dst, src, ACT.Copy, scale=k).then_inc(evac, 1)
                else:
                    nc.scalar.activation(dst, src, ACT.Identity, bias=S.bqk[:, side:side + 1],
                                         scale=k).then_inc(evac, 1)

        @block.vector
        def _(dve):
            own = Order(nc, ctx, dve, f"{name}_dve")
            for i, (b, side) in enumerate(jobs):
                s = i % 2
                dve.wait_ge(evac, i + 1)
                if i >= 2:
                    dve.wait_ge(stored[s], 16 * NP_ * (i // 2))
                f, r = full[:, s, :], rest[:, s, :]
                own.step(nc.vector.tensor_copy(parts[:, s, 0, :], f))
                own.step(nc.vector.tensor_tensor(r, f, parts[:, s, 0, :], ALU.subtract))
                own.step(nc.vector.tensor_copy(parts[:, s, 1, :], r))
                nc.vector.tensor_tensor(parts[:, s, 2, :], r, parts[:, s, 1, :],
                                        ALU.subtract).then_inc(split, 1)
            dve.wait_ge(v_filled, 2)
            for t in range(NT):
                dve.wait_ge(v_ready, t + 1)
                dst = v[:, t // BT, :, t % BT, 0:HD]
                src = pv[:, t % 2, 0:P].rearrange("p (h d) -> p h d", h=HEADS)
                if layer == 0:
                    nc.vector.tensor_copy(dst, src).then_inc(v_done, 1)
                else:
                    nc.vector.tensor_tensor(dst, src, S.bv[:].rearrange("p (h d) -> p h d", h=HEADS),
                                            ALU.add).then_inc(v_done, 1)

        @block.gpsimd
        def _(pool):
            nc.gpsimd.memset(S.oT[:], 0.0).then_inc(v_filled, 1)
            pool.wait_ge(v_filled, 1)
            nc.gpsimd.memset(v[:, :, :, :, HD:HD + 1], 1.0).then_inc(v_filled, 1)

        @block.sync
        def _(sp):
            for i, (b, side) in enumerate(jobs):
                sp.wait_ge(split, i + 1)
                for n, pair in enumerate(PAIRS):
                    sp.dma_start(S.stack[b, :, n, side, :], parts[:, i % 2, pair[side], :]
                                 ).then_inc(stored[i % 2], 16)
            sp.wait_ge(v_done, NT)
            for b in range(BATCH):
                sp.dma_start(S.vstack[b].rearrange("h p c -> p h c"),
                             v[:, b].rearrange("p h t c -> p h (t c)")).then_inc(vsplit, 16)
            for s in range(2):
                sp.wait_ge(stored[s], 16 * NP_ * (len(jobs) // 2))
            sp.wait_ge(vsplit, 16 * BATCH)


def attention_phase(nc, S, name, causal):
    units = [(pr, qt, jj) for pr in range(2) for qt in range(BT) for jj in range(2)]
    uses = units[:2] + ["late"] + units[2:18] + ["turn"] + units[18:]
    USES = len(uses)
    LATE, TURN = uses.index("late"), uses.index("turn")
    LEAD = 8
    PAIR_END = [uses.index((pr, BT - 1, 1)) + 1 for pr in range(2)]
    groups = [(h, kt) for h in range(2) for kt in range(4 * h + 4 if causal else BT)]
    lows = [max(kt * P - 512 * h, 0) if causal else 0 for h, kt in groups]
    widths = np.array([512 - lo for lo in lows])
    share = [round(float(c)) for c in np.cumsum(widths) * USES / widths.sum()]
    share = [b - a for a, b in zip([0] + share, share)]
    G = len(groups)
    STEPS = QUAD * G
    NE = 3
    A_DMA, B_DMA = (96, 144) if causal else (64, 80)
    assert USES % 2 == 0 and G % 2 == 0 and sum(share) == USES
    with nc.cleanup_on_exit(), ExitStack() as ctx:
        sb = lambda n, s, d=F32: ctx.enter_context(nc.sbuf_tensor(f"{name}_{n}", s, d))
        sem = lambda n: nc.alloc_semaphore(f"{name}_{n}")
        slot_v = sb("slot_v", [P, 2, QUAD, BT, VW])
        if causal:
            bias_a = sb("bias_a", [P, QUAD, NEAR], BF16)
            bias_b = sb("bias_b", [P, 2, QUAD, PARTS, NEAR], BF16)
        probs = sb("probs", [P, 2, QUAD, 512])
        negmax = sb("negmax", [P, 2, 2 * BT])
        mparts = sb("mparts", [2 * BT, 2, 2, P], BF16)
        mbank = ctx.enter_context(nc.psum_tensor(f"{name}_mbank", [P, 2, SEQ], F32))
        ebank = ctx.enter_context(nc.psum_tensor(f"{name}_ebank", [P, NE, 512], F32))
        acc = ctx.enter_context(nc.psum_tensor(f"{name}_acc", [P, 512], F32))
        a_loaded = [sem(f"a_loaded{pr}") for pr in range(2)]
        b_loaded = [sem(f"b_loaded{buf}") for buf in range(2)]
        rows_loaded = [sem(f"rows_loaded{pr}") for pr in range(2)]
        zeroed, m_full, m_empty, part_ready, e_full, p_full, p_empty, acc_empty = (
            sem(n) for n in ("zeroed", "m_full", "m_empty", "part_ready",
                             "e_full", "p_full", "p_empty", "acc_empty"))
        block = ctx.enter_context(nc.Block())
        a_src = S.stack_heads.rearrange("(q pr jj) r (s t) -> pr jj s q r t", pr=2, jj=2, s=2)
        b_src = S.stack_heads.rearrange("(q pr jj) r (s t) -> jj s q r pr t", pr=2, jj=2, s=2)
        v_src = S.v_heads.rearrange("(q j) p c -> q p j c", j=QUAD)

        @block.sync
        def _(sp):
            def load_a(q, pr):
                for jj in range(2):
                    for s, dst in enumerate((S.a_still[64 * jj:64 * jj + ROWS, pr, jj, :],
                                             S.a_moving[64 * jj:64 * jj + ROWS, pr, :])):
                        sp.dma_start(dst, a_src[pr, jj, s][bass.ds(q, 1)].rearrange("o r t -> (o r) t")
                                     ).then_inc(a_loaded[pr], 16)
                    if causal:
                        sp.dma_start(bias_a[:, 2 * pr + jj, :], S.hankel(q * QUAD + (2 * pr + jj), 0)
                                     ).then_inc(a_loaded[pr], 16)

            def load_b(q, buf):
                for jj in range(2):
                    for s, dst in enumerate((S.b_moving[64 * jj:64 * jj + ROWS, buf],
                                             S.b_still[64 * jj:64 * jj + ROWS, buf, :, jj, :])):
                        sp.dma_start(dst, b_src[jj, s][bass.ds(q, 1)].rearrange("o r pr t -> (o r) pr t")
                                     ).then_inc(b_loaded[buf], 16)
                sp.dma_start(slot_v[:, buf].rearrange("p j t c -> p j (t c)"),
                             v_src[bass.ds(q, 1)].rearrange("o p j c -> (o p) j c")).then_inc(b_loaded[buf], 16)
                if causal:
                    for j in range(QUAD):
                        sp.dma_start(bias_b[:, buf, j], S.hankel(q * QUAD + j, None)).then_inc(b_loaded[buf], 16)

            def load_rows(pr, buf):
                for jj in range(2):
                    for i in range(2):
                        row = 64 * jj + ROWS + i
                        sp.dma_start(S.b_moving[row:row + 1, buf, pr, :],
                                     mparts[jj * BT:(jj + 1) * BT, pr, i, :]).then_inc(rows_loaded[pr], 16)

            def quad(q, buf, first=False, reuse=True, more=True):
                if not first:
                    sp.wait_ge(m_empty, q * USES + (LATE + 3))
                    load_rows(1, 1 - buf)
                if reuse:
                    sp.wait_ge(p_empty, q * G + (2 - G))
                load_b(q, buf)
                if more:
                    sp.wait_ge(m_full, q * USES + PAIR_END[0])
                    load_a(q + 1, 0)
                sp.wait_ge(m_empty, q * USES + (TURN + 3))
                load_rows(0, buf)
                if more:
                    sp.wait_ge(m_full, q * USES + PAIR_END[1])
                    load_a(q + 1, 1)

            load_a(0, 0)
            load_a(0, 1)
            quad(0, 0, first=True, reuse=False)
            quad(1, 1, reuse=False)
            with sp.Fori(1, NQUAD // 2 - 1) as i:
                quad(i * 2, 0)
                quad(i * 2 + 1, 1)
            quad(NQUAD - 2, 0)
            quad(NQUAD - 1, 1, more=False)
            sp.wait_ge(m_empty, NQUAD * USES + 3)
            load_rows(1, (NQUAD - 1) % 2)

        @block.tensor
        def _(pe):
            def transpose_maxima(index, bank, pr):
                pe.wait_ge(m_empty, index)
                nc.tensor.transpose(mbank[0:2 * BT, bank, 0:P], negmax[:, pr, :], S.ident[:]).then_inc(m_full, 1)

            def a_use(q, use):
                bank = use % 2
                if uses[use] in ("late", "turn"):
                    transpose_maxima(q * USES + (use + 1), bank, 1 if uses[use] == "late" else 0)
                    return
                pr, qt, jj = uses[use]
                if (qt, jj) == (0, 0):
                    pe.wait_ge(a_loaded[pr], q * A_DMA + A_DMA)
                pe.wait_ge(m_empty, q * USES + (use + 1))
                width = (qt + 1) * P if causal else SEQ
                for h in range(2):
                    lo, hi = 512 * h, min(512 * (h + 1), width)
                    if lo >= hi:
                        continue
                    near = [kt for kt in (qt - 1, qt) if causal and 4 * h <= kt < 4 * h + 4]
                    last = nc.tensor.matmul(mbank[:, bank, lo:hi], S.a_still[:, pr, jj, qt * P:(qt + 1) * P],
                                            S.a_moving[:, pr, lo:hi], start=True, stop=not near)
                    for kt in near:
                        last = nc.tensor.matmul(mbank[:, bank, kt * P:(kt + 1) * P],
                                                bias_a[:, 2 * pr + jj, (qt - kt) * P:(qt - kt + 1) * P],
                                                S.anti[:], start=False, stop=kt == near[-1])
                last.then_inc(m_full, 1)

            def scores(q, g, j, buf):
                h, kt = groups[g]
                s = g * QUAD + j
                pr, jj = j // 2, j % 2
                if g == 0:
                    for other in range(2):
                        pe.wait_ge(rows_loaded[other], q * 64 + 64)
                step = q * STEPS + s
                pe.wait_ge(p_full, step + (NE if s == 0 and (STEPS - 1) % NE == 0 else 1))
                lo = lows[g]
                near = [qt for qt in (kt, kt + 1) if causal and 4 * h <= qt < 4 * h + 4]
                last = nc.tensor.matmul(ebank[:, s % NE, lo:512], S.b_still[:, buf, pr, jj, kt * P:(kt + 1) * P],
                                        S.b_moving[:, buf, pr, 512 * h + lo:512 * (h + 1)],
                                        start=True, stop=not near)
                if near:
                    a, b = (near[0] - kt) * P, (near[-1] + 1 - kt) * P
                    at = near[0] * P - 512 * h
                    for part in range(PARTS):
                        last = nc.tensor.matmul(ebank[:, s % NE, at:at + b - a], S.anti[:],
                                                bias_b[:, buf, j, part, a:b], start=False, stop=part == PARTS - 1)
                last.then_inc(e_full, 1)

            def values(q, g, buf):
                h, kt = groups[g]
                if kt == 0:
                    pe.wait_ge(acc_empty, q * 2 + (h + 1))
                pe.wait_ge(p_full, q * STEPS + (g * QUAD + QUAD + NE))
                lo = lows[g]
                for j in range(QUAD):
                    last = nc.tensor.matmul(acc[32 * j:32 * (j + 1), lo:512], slot_v[:, buf, j, kt, :],
                                            probs[:, g % 2, j, lo:512], start=kt == 0,
                                            stop=g + 1 == G or groups[g + 1][0] != h)
                last.then_inc(p_empty, 1)

            def turn(q, buf, half, ahead, after):
                pe.wait_ge(b_loaded[buf], half * B_DMA + B_DMA)
                use = LEAD
                for g in range(G):
                    todo = [use + i for i in range(share[g])]
                    use += share[g]
                    cut = [len(todo) * i // 3 for i in range(4)]
                    def some(i):
                        for n in todo[cut[i]:cut[i + 1]]:
                            if n < USES and ahead:
                                a_use(q + 1, n)
                            elif n >= USES and after:
                                a_use(q + 2, n - USES)
                    scores(q, g, 0, buf)
                    scores(q, g, 1, buf)
                    some(0)
                    scores(q, g, 2, buf)
                    if g:
                        values(q, g - 1, buf)
                    some(1)
                    scores(q, g, 3, buf)
                    some(2)
                values(q, G - 1, buf)

            pe.sem_inc(p_empty, 2)
            pe.wait_ge(zeroed, 1)
            for use in range(USES):
                a_use(0, use)
            for use in range(LEAD):
                a_use(1, use)
            with pe.Fori(0, NQUAD // 2 - 1) as i:
                turn(i * 2, 0, i, True, True)
                turn(i * 2 + 1, 1, i, True, True)
            turn(NQUAD - 2, 0, NQUAD // 2 - 1, True, False)
            transpose_maxima(NQUAD * USES + 2, 0, 1)
            turn(NQUAD - 1, 1, NQUAD // 2 - 1, False, False)

        @block.scalar
        def _(act):
            act.sem_inc(p_full, NE)
            act.sem_inc(acc_empty, 1)

            def copy_out(u, h):
                end = max(g for g in range(G) if groups[g][0] == h)
                act.wait_ge(p_empty, u * G + (end + 3))
                nc.scalar.copy(S.oT[:, bass.ds(u, 1), 512 * h:512 * (h + 1)].rearrange("p o q -> p (o q)"),
                               acc[:]).then_inc(acc_empty, 1)

            with act.Fori(0, NQUAD) as u:
                for g, (h, kt) in enumerate(groups):
                    act.wait_ge(p_empty, u * G + (g + 1))
                    for j in range(QUAD):
                        s = g * QUAD + j
                        act.wait_ge(e_full, u * STEPS + (s + 1))
                        if h == 1 and kt == 0 and j == 3:
                            copy_out(u, 0)
                        nc.scalar.activation(probs[:, g % 2, j, lows[g]:512], ebank[:, s % NE, lows[g]:512],
                                             ACT.Exp).then_inc(p_full, 1)
                copy_out(u, 1)

        @block.vector
        def _(dve):
            dve.sem_inc(m_empty, 2)
            nc.vector.memset(negmax[:], 0.0).then_inc(zeroed, 1)
            dve.wait_ge(zeroed, 1)

            def split(index, number, loads, bank, pr):
                dve.wait_ge(m_full, index)
                if loads is not None:
                    dve.wait_ge(rows_loaded[pr], loads)
                src = mbank[0:2 * BT, bank, 0:P]
                nc.vector.tensor_copy(mparts[:, pr, 0, :], src).then_inc(part_ready, 1)
                dve.wait_ge(part_ready, number)
                nc.vector.tensor_tensor(mparts[:, pr, 1, :], src, mparts[:, pr, 0, :],
                                        ALU.subtract).then_inc(m_empty, 1)

            def quad(q, loaded, earlier):
                for use, what in enumerate(uses):
                    index = q * USES + (use + 1)
                    if what == "late":
                        split(index, q * 2 + 1, q * 64 - 64 if earlier else None, use % 2, 1)
                    elif what == "turn":
                        split(index, q * 2 + 2, q * 64 if loaded else None, use % 2, 0)
                    else:
                        pr, qt, jj = what
                        dve.wait_ge(m_full, index)
                        at = jj * BT + qt
                        nc.vector.tensor_reduce(negmax[:, pr, at:at + 1],
                                                mbank[:, use % 2, 0:(qt + 1) * P if causal else SEQ],
                                                AX.X, ALU.max, negate=True).then_inc(m_empty, 1)

            quad(0, False, False)
            quad(1, True, False)
            with dve.Fori(2, NQUAD) as u:
                quad(u, True, True)
            split(NQUAD * USES + 1, NQUAD * 2 + 1, NQUAD * 64 - 64, 0, 1)
def project_phase(nc, S, name, w, bias, linear=None):
    BQ = HEADS // QUAD
    with nc.cleanup_on_exit(), ExitStack() as ctx:
        sb = lambda n, s, d=F32: ctx.enter_context(nc.sbuf_tensor(f"{name}_{n}", s, d))
        sem = lambda n: nc.alloc_semaphore(f"{name}_{n}")
        y = sb("y", [P, 2, P])
        yT = sb("yT", [P, 2, P])
        rden = sb("rden", [P, 2, HEADS])
        den = sb("den", [P, 2, HEADS])
        xb = sb("xb", [P, NT, P])
        op = ctx.enter_context(nc.psum_tensor(f"{name}_op", [P, 2, 512], F32))
        tp = ctx.enter_context(nc.psum_tensor(f"{name}_tp", [P, 2, 512], F32))
        pr = ctx.enter_context(nc.psum_tensor(f"{name}_pr", [P, 2, 512], F32))
        o_turned, r_ready, y_ready, y_turned, copied, product, added, biased, den_ready = (
            sem(n) for n in ("o_turned", "r_ready", "y_ready", "y_turned", "copied", "product", "added", "biased",
                             "den_ready"))
        block = ctx.enter_context(nc.Block())

        @block.tensor
        def _(pe):
            for i in range(NT + 2):
                if i < NT:
                    if i >= 2:
                        pe.wait_ge(y_ready, i - 1)
                    if linear:
                        last = nc.tensor.matmul(op[:, i % 2, 0:P + HEADS], linear[0][:, i * P:(i + 1) * P],
                                                linear[1][:, i // BT, :], start=True, stop=True)
                    for q in range(0 if linear else BQ):
                        last = nc.tensor.transpose(
                            op[:, i % 2, q * P:(q + 1) * P],
                            S.oT[:, i // BT * BQ + q, i % BT * P:(i % BT + 1) * P], S.ident[:])
                    last.then_inc(o_turned, 1)
                t = i - 1
                if 0 <= t < NT:
                    pe.wait_ge(y_ready, t + 1)
                    if t >= 2:
                        pe.wait_ge(copied, t - 1)
                    nc.tensor.transpose(tp[:, t % 2, 0:P], y[:, t % 2, :], S.ident[:]).then_inc(y_turned, 1)
                t = i - 2
                if t >= 0:
                    pe.wait_ge(copied, t + 1)
                    if t >= 2:
                        pe.wait_ge(added, t - 1)
                    nc.tensor.matmul(pr[:, t % 2, 0:P], yT[:, t % 2, :], w, start=True, stop=True
                                     ).then_inc(product, 1)

        @block.vector
        def _(dve):
            nc.vector.tensor_tensor(xb[:], S.x[:], bias.unsqueeze(1).to_broadcast([P, NT, P]),
                                    ALU.add).then_inc(biased, 1)
            dve.wait_ge(biased, 1)
            for i in range(NT + 2):
                if i < NT:
                    dve.wait_ge(o_turned, i + 1)
                    if linear:
                        o = op[:, i % 2, 0:P].rearrange("p (h d) -> p h d", d=HD)
                        nc.vector.tensor_scalar(den[:, i % 2, :], op[:, i % 2, P:P + HEADS], 1e-6, None,
                                                ALU.max).then_inc(den_ready, 1)
                        dve.wait_ge(den_ready, i + 1)
                        sums = den[:, i % 2, :]
                    else:
                        o = op[:, i % 2, :].rearrange("p (h c) -> p h c", c=32)
                        sums = o[:, :, HD]
                    nc.vector.reciprocal(rden[:, i % 2, :], sums).then_inc(r_ready, 1)
                    dve.wait_ge(r_ready, i + 1)
                    if i >= 2:
                        dve.wait_ge(y_turned, i - 1)
                    nc.vector.tensor_tensor(y[:, i % 2, :].rearrange("p (h d) -> p h d", d=HD), o[:, :, 0:HD],
                                            rden[:, i % 2, :].unsqueeze(2).to_broadcast([P, HEADS, HD]),
                                            ALU.mult).then_inc(y_ready, 1)
                t = i - 2
                if t >= 0:
                    dve.wait_ge(product, t + 1)
                    nc.vector.tensor_tensor(S.x[:, t, :], pr[:, t % 2, 0:P], xb[:, t, :],
                                            ALU.add).then_inc(added, 1)

        @block.scalar
        def _(act):
            for t in range(NT):
                act.wait_ge(y_turned, t + 1)
                if t >= 2:
                    act.wait_ge(product, t - 1)
                nc.scalar.copy(yT[:, t % 2, :], tp[:, t % 2, 0:P]).then_inc(copied, 1)
            act.wait_ge(copied, NT)
def moe_phase(nc, S, name, top, w_gate, gate_bias, w1, b1, w2, b2):
    MC = w2.shape[2]
    CH = 512
    HB = 4
    E = EXPERTS
    with nc.cleanup_on_exit(), ExitStack() as ctx:
        sb = lambda n, s, d=F32: ctx.enter_context(nc.sbuf_tensor(f"{name}_{n}", s, d))
        sem = lambda n: nc.alloc_semaphore(f"{name}_{n}")
        logit, expo, tie, pick, left, pick2, w = (
            sb(n, [P, NT, E]) for n in ("logit", "expo", "tie", "pick", "left", "pick2", "w"))
        mx = sb("mx", [P, 8, NT])
        wT = sb("wT", [P, P])
        wE = sb("wE", [E, TOK])
        wb = sb("wb", [P, 4, CH])
        hid = sb("hid", [P, 2, MC, CH])
        prod = sb("prod", [P, 2, CH])
        total = sb("total", [P, TOK])
        gp = ctx.enter_context(nc.psum_tensor(f"{name}_gp", [P, 512], F32))
        hp = ctx.enter_context(nc.psum_tensor(f"{name}_hp", [P, HB, 512], F32))
        yp = ctx.enter_context(nc.psum_tensor(f"{name}_yp", [P, 2, 512], F32))
        wb_loaded = [sem(f"wb_loaded{i}") for i in range(4)]
        gated, shifted, exped, w_ready, w_turned, wT_ready, w_stored, wE_loaded, b2_full, h_full, h_done, y_full, y_empty, summed, summed_start, turned, added = (
            sem(n) for n in ("gated", "shifted", "exped", "w_ready", "w_turned", "wT_ready", "w_stored",
                             "wE_loaded", "b2_full", "h_full", "h_done", "y_full", "y_empty", "summed",
                             "summed_start", "turned", "added"))
        block = ctx.enter_context(nc.Block())

        @block.tensor
        def _(pe):
            for t in range(NT):
                last = nc.tensor.matmul(gp[:, t * E:(t + 1) * E], S.xnT[:, t * P:(t + 1) * P], w_gate,
                                        start=True, stop=True)
            last.then_inc(gated, 1)
            pe.sem_inc(y_full, 2)

            def hidden(c, e):
                for m in range(MC):
                    k = e * MC + m
                    pe.wait_ge(h_done, c * (E * MC) + (k + 1))
                    nc.tensor.matmul(hp[:, k % HB, :], w1[:, e, m * P:(m + 1) * P],
                                     S.xnT[:, bass.ds(c * CH, CH)], start=True, stop=True).then_inc(h_full, 1)

            def output(c, e):
                pe.wait_ge(h_done, c * (E * MC) + (e + 1) * MC + HB)
                pe.wait_ge(y_empty, c * E + (e + 1))
                for m in range(MC):
                    last = nc.tensor.matmul(yp[:, e % 2, :], w2[:, e, m, :], hid[:, e % 2, m, :],
                                            start=m == 0, stop=m == MC - 1)
                last.then_inc(y_full, 1)

            pe.wait_ge(w_ready, 1)
            nc.tensor.transpose(yp[:, 0, 0:P], w[:].rearrange("p t e -> p (t e)"), S.ident[:]
                                ).then_inc(w_turned, 1)
            pe.wait_ge(wT_ready, 1)
            with pe.Fori(0, TOK // CH) as c:
                hidden(c, 0)
                for e in range(E):
                    if e + 1 < E:
                        hidden(c, e + 1)
                    output(c, e)
            pe.wait_ge(wE_loaded, 16)
            pe.wait_ge(h_done, TOK // CH * E * MC + HB)
            pe.wait_ge(summed, E * (TOK // CH))
            for t in range(NT):
                if t >= HB:
                    pe.wait_ge(added, t - HB + 1)
                nc.tensor.matmul(hp[:, t % HB, 0:P], wE[:, t * P:(t + 1) * P], b2, start=True, stop=False)
                nc.tensor.matmul(hp[:, t % HB, 0:P], total[:, t * P:(t + 1) * P], S.ident[:],
                                 start=False, stop=True).then_inc(turned, 1)

        @block.scalar
        def _(act):
            if top == 1:
                act.wait_ge(shifted, 1)
                nc.scalar.activation(expo[:], logit[:], ACT.Exp).then_inc(exped, 1)
            act.sem_inc(h_done, HB)
            with act.Fori(0, TOK // CH) as c:
                for e in range(E):
                    act.wait_ge(y_full, c * E + (e + 1))
                    for m in range(MC):
                        k = e * MC + m
                        act.wait_ge(h_full, c * (E * MC) + (k + 1))
                        nc.scalar.activation(hid[:, e % 2, m, :], hp[:, k % HB, :], ACT.Relu,
                                             bias=b1[:, k:k + 1]).then_inc(h_done, 1)

        @block.sync
        def _(sp):
            sp.wait_ge(wT_ready, 1)
            sp.dma_start(S.w_dram.rearrange("e (t p) -> t e p", p=P), wT[:]).then_inc(w_stored, 16)
            sp.wait_ge(w_stored, 16)
            sp.dma_start(wE[:], S.w_dram).then_inc(wE_loaded, 16)

            def load_wb(c, e):
                sp.dma_start(wb[:, e % 4, :], S.w_dram[e:e + 1, bass.ds(c * CH, CH)].to_broadcast([P, CH])
                             ).then_inc(wb_loaded[e % 4], 16)

            for e in range(4):
                load_wb(0, e)

            def turn(c, more):
                for e in range(E):
                    if e < 4 or more:
                        sp.wait_ge(y_empty, c * E + (e + 3))
                        load_wb(c + (e + 4) // E, (e + 4) % E)

            with sp.Fori(0, TOK // CH - 1) as c:
                turn(c, True)
            turn(TOK // CH - 1, False)

        @block.vector
        def _(dve):
            own = Order(nc, ctx, dve, f"{name}_dve")
            logit3 = logit[:]

            def row_max(i, src):
                own.step(nc.vector.tensor_reduce(mx[:, i, :], src[:], AX.X, ALU.max))
                return mx[:, i, :].unsqueeze(2).to_broadcast([P, NT, E])

            def best(i, src, out):
                m = row_max(i, src)
                own.step(nc.vector.tensor_tensor(tie[:], src[:], m, ALU.is_ge))
                own.step(nc.vector.tensor_tensor(tie[:], tie[:], S.falling[:].unsqueeze(1).to_broadcast([P, NT, E]),
                                                 ALU.mult))
                m = row_max(i + 1, tie)
                own.step(nc.vector.tensor_tensor(out[:], tie[:], m, ALU.is_equal))

            dve.wait_ge(gated, 1)
            own.step(nc.vector.tensor_tensor(logit3, gp[:, 0:NT * E].rearrange("p (t e) -> p t e", e=E),
                                             gate_bias.unsqueeze(1).to_broadcast([P, NT, E]), ALU.add))
            if top == 1:
                m = row_max(0, logit)
                nc.vector.tensor_tensor(logit3, logit3, m, ALU.subtract).then_inc(shifted, 1)
                dve.wait_ge(exped, 1)
                best(1, expo, pick)
                own.step(nc.vector.tensor_reduce(mx[:, 3, :], expo[:], AX.X, ALU.add))
                own.step(nc.vector.reciprocal(mx[:, 4, :], mx[:, 3, :]))
                own.step(nc.vector.tensor_tensor(left[:], expo[:],
                                                 mx[:, 4, :].unsqueeze(2).to_broadcast([P, NT, E]), ALU.mult))
                nc.vector.tensor_tensor(w[:], left[:], pick[:], ALU.mult).then_inc(w_ready, 1)
            else:
                best(0, logit, pick)
                own.step(nc.vector.scalar_tensor_tensor(left[:], pick[:], -3e38, logit3, ALU.mult, ALU.add))
                best(2, left, pick2)
                own.step(nc.vector.tensor_tensor(pick[:], pick[:], pick2[:], ALU.add))
                nc.vector.tensor_tensor(w[:], logit3, pick[:], ALU.mult).then_inc(w_ready, 1)
            dve.wait_ge(w_turned, 1)
            nc.vector.tensor_copy(wT[:], yp[:, 0, 0:P]).then_inc(wT_ready, 1)
            nc.vector.memset(total[:], 0.0).then_inc(summed_start, 1)
            dve.wait_ge(summed_start, 1)
            dve.sem_inc(y_empty, 2)
            with dve.Fori(0, TOK // CH) as c:
                for e in range(E):
                    dve.wait_ge(y_full, c * E + (e + 3))
                    dve.wait_ge(wb_loaded[e % 4], c * 32 + (16 + 16 * (e // 4)))
                    nc.vector.tensor_tensor(prod[:, e % 2, :], yp[:, e % 2, :], wb[:, e % 4, :],
                                            ALU.mult).then_inc(y_empty, 1)
                    dve.wait_ge(y_empty, c * E + (e + 3))
                    if e:
                        dve.wait_ge(summed, c * E + e)
                    part = total[:, bass.ds(c * CH, CH)]
                    nc.vector.tensor_tensor(part, part, prod[:, e % 2, :], ALU.add).then_inc(summed, 1)
            for t in range(NT):
                dve.wait_ge(turned, t + 1)
                nc.vector.tensor_tensor(S.x[:, t, :], hp[:, t % HB, 0:P], S.x[:, t, :], ALU.add).then_inc(added, 1)
def linear_phase(nc, S, name, qT, state):
    with nc.cleanup_on_exit(), ExitStack() as ctx:
        sb = lambda n, s, d=F32: ctx.enter_context(nc.sbuf_tensor(f"{name}_{n}", s, d))
        sem = lambda n: nc.alloc_semaphore(f"{name}_{n}")
        z = sb("z", [P, 2, 512])
        low = sb("low", [P, 2, 512])
        expo = sb("expo", [P, 2, 512])
        k = sb("k", [P, NT, P])
        v = sb("v", [P, NT, P + 1])
        ps = ctx.enter_context(nc.psum_tensor(f"{name}_ps", [P, 2, 512], F32))
        pv = ctx.enter_context(nc.psum_tensor(f"{name}_pv", [P, 2, 512], F32))
        kv = ctx.enter_context(nc.psum_tensor(f"{name}_kv", [P, 2, 512], F32))
        proj, z_ready, low_ready, exp_ready, act_ready, v_proj, v_ready, kv_ready = (
            sem(n) for n in ("proj", "z_ready", "low_ready", "exp_ready", "act_ready", "v_proj", "v_ready",
                             "kv_ready"))
        G = NT // 4
        block = ctx.enter_context(nc.Block())

        @block.tensor
        def _(pe):
            for i in range(2 * G):
                if i >= 2:
                    pe.wait_ge(z_ready, i - 1)
                g = i % G
                if i < G:
                    last = nc.tensor.matmul(ps[:, i % 2, :], S.wot[:, 1, :], S.xnT[:, g * 512:(g + 1) * 512],
                                            start=True, stop=True)
                else:
                    for t in range(4):
                        last = nc.tensor.matmul(ps[:, i % 2, t * P:(t + 1) * P],
                                                S.xnT[:, (4 * g + t) * P:(4 * g + t + 1) * P], S.wot[:, 2, :],
                                                start=True, stop=True)
                last.then_inc(proj, 1)
            for g in range(G):
                if g >= 2:
                    pe.wait_ge(v_ready, g)
                for t in range(4):
                    last = nc.tensor.matmul(pv[:, g % 2, t * P:(t + 1) * P],
                                            S.xnT[:, (4 * g + t) * P:(4 * g + t + 1) * P], S.wot[:, 3, :],
                                            start=True, stop=True)
                last.then_inc(v_proj, 1)
            pe.wait_ge(act_ready, 2 * G)
            pe.wait_ge(v_ready, G + 1)
            for b in range(BATCH):
                for t in range(BT):
                    last = nc.tensor.matmul(kv[:, b, 0:P + 1], k[:, b * BT + t, :], v[:, b * BT + t, :],
                                            start=t == 0, stop=t == BT - 1)
                last.then_inc(kv_ready, 1)

        @block.scalar
        def _(act):
            for i in range(2 * G):
                act.wait_ge(low_ready, i + 1)
                if i >= 2:
                    act.wait_ge(act_ready, i - 1)
                nc.scalar.activation(expo[:, i % 2, :], low[:, i % 2, :], ACT.Exp).then_inc(exp_ready, 1)

        @block.vector
        def _(dve):
            own = Order(nc, ctx, dve, f"{name}_dve")
            nc.vector.memset(v[:, :, P:P + 1], 1.0).then_inc(v_ready, 1)

            def front(i):
                dve.wait_ge(proj, i + 1)
                if i >= 2:
                    dve.wait_ge(act_ready, i - 1)
                    dve.wait_ge(exp_ready, i - 1)
                if i < G:
                    nc.vector.tensor_scalar(z[:, i % 2, :], ps[:, i % 2, :], S.b2col[:, 0:1], None,
                                            ALU.add).then_inc(z_ready, 1)
                else:
                    nc.vector.tensor_tensor(z[:, i % 2, :].rearrange("p (t c) -> p t c", c=P),
                                            ps[:, i % 2, :].rearrange("p (t c) -> p t c", c=P),
                                            S.b_row[:, 3, :].unsqueeze(1).to_broadcast([P, 4, P]),
                                            ALU.add).then_inc(z_ready, 1)
                dve.wait_ge(z_ready, i + 1)
                nc.vector.tensor_scalar(low[:, i % 2, :], z[:, i % 2, :], 0.0, None, ALU.min).then_inc(low_ready, 1)

            def back(i):
                dve.wait_ge(exp_ready, i + 1)
                g = i % G
                dst = (qT[:, g * 512:(g + 1) * 512] if i < G
                       else k[:, 4 * g:4 * g + 4, :].rearrange("p t c -> p (t c)"))
                nc.vector.scalar_tensor_tensor(dst, z[:, i % 2, :], 0.0, expo[:, i % 2, :], ALU.max,
                                               ALU.add).then_inc(act_ready, 1)

            for i in range(2 * G):
                front(i)
                if i:
                    back(i - 1)
            back(2 * G - 1)
            for g in range(G):
                dve.wait_ge(v_proj, g + 1)
                nc.vector.tensor_tensor(v[:, 4 * g:4 * g + 4, 0:P],
                                        pv[:, g % 2, :].rearrange("p (t c) -> p t c", c=P),
                                        S.b_row[:, 4, :].unsqueeze(1).to_broadcast([P, 4, P]),
                                        ALU.add).then_inc(v_ready, 1)
            for b in range(BATCH):
                dve.wait_ge(kv_ready, b + 1)
                own.done(nc.vector.tensor_tensor(state[:, b, 0:P], kv[:, b, 0:P], S.same_head[:], ALU.mult))
                own.done(nc.vector.tensor_tensor(state[:, b, P:P + HEADS], S.head_of[:],
                                                 kv[:, b, P:P + 1].to_broadcast([P, HEADS]), ALU.mult))
            own.settle()


FP4 = 16


def fp4_steps(nc, own, src, out, blocks, tmp):
    V = nc.vector
    n = blocks * FP4
    s3 = src.rearrange("p (b k) -> p b k", k=FP4)
    u, acc, cmp_, half, inv, big = (tmp[i] for i in ("u", "acc", "cmp", "half", "inv", "big"))
    u, acc, cmp_ = u[:, 0:n], acc[:, 0:n], cmp_[:, 0:n]
    half, inv, big = half[:, 0:blocks], inv[:, 0:blocks], big[:, 0:blocks]
    own.step(V.tensor_reduce(big, s3, AX.X, ALU.max, apply_absolute_value=True))
    own.step(V.tensor_scalar(big, big, 1.0 / 6.0, 1e-12, ALU.mult, ALU.max))
    own.done(V.reciprocal(inv, big))
    own.step(V.tensor_scalar(half, big, 0.5, None, ALU.mult))
    own.step(V.tensor_tensor(u.rearrange("p (b k) -> p b k", k=FP4), s3,
                             inv.unsqueeze(2).to_broadcast([P, blocks, FP4]), ALU.mult))
    own.step(V.tensor_scalar(u.bitcast(I32), u.bitcast(I32), 0x7FFFFFFF, None, ALU.bitwise_and))
    own.done(V.tensor_scalar(cmp_, u, 1.75, None, ALU.is_gt))
    own.step(V.tensor_scalar(acc, u, 5.0, 2.0, ALU.is_gt, ALU.mult))
    own.step(V.scalar_tensor_tensor(acc, u, 3.5, acc, ALU.is_gt, ALU.add))
    own.step(V.scalar_tensor_tensor(acc, u, 2.5, acc, ALU.is_gt, ALU.add))
    own.step(V.scalar_tensor_tensor(acc, acc, 2.0, cmp_, ALU.mult, ALU.add))
    for mid in (1.25, 0.75, 0.25):
        own.step(V.scalar_tensor_tensor(acc, u, mid, acc, ALU.is_gt, ALU.add))
    own.step(V.tensor_tensor(u.rearrange("p (b k) -> p b k", k=FP4), acc.rearrange("p (b k) -> p b k", k=FP4),
                             half.unsqueeze(2).to_broadcast([P, blocks, FP4]), ALU.mult))
    return V.scalar_tensor_tensor(out.bitcast(I32), src.bitcast(I32), SIGN, u.bitcast(I32),
                                  ALU.bitwise_and, ALU.bitwise_or)


SIGN = -2 ** 31


def fp4_phase(nc, S, name):
    F = 352
    FC = [(0, P), (P, P), (2 * P, F - 2 * P)]
    WB = (6 * P + F) // FP4
    G = 2
    NG = NT // G
    with nc.cleanup_on_exit(), ExitStack() as ctx:
        sb = lambda n, s, d=F32: ctx.enter_context(nc.sbuf_tensor(f"{name}_{n}", s, d))
        sem = lambda n: nc.alloc_semaphore(f"{name}_{n}")
        wq = sb("wq", [P, 6 * P + F])
        wgu = sb("wgu", [P, 2, 3 * P])
        wd = sb("wd", [P, 3, P])
        xq = sb("xq", [P, NT * P])
        xqT = sb("xqT", [P, TOK])
        sil = sb("sil", [P, 2, F])
        h = sb("h", [P, 2, G * F])
        hq = sb("hq", [P, 2, G * F])
        hT = sb("hT", [P, 2, 3, P])
        tmp = {n: sb(n, [P, NT * P]) for n in ("u", "acc", "cmp")}
        tmp.update({n: sb(n, [P, NT * P // FP4]) for n in ("half", "inv", "big")})
        ps = ctx.enter_context(nc.psum_tensor(f"{name}_ps", [P, 2, 2, 512], F32))
        tp = ctx.enter_context(nc.psum_tensor(f"{name}_tp", [P, 2, 512], F32))
        po = ctx.enter_context(nc.psum_tensor(f"{name}_po", [P, 2, 512], F32))
        wq_ready, x_ready, turned, copied, gu, siluted, h_ready, hq_ready, h_turned, h_copied, down, added = (
            sem(n) for n in ("wq_ready", "x_ready", "turned", "copied", "gate_up", "silu", "h_ready",
                             "hq_ready", "h_turned", "h_copied", "down", "added"))
        block = ctx.enter_context(nc.Block())

        @block.tensor
        def _(pe):
            pe.wait_ge(wq_ready, 1)
            for i in range(2):
                for j in range(3):
                    last = nc.tensor.transpose(tp[:, i, j * P:(j + 1) * P], wq[:, (3 * i + j) * P:(3 * i + j + 1) * P],
                                               S.ident[:])
                last.then_inc(turned, 1)
            pe.wait_ge(copied, 1)
            for j, (at, w) in enumerate(FC):
                last = nc.tensor.transpose(tp[0:w, 0, j * P:(j + 1) * P], wq[:, 6 * P + at:6 * P + at + w], S.ident[:])
            last.then_inc(turned, 1)
            pe.wait_ge(x_ready, 1)
            for i in range(NT // 4):
                pe.wait_ge(copied, i + 2)
                for t in range(4):
                    last = nc.tensor.transpose(tp[:, (i + 1) % 2, t * P:(t + 1) * P],
                                               xq[:, (4 * i + t) * P:(4 * i + t + 1) * P], S.ident[:])
                last.then_inc(turned, 1)
            pe.wait_ge(copied, 3 + NT // 4)
            for i in range(NT + 2 * G):
                if i < NT:
                    if i >= 2:
                        pe.wait_ge(h_ready, i - 1)
                    for side in range(2):
                        last = nc.tensor.matmul(ps[:, i % 2, side, 0:F], xqT[:, i * P:(i + 1) * P],
                                                wgu[:, side, 0:F], start=True, stop=True)
                    last.then_inc(gu, 1)
                t = i - 2 * G
                if t >= 0:
                    pe.wait_ge(hq_ready, t // G + 1)
                    if t >= 2:
                        pe.wait_ge(h_copied, t - 1)
                    for j, (at, w) in enumerate(FC):
                        o = (t % G) * F + at
                        last = nc.tensor.transpose(tp[0:w, t % 2, j * P:(j + 1) * P],
                                                   hq[:, t // G % 2, o:o + w], S.ident[:])
                    last.then_inc(h_turned, 1)
                    pe.wait_ge(h_copied, t + 1)
                    if t >= 2:
                        pe.wait_ge(added, t - 1)
                    for j, (at, w) in enumerate(FC):
                        last = nc.tensor.matmul(po[:, t % 2, 0:P], hT[0:w, t % 2, j, :], wd[0:w, j, :],
                                                start=j == 0, stop=j == 2)
                    last.then_inc(down, 1)

        @block.scalar
        def _(act):
            for i in range(2):
                act.wait_ge(turned, i + 1)
                nc.scalar.copy(wgu[:, i, :], tp[:, i, 0:3 * P]).then_inc(copied, 1)
            act.wait_ge(turned, 3)
            nc.scalar.copy(wd[0:FC[2][1], :, :].rearrange("p j c -> p (j c)"), tp[0:FC[2][1], 0, 0:3 * P])
            nc.scalar.copy(wd[FC[2][1]:P, 0:2, :].rearrange("p j c -> p (j c)"),
                           tp[FC[2][1]:P, 0, 0:2 * P]).then_inc(copied, 1)
            for i in range(NT // 4):
                act.wait_ge(turned, 4 + i)
                nc.scalar.copy(xqT[:, i * 512:(i + 1) * 512], tp[:, (i + 1) % 2, :]).then_inc(copied, 1)
            for i in range(NT + 2 * G):
                if i < NT:
                    act.wait_ge(gu, i + 1)
                    if i >= 2:
                        act.wait_ge(h_ready, i - 1)
                    nc.scalar.activation(sil[:, i % 2, :], ps[:, i % 2, 0, 0:F], ACT.Silu).then_inc(siluted, 1)
                t = i - 2 * G
                if t >= 0:
                    act.wait_ge(h_turned, t + 1)
                    if t >= 2:
                        act.wait_ge(down, t - 1)
                    nc.scalar.copy(hT[0:FC[2][1], t % 2, :, :].rearrange("p j c -> p (j c)"),
                                   tp[0:FC[2][1], t % 2, 0:3 * P])
                    nc.scalar.copy(hT[FC[2][1]:P, t % 2, 0:2, :].rearrange("p j c -> p (j c)"),
                                   tp[FC[2][1]:P, t % 2, 0:2 * P]).then_inc(h_copied, 1)
            act.wait_ge(h_copied, NT)

        @block.vector
        def _(dve):
            own = Order(nc, ctx, dve, f"{name}_dve")
            fp4_steps(nc, own, S.wfp[:], wq[:], WB, tmp).then_inc(wq_ready, 1)
            dve.wait_ge(wq_ready, 1)
            fp4_steps(nc, own, S.xn[:].rearrange("p t c -> p (t c)"), xq[:], NT * P // FP4, tmp).then_inc(x_ready, 1)
            dve.wait_ge(x_ready, 1)

            def add(t):
                dve.wait_ge(down, t + 1)
                nc.vector.tensor_tensor(S.x[:, t, :], po[:, t % 2, 0:P], S.x[:, t, :], ALU.add).then_inc(added, 1)

            for g in range(NG):
                for t in range(G * g, G * g + G):
                    dve.wait_ge(siluted, t + 1)
                    if g >= 2:
                        dve.wait_ge(hq_ready, g - 1)
                    nc.vector.tensor_tensor(h[:, g % 2, (t % G) * F:(t % G + 1) * F], sil[:, t % 2, :],
                                            ps[:, t % 2, 1, 0:F], ALU.mult).then_inc(h_ready, 1)
                dve.wait_ge(h_ready, G * (g + 1))
                if g >= 2:
                    dve.wait_ge(h_turned, G * (g - 1))
                fp4_steps(nc, own, h[:, g % 2, :], hq[:, g % 2, :], G * F // FP4, tmp).then_inc(hq_ready, 1)
                dve.wait_ge(hq_ready, g + 1)
                if g >= 2:
                    for t in range(G * (g - 2), G * (g - 1)):
                        add(t)
            for t in range(G * (NG - 2), NT):
                add(t)
GROUP = 32
HIDDEN = 2 * P


def renorm_phase(nc, S, name):
    with nc.cleanup_on_exit(), ExitStack() as ctx:
        sb = lambda n, s, d=F32: ctx.enter_context(nc.sbuf_tensor(f"{name}_{n}", s, d))
        sem = lambda n: nc.alloc_semaphore(f"{name}_{n}")
        stats = sb("stats", [P, NT, 6])
        mv = sb("mv", [P, NT, 2])
        std = sb("std", [P, NT])
        rstd = sb("rstd", [P, NT])
        eps = sb("eps", [P, 1])
        z = sb("z", [P, NT, P])
        zw = sb("zw", [P, NT, P])
        zg = sb("zg", [P, NT, P])
        tp = ctx.enter_context(nc.psum_tensor(f"{name}_tp", [P, 4, 4, P], F32))
        var_ready, std_ready, z_ready, zw_ready, side, turned, copied = (
            sem(n) for n in ("var_ready", "std_ready", "z_ready", "zw_ready", "side", "turned", "copied"))
        block = ctx.enter_context(nc.Block())
        row = lambda i: S.row3[:, i, :].unsqueeze(1).to_broadcast([P, 4, P])

        @block.vector
        def _(dve):
            own = Order(nc, ctx, dve, f"{name}_dve")
            own.done(nc.vector.memset(eps[:], LN_EPS))
            for t in range(NT):
                own.done(nc.vector.bn_stats(stats[:, t, :], S.xn[:, t, :]))
            own.settle()
            for t in range(NT):
                last = nc.vector.bn_aggr(mv[:, t, :], stats[:, t, :])
            last.then_inc(var_ready, 1)
            dve.wait_ge(std_ready, 1)
            own.step(nc.vector.reciprocal(rstd[:], std[:]))
            for t in range(NT):
                nc.vector.tensor_scalar(z[:, t, :], S.xn[:, t, :], mv[:, t, 0:1], rstd[:, t:t + 1],
                                        ALU.subtract, ALU.mult).then_inc(z_ready, 1)
            for g in range(NT // 4):
                s = slice(4 * g, 4 * g + 4)
                dve.wait_ge(z_ready, 4 * g + 4)
                own.step(nc.vector.tensor_tensor(zw[:, s], z[:, s], row(0), ALU.mult))
                nc.vector.tensor_tensor(zw[:, s], zw[:, s], row(1), ALU.add).then_inc(zw_ready, 1)
            for g in range(NT // 4):
                s = slice(4 * g, 4 * g + 4)
                dve.wait_ge(side, 3 * g + 3)
                own.step(nc.vector.tensor_tensor(S.x[:, s], S.x[:, s], S.xn[:, s], ALU.add))
                own.step(nc.vector.tensor_tensor(S.x[:, s], S.x[:, s], zg[:, s], ALU.add))

        @block.gpsimd
        def _(pool):
            for g in range(NT // 4):
                s = slice(4 * g, 4 * g + 4)
                pool.wait_ge(z_ready, 4 * g + 4)
                for i, op in ((2, ALU.mult), (3, ALU.add), (4, ALU.add)):
                    src = z[:, s] if i == 2 else zg[:, s]
                    nc.gpsimd.tensor_tensor(zg[:, s], src, row(i), op).then_inc(side, 1)
                    pool.wait_ge(side, 3 * g + i - 1)

        @block.scalar
        def _(act):
            act.wait_ge(var_ready, 1)
            nc.scalar.activation(std[:], mv[:, :, 1], ACT.Sqrt, bias=eps[:]).then_inc(std_ready, 1)
            for g in range(NT // 4):
                act.wait_ge(turned, g + 1)
                nc.scalar.copy(S.xnT[:, g * 512:(g + 1) * 512],
                               tp[:, g].rearrange("p a b -> p (a b)")).then_inc(copied, 1)
            act.wait_ge(copied, NT // 4)

        @block.tensor
        def _(pe):
            for g in range(NT // 4):
                pe.wait_ge(zw_ready, g + 1)
                for t in range(4):
                    last = nc.tensor.transpose(tp[:, g, t, :], zw[:, 4 * g + t, :], S.ident[:])
                last.then_inc(turned, 1)


def gau_phase(nc, S, name):
    with nc.cleanup_on_exit(), ExitStack() as ctx:
        sb = lambda n, s, d=F32: ctx.enter_context(nc.sbuf_tensor(f"{name}_{n}", s, d))
        sem = lambda n: nc.alloc_semaphore(f"{name}_{n}")
        pre = sb("pre", [P, 2, 512])
        hv = sb("hv", [P, NT, 4 * P])
        qk = sb("qk", [P, 2, 512])
        quad_q, lin_q, quad_k, lin_k = (sb(n, [P, TOK]) for n in ("quad_q", "lin_q", "quad_k", "lin_k"))
        lin_kt = sb("lin_kt", [P, NT, P])
        sim = sb("sim", [P, 2, P])
        sq = sb("sq", [P, 2, P])
        lin = sb("lin", [P, 2, P])
        amat = sb("amat", [P, 2, P])
        state = sb("state", [P, 2, HIDDEN])
        gated = sb("gated", [P, 2, HIDDEN])
        gT = sb("gT", [P, 2, HIDDEN])
        biasT = sb("biasT", [P, P])
        b_rev = sb("b_rev", [P, P])
        row = sb("row", [1, 2 * P])
        ps = ctx.enter_context(nc.psum_tensor(f"{name}_ps", [P, 2, 512], F32))
        pa = ctx.enter_context(nc.psum_tensor(f"{name}_pa", [P, 2, 512], F32))
        pst = ctx.enter_context(nc.psum_tensor(f"{name}_pst", [P, 512], F32))
        po = ctx.enter_context(nc.psum_tensor(f"{name}_po", [P, 512], F32))
        pg = ctx.enter_context(nc.psum_tensor(f"{name}_pg", [P, 2, 512], F32))
        (row_full, row_ready, row_stored, rev_loaded, rev_full, bias_ready, h_full, pre_ready, hv_ready, qk_full, qk_ready,
         aff_ready, kt_full, kt_ready, a_full, parts_ready, a_ready, st_full, st_ready, o_full, gated_ready, g_full,
         gT_ready, p_full, added) = (
            sem(n) for n in ("row_full", "row_ready", "row_stored", "rev_loaded", "rev_full", "bias_ready", "h_full",
                             "pre_ready", "hv_ready", "qk_full", "qk_ready", "aff_ready", "kt_full", "kt_ready",
                             "a_full", "parts_ready", "a_ready", "st_full", "st_ready", "o_full", "gated_ready",
                             "g_full", "gT_ready", "p_full", "added"))
        G = NT // 4
        affine = ((quad_q, 0), (lin_q, 1), (quad_k, 2), (lin_k, 3))
        block = ctx.enter_context(nc.Block())

        @block.sync
        def _(sp):
            sp.wait_ge(row_ready, 1)
            sp.dma_start(S.row3_dram, row[:]).then_inc(row_stored, 16)
            sp.wait_ge(row_stored, 16)
            sp.dma_start(b_rev[:], bass.AP(S.row3_dram.tensor, 0, [[1, P], [1, P]])).then_inc(rev_loaded, 16)

        @block.tensor
        def _(pe):
            nc.tensor.matmul(po[0:1, 0:2 * P], S.rel3[:], S.table3[:], start=True, stop=True).then_inc(row_full, 1)
            for g in range(G):
                if g >= 2:
                    pe.wait_ge(qk_ready, g - 1)
                nc.tensor.matmul(pg[:, g % 2, :], S.wqk3[:], S.xnT[:, g * 512:(g + 1) * 512], start=True,
                                 stop=True).then_inc(qk_full, 1)
            for t in range(NT):
                if t >= 2:
                    pe.wait_ge(pre_ready, t - 1)
                nc.tensor.matmul(ps[:, t % 2, :], S.xnT[:, t * P:(t + 1) * P], S.wh3[:], start=True,
                                 stop=True).then_inc(h_full, 1)
            pe.wait_ge(rev_loaded, 16)
            pe.wait_ge(row_ready, 1)
            nc.tensor.matmul(po[:, 0:P], S.anti32[:], b_rev[:], start=True, stop=True).then_inc(rev_full, 1)
            pe.wait_ge(aff_ready, 4 * G)
            pe.wait_ge(qk_ready, G)
            for g in range(G):
                if g >= 2:
                    pe.wait_ge(kt_ready, g - 1)
                for t in range(4):
                    last = nc.tensor.transpose(pg[:, g % 2, t * P:(t + 1) * P],
                                               lin_k[:, (4 * g + t) * P:(4 * g + t + 1) * P], S.ident[:])
                last.then_inc(kt_full, 1)
            pe.wait_ge(kt_ready, G)
            pe.wait_ge(hv_ready, NT)

            def square(t):
                if t >= 2:
                    pe.wait_ge(a_ready, t - 1)
                c = slice(t * P, (t + 1) * P)
                nc.tensor.matmul(pa[:, t % 2, 0:P], quad_k[:, c], quad_q[:, c], start=True, stop=True)
                nc.tensor.matmul(pa[:, t % 2, P:2 * P], lin_k[:, c], lin_q[:, c], start=True,
                                 stop=True).then_inc(a_full, 1)

            def out(t):
                b0 = t % BT == 0
                if t % BT < BT - 1:
                    if not b0 or t:
                        pe.wait_ge(st_ready, t - t // BT)
                    nc.tensor.matmul(pst[:, 0:HIDDEN], lin_kt[:, t, :], hv[:, t, 0:HIDDEN], start=b0,
                                     stop=t % BT == BT - 2, skip_group_check=True).then_inc(st_full, 1)
                pe.wait_ge(a_ready, t + 1)
                if t:
                    pe.wait_ge(gated_ready, t)
                nc.tensor.matmul(po[:, 0:HIDDEN], amat[:, t % 2, :], hv[:, t, 0:HIDDEN], start=True, stop=b0
                                 ) if not b0 else nc.tensor.matmul(
                    po[:, 0:HIDDEN], amat[:, t % 2, :], hv[:, t, 0:HIDDEN], start=True, stop=True
                    ).then_inc(o_full, 1)
                if not b0:
                    n = t - t // BT
                    pe.wait_ge(st_ready, n)
                    nc.tensor.matmul(po[:, 0:HIDDEN], lin_q[:, t * P:(t + 1) * P], state[:, (n - 1) % 2, :],
                                     start=False, stop=True).then_inc(o_full, 1)

            def project(t):
                pe.wait_ge(gated_ready, t + 1)
                if t >= 2:
                    pe.wait_ge(gT_ready, t - 1)
                    pe.wait_ge(added, t - 1)
                for j in range(2):
                    last = nc.tensor.transpose(pg[:, t % 2, j * P:(j + 1) * P], gated[:, t % 2, j * P:(j + 1) * P],
                                               S.ident[:])
                last.then_inc(g_full, 1)
                pe.wait_ge(gT_ready, t + 1)
                for j in range(2):
                    last = nc.tensor.matmul(pg[:, t % 2, HIDDEN:HIDDEN + P], gT[:, t % 2, j * P:(j + 1) * P],
                                            S.wo3[:, j, :], start=j == 0, stop=j == 1)
                last.then_inc(p_full, 1)

            square(0)
            for t in range(NT + 1):
                if t + 1 < NT:
                    square(t + 1)
                if t < NT:
                    out(t)
                if t:
                    project(t - 1)

        @block.scalar
        def _(act):
            for g in range(G):
                act.wait_ge(qk_full, g + 1)
                if g >= 2:
                    act.wait_ge(aff_ready, 4 * (g - 1))
                nc.scalar.activation(qk[:, g % 2, :], pg[:, g % 2, :], ACT.Silu, bias=S.col3[:, 0:1]
                                     ).then_inc(qk_ready, 1)
            for t in range(NT):
                act.wait_ge(pre_ready, t + 1)
                nc.scalar.activation(hv[:, t, :], pre[:, t % 2, :], ACT.Silu).then_inc(hv_ready, 1)
            for g in range(G):
                act.wait_ge(kt_full, g + 1)
                nc.scalar.copy(lin_kt[:, 4 * g:4 * g + 4, :].rearrange("p t c -> p (t c)"), pg[:, g % 2, :]
                               ).then_inc(kt_ready, 1)
            for t in range(NT + 1):
                if t < NT and t % BT < BT - 1:
                    n = t - t // BT
                    act.wait_ge(st_full, n + 1)
                    if n >= 2:
                        act.wait_ge(o_full, t)
                    nc.scalar.copy(state[:, n % 2, :], pst[:, 0:HIDDEN]).then_inc(st_ready, 1)
                if t:
                    act.wait_ge(g_full, t)
                    if t >= 3:
                        act.wait_ge(p_full, t - 2)
                    nc.scalar.copy(gT[:, (t - 1) % 2, :], pg[:, (t - 1) % 2, 0:HIDDEN]).then_inc(gT_ready, 1)

        @block.vector
        def _(dve):
            own = Order(nc, ctx, dve, f"{name}_dve")
            dve.wait_ge(row_full, 1)
            nc.vector.tensor_copy(row[:], po[0:1, 0:2 * P]).then_inc(row_ready, 1)
            for g in range(G):
                dve.wait_ge(qk_ready, g + 1)
                for dst, i in affine:
                    nc.vector.tensor_scalar(dst[:, g * 512:(g + 1) * 512], qk[:, g % 2, :], S.aff3[:, i:i + 1],
                                            S.aff3[:, 4 + i:5 + i], ALU.mult, ALU.add).then_inc(aff_ready, 1)
            for t in range(NT):
                dve.wait_ge(h_full, t + 1)
                if t >= 2:
                    dve.wait_ge(hv_ready, t - 1)
                nc.vector.tensor_tensor(pre[:, t % 2, :], ps[:, t % 2, :], S.bh3[:], ALU.add).then_inc(pre_ready, 1)
            dve.wait_ge(rev_full, 1)
            own.step(nc.vector.tensor_tensor(biasT[:], po[:, 0:P], S.quad_mask[:, 0, :], ALU.mult))
            nc.vector.tensor_tensor(biasT[:], biasT[:], S.quad_mask[:, 1, :], ALU.add).then_inc(bias_ready, 1)
            dve.wait_ge(bias_ready, 1)

            def weights(t):
                s = t % 2
                dve.wait_ge(a_full, t + 1)
                own.done(nc.vector.tensor_tensor(sim[:, s, :], pa[:, s, 0:P], biasT[:], ALU.add))
                own.step(nc.vector.tensor_tensor(lin[:, s, :], pa[:, s, P:2 * P], S.lin_mask[:], ALU.mult))
                own.step(nc.vector.scalar_tensor_tensor(sq[:, s, :], sim[:, s, :], 0.0, sim[:, s, :], ALU.max,
                                                        ALU.mult))
                if t >= 2:
                    dve.wait_ge(o_full, t - 1)
                nc.vector.tensor_tensor(amat[:, s, :], sq[:, s, :], lin[:, s, :], ALU.add).then_inc(a_ready, 1)

            def add(t):
                dve.wait_ge(p_full, t + 1)
                nc.vector.tensor_tensor(S.x[:, t, :], pg[:, t % 2, HIDDEN:HIDDEN + P], S.x[:, t, :],
                                        ALU.add).then_inc(added, 1)

            weights(0)
            for t in range(NT + 1):
                if t + 1 < NT:
                    weights(t + 1)
                if t < NT:
                    dve.wait_ge(o_full, t + 1)
                    if t >= 2:
                        dve.wait_ge(g_full, t - 1)
                    nc.vector.tensor_tensor(gated[:, t % 2, :], po[:, 0:HIDDEN], hv[:, t, HIDDEN:2 * HIDDEN],
                                            ALU.mult).then_inc(gated_ready, 1)
                if t:
                    add(t - 1)
def buckets():
    dist = np.arange(-(P - 1), NEAR + 1)
    bucket = bucket_of(dist)
    table = np.zeros((BUCKETS + 1, len(dist)), np.float32)
    table[bucket, np.arange(len(dist))] = 1.0
    table[BUCKETS - 1] -= 1.0
    table[:, dist < 0] = 0.0
    table[BUCKETS, dist < 0] = NEG
    return table


def bucket_of(dist):
    half = BUCKETS // 2
    far = half + (np.log(np.maximum(dist, 1).astype(np.float32) / np.float32(half)) / np.float32(np.log(8.0))
                  * half).astype(np.int32)
    return np.where(dist < half, np.maximum(dist, 0), np.minimum(far, BUCKETS - 1))


def buckets3():
    table = np.zeros((BUCKETS, 2 * P), np.float32)
    dist = np.arange(2 * P) - (P - 1)
    table[bucket_of(dist), np.arange(2 * P)] = np.float32(np.sqrt(P))
    return table


def group_masks():
    i = np.arange(P)
    same = (i[:, None] // GROUP == i[None, :] // GROUP) & (i[:, None] <= i[None, :])
    earlier = i[:, None] // GROUP < i[None, :] // GROUP
    quad = np.stack([same.astype(np.float32), np.where(same, 0.0, NEG).astype(np.float32)], axis=1)
    return np.ascontiguousarray(quad), earlier.astype(np.float32)


class Store:
    pass


def setup_phase(nc, S, I):
    with nc.cleanup_on_exit(), ExitStack() as ctx:
        sb = lambda n, s, d=F32: ctx.enter_context(nc.sbuf_tensor(f"setup_{n}", s, d))
        sem = lambda n: nc.alloc_semaphore(f"setup_{n}")
        tall = sb("tall", [P, 3, HD])
        small = sb("small", [P, 3, P])
        ones_row = sb("ones_row", [2, SEQ], BF16)
        wo = sb("wo", [P, 5, P])
        b1 = sb("b1", [5 * EXPERTS, P])
        aff_rows = sb("aff_rows", [8, P])
        table = sb("table", [BUCKETS + 1, P + NEAR])
        rel = sb("rel", [BUCKETS + 1, HEADS])
        brow = sb("brow", [HEADS, P + NEAR])
        brow2 = sb("brow2", [HEADS, P + NEAR])
        bparts = sb("bparts", [HEADS, PARTS, P + NEAR], BF16)
        ps = ctx.enter_context(nc.psum_tensor("setup_ps", [P, 8, 512], F32))
        consts, first, blocks, blocked, rest, zeroed, ones_set, ones_loaded, turned, copied, stored, rel_ready = (
            sem(n) for n in ("consts", "first", "blocks", "blocked", "rest", "zeroed", "ones_set",
                             "ones_loaded", "turned", "copied", "stored", "rel"))
        block = ctx.enter_context(nc.Block())
        W = P + NEAR
        small_names = ("L0_attn_Wq", "L0_attn_Wk", "L0_attn_Wv")
        square = ("L0_attn_Wo", "L2_attn_Wq", "L2_attn_Wk", "L2_attn_Wv", "L2_attn_Wo")
        loads = [
            (S.wa1[:], I["L1_attn_W_attn"]),
            (S.wp1[:], I["L1_attn_W_proj"]),
            (S.b_row[:, 0, :], rows_bcast(I["L0_attn_bo"], P)),
            (S.b_row[:, 1, :], rows_bcast(I["L1_attn_b_proj"], P)),
            (S.b_row[:, 2, :], rows_bcast(I["L1_attn_b_attn"][2 * P:3 * P], P)),
            (S.bqk_raw[:, 0:1], column(I["L1_attn_b_attn"][0:P])),
            (S.bqk_raw[:, 1:2], column(I["L1_attn_b_attn"][P:2 * P])),
            (S.gate_w[:, 0, :], I["L0_ffn_w_gate"]),
            (S.gate_w[:, 1, :], I["L1_ffn_W_gate"]),
            (S.gate_b[:, 0, :], rows_bcast(I["L0_ffn_b_gate"], P)),
            (S.gate_b[:, 1, :], rows_bcast(I["L1_ffn_b_gate"], P)),
            (S.w1_0[:], I["L0_ffn_W1"].rearrange("e c m -> c e m")),
            (S.w2_0[:], I["L0_ffn_W2"].rearrange("e (m p) d -> p e m d", p=P)),
            (S.w1_1[:], I["L1_ffn_W1"].rearrange("e c m -> c e m")),
            (S.w2_1[:, :, 0, :], I["L1_ffn_W2"].rearrange("e c m -> c e m")),
            (S.b2_0[:], I["L0_ffn_b2"]),
            (S.b2_1[:], I["L1_ffn_b2"]),
            (b1[0:4 * EXPERTS, :], I["L0_ffn_b1"].rearrange("e (m p) -> (e m) p", p=P)),
            (b1[4 * EXPERTS:5 * EXPERTS, :], I["L1_ffn_b1"]),
            (S.same_head[:], I["same_head"]),
            (S.quad_mask[:], I["quad_mask"]),
            (S.lin_mask[:], I["lin_mask"]),
            (S.table3[:], I["buckets3"]),
            (S.rel3[:], column(I["L3_attn_rel_table"])),
            (S.wh3[:], I["L3_attn_Wh"]),
            (S.wqk3[:], I["L3_attn_Wqk"]),
            (S.wo3[:], I["L3_attn_Wout"].rearrange("(j p) c -> p j c", p=P)),
            (S.bh3[:], rows_bcast(I["L3_attn_bh"], P)),
            (S.col3[:], column(I["L3_attn_bqk"])),
            (S.row3[:, 0, :], rows_bcast(I["L3_attn_ln_w"], P)),
            (S.row3[:, 1, :], rows_bcast(I["L3_attn_ln_b"], P)),
            (S.row3[:, 2, :], rows_bcast(I["L3_ffn_ln_g"], P)),
            (S.row3[:, 3, :], rows_bcast(I["L3_ffn_ln_b"], P)),
            (S.row3[:, 4, :], rows_bcast(I["L3_attn_bout"], P)),
            (aff_rows[0:4, :], I["L3_attn_qk_w"]),
            (aff_rows[4:8, :], I["L3_attn_qk_b"]),
            (S.head_of[:], I["head_of"]),
            (S.b2col[:, 0:1], column(I["L2_attn_bq"])),
            (S.b_row[:, 3, :], rows_bcast(I["L2_attn_bk"], P)),
            (S.b_row[:, 4, :], rows_bcast(I["L2_attn_bv"], P)),
            (S.b_row[:, 5, :], rows_bcast(I["L2_attn_bo"], P)),
            (S.wfp[:, 6 * P:6 * P + 352], I["L2_ffn_w_down"]),
        ] + [(wo[:, i, :], I[n]) for i, n in enumerate(square)]
        for i, n in enumerate(("L2_ffn_w_gate", "L2_ffn_w_up")):
            loads += [(S.wfp[:, (3 * i + j) * P:(3 * i + j + 1) * P], I[n][j * P:(j + 1) * P]) for j in range(2)]
            loads.append((S.wfp[0:352 - 2 * P, (3 * i + 2) * P:(3 * i + 3) * P], I[n][2 * P:352]))

        @block.sync
        def _(sp):
            sp.dma_start(S.ident[:], I["ident"]).then_inc(consts, 16)
            sp.dma_start(S.anti32[:], I["anti"]).then_inc(consts, 16)
            sp.dma_start(table[:], I["buckets"]).then_inc(consts, 16)
            sp.dma_start(rel[0:BUCKETS, :], I["L1_attn_bias_table"]).then_inc(consts, 16)
            sp.dma_start(S.x[:], I["L0_attn_X"].rearrange("b (t p) c -> p (b t) c", p=P)).then_inc(first, 16)
            for i, n in enumerate(small_names):
                sp.dma_start(tall[:, i, :], bass.AP(I[n].tensor, I[n].offset, [[0, HEADS], [HD, HD], [1, HD]])
                             ).then_inc(blocks, 16)
            for dst, src in loads:
                sp.dma_start(dst, src).then_inc(rest, 16)
            sp.wait_ge(consts, 64)
            sp.wait_ge(blocks, 48)
            sp.wait_ge(first, 16)
            sp.wait_ge(rest, 16 * len(loads))
            sp.wait_ge(rel_ready, 6)
            for copy in range(BATCH):
                sp.dma_start(S.trow.ap()[copy * HEADS:(copy + 1) * HEADS], bparts[:]).then_inc(stored, 16)
            sp.wait_ge(stored, 16 * BATCH)

        @block.gpsimd
        def _(pool):
            nc.gpsimd.memset(ones_row[:], 1.0).then_inc(ones_set, 1)
            for t in (S.a_still, S.a_moving, S.b_moving, S.b_still):
                last = nc.gpsimd.memset(t[:], 0.0)
            last.then_inc(zeroed, 1)

        @block.scalar
        def _(act):
            act.wait_ge(ones_set, 1)
            act.wait_ge(zeroed, 1)
            for jj in range(2):
                for buf in range(2):
                    for pr in range(2):
                        act.dma_start(S.b_still[64 * jj + ROWS:64 * jj + SROWS, buf, pr, jj, :],
                                      ones_row[:]).then_inc(ones_loaded, 16)
            act.wait_ge(ones_loaded, 16 * 8)

        @block.vector
        def _(dve):
            for i in range(2):
                nc.vector.memset(S.wfp[352 - 2 * P:P, (3 * i + 2) * P:(3 * i + 3) * P], 0.0)
            nc.vector.memset(rel[BUCKETS:BUCKETS + 1, :], 1.0).then_inc(rel_ready, 1)
            dve.wait_ge(consts, 64)
            nc.vector.tensor_copy(S.anti[:], S.anti32[:])
            dve.wait_ge(rest, 16 * len(loads))
            dve.wait_ge(blocks, 48)
            for i in range(3):
                last = nc.vector.tensor_tensor(small[:, i, :].rearrange("p (h d) -> p h d", d=HD),
                                               tall[:, i, :].unsqueeze(1).to_broadcast([P, HEADS, HD]),
                                               S.same_head[:].rearrange("p (h d) -> p h d", d=HD), ALU.mult)
            last.then_inc(blocked, 1)
            nc.vector.tensor_scalar(S.bqk[:, 0:1], S.bqk_raw[:, 0:1], 1.0 / np.sqrt(HD), None, ALU.mult)
            nc.vector.tensor_copy(S.bqk[:, 1:2], S.bqk_raw[:, 1:2])
            dve.wait_ge(turned, 1)
            nc.vector.tensor_copy(brow[:], ps[0:HEADS, 0, 0:W]).then_inc(rel_ready, 1)
            dve.wait_ge(rel_ready, 2)
            nc.vector.tensor_copy(bparts[:, 0, :], brow[:]).then_inc(rel_ready, 1)
            dve.wait_ge(rel_ready, 3)
            nc.vector.tensor_tensor(brow2[:], brow[:], bparts[:, 0, :], ALU.subtract).then_inc(rel_ready, 1)
            dve.wait_ge(rel_ready, 4)
            nc.vector.tensor_copy(bparts[:, 1, :], brow2[:]).then_inc(rel_ready, 1)
            dve.wait_ge(rel_ready, 5)
            nc.vector.tensor_tensor(bparts[:, 2, :], brow2[:], bparts[:, 1, :], ALU.subtract).then_inc(rel_ready, 1)
            dve.wait_ge(turned, 2)
            nc.vector.tensor_copy(S.wt0[:], ps[:, 1:4, 0:P])
            nc.vector.tensor_copy(S.wot[:], ps[:, 4:8, 0:P]).then_inc(copied, 1)
            dve.wait_ge(turned, 3)
            for e in range(EXPERTS):
                nc.vector.memset(S.falling[:, e:e + 1], float(EXPERTS - e))
            for at, scale in ((0, 1.0), (2, 1.0 / GROUP), (4, 1.0), (6, 1.0 / GROUP)):
                nc.vector.tensor_scalar(S.aff3[:, at:at + 2], ps[:, 0, 2 * P + at:2 * P + at + 2], scale, None,
                                        ALU.mult)
            nc.vector.tensor_copy(S.b1[:], ps[:, 0, P:P + 5 * EXPERTS])
            nc.vector.tensor_copy(S.wot4[:], ps[:, 0, 0:P]).then_inc(copied, 1)
            dve.wait_ge(copied, 2)

        @block.tensor
        def _(pe):
            pe.wait_ge(consts, 64)
            pe.wait_ge(rel_ready, 1)
            nc.tensor.matmul(ps[0:HEADS, 0, 0:W], rel[:], table[:], start=True, stop=True).then_inc(turned, 1)
            pe.wait_ge(blocked, 1)
            pe.wait_ge(rest, 16 * len(loads))
            for i in range(3):
                nc.tensor.transpose(ps[:, 1 + i, 0:P], small[:, i, :], S.ident[:])
            for i in range(4):
                last = nc.tensor.transpose(ps[:, 4 + i, 0:P], wo[:, i, :], S.ident[:])
            last.then_inc(turned, 1)
            pe.wait_ge(rel_ready, 2)
            nc.tensor.transpose(ps[:, 0, 0:P], wo[:, 4, :], S.ident[:])
            nc.tensor.transpose(ps[:, 0, 2 * P:2 * P + 8], aff_rows[:], S.ident[0:8, 0:8])
            nc.tensor.transpose(ps[:, 0, P:P + 5 * EXPERTS], b1[:], S.ident[0:5 * EXPERTS, 0:5 * EXPERTS]
                                ).then_inc(turned, 1)


def network(nc, I, out, layers=(0, 1, 2, 3)):
    with ExitStack() as ctx:
        sb = lambda n, s, d=F32: ctx.enter_context(nc.sbuf_tensor(n, s, d))
        S = Store()
        S.x = sb("x", [P, NT, P])
        S.xn = sb("xn", [P, NT, P])
        S.xnT = sb("xnT", [P, TOK])
        S.ident = sb("ident", [P, P])
        S.anti32 = sb("anti32", [P, P])
        S.anti = sb("anti", [P, P], BF16)
        S.b_row = sb("b_row", [P, 6, P])
        S.b2col = sb("b2col", [P, 1])
        S.same_head = sb("same_head", [P, P])
        S.head_of = sb("head_of", [P, HEADS])
        S.wfp = sb("wfp", [P, 6 * P + 352])
        S.bqk_raw = sb("bqk_raw", [P, 2])
        S.bqk = sb("bqk", [P, 2])
        S.wt0 = sb("wt0", [P, 3, P])
        S.wot = sb("wot", [P, 4, P])
        S.wot4 = sb("wot4", [P, P])
        S.gate_w = sb("gate_w", [P, 2, EXPERTS])
        S.gate_b = sb("gate_b", [P, 2, EXPERTS])
        S.falling = sb("falling", [P, EXPERTS])
        S.b1 = sb("b1", [P, 5 * EXPERTS])
        S.b2_0 = sb("b2_0", [EXPERTS, P])
        S.b2_1 = sb("b2_1", [EXPERTS, P])
        S.w_dram = nc.dram_tensor("w_rows", (EXPERTS, TOK), F32).ap()
        S.quad_mask = sb("quad_mask", [P, 2, P])
        S.lin_mask = sb("lin_mask", [P, P])
        S.table3 = sb("table3", [BUCKETS, 2 * P])
        S.rel3 = sb("rel3", [BUCKETS, 1])
        S.wh3 = sb("wh3", [P, 4 * P])
        S.wqk3 = sb("wqk3", [P, P])
        S.wo3 = sb("wo3", [P, 2, P])
        S.bh3 = sb("bh3", [P, 4 * P])
        S.col3 = sb("col3", [P, 1])
        S.row3 = sb("row3", [P, 5, P])
        S.aff3 = sb("aff3", [P, 8])
        S.row3_dram = nc.dram_tensor("row3_dram", (1, 2 * P), F32).ap()
        S.bv = S.b_row[:, 2, :]
        stack = nc.dram_tensor("stack", (BATCH, P, NP_, 2, SEQ), BF16)
        vstack = nc.dram_tensor("vstack", (BATCH, HEADS, P, BT * VW), F32)
        S.trow = nc.dram_tensor("trow", (BATCH * HEADS, PARTS, P + NEAR), BF16)
        S.stack, S.vstack = stack.ap(), vstack.ap()
        S.stack_heads = S.stack.rearrange("b (h d) n s t -> (b h) (d n) (s t)", h=HEADS)
        S.v_heads = S.vstack.rearrange("b h p c -> (b h) p c")

        def hankel(n, part):
            at = S.trow.ap()[bass.ds(n, 1)].offset
            W = P + NEAR
            if part is None:
                return bass.AP(S.trow, at, [[1, P], [W, PARTS], [1, NEAR]])
            return bass.AP(S.trow, at, [[1, P], [1, NEAR]])

        S.hankel = hankel
        first_half = ctx.enter_context(ExitStack())
        early = lambda n, s, d=F32: first_half.enter_context(nc.sbuf_tensor(n, s, d))
        S.oT = early("oT", [P, NQUAD, SEQ])
        S.a_still = early("a_still", [P, 2, 2, SEQ], BF16)
        S.a_moving = early("a_moving", [P, 2, SEQ], BF16)
        S.b_still = early("b_still", [P, 2, 2, 2, SEQ], BF16)
        S.b_moving = early("b_moving", [P, 2, 2, SEQ], BF16)
        S.wa1 = early("wa1", [P, 3 * P])
        S.wp1 = early("wp1", [P, P])
        S.w1_0 = early("w1_0", [P, EXPERTS, 4 * P])
        S.w2_0 = early("w2_0", [P, EXPERTS, 4, P])
        S.w1_1 = early("w1_1", [P, EXPERTS, P])
        S.w2_1 = early("w2_1", [P, EXPERTS, 1, P])
        S.wqk = [[S.wt0[:, 0, :], S.wt0[:, 1, :]], [S.wa1[:, 0:P], S.wa1[:, P:2 * P]]]
        S.wv = [S.wt0[:, 2, :], S.wa1[:, 2 * P:3 * P]]
        setup_phase(nc, S, I)
        if 0 in layers:
            norm_phase(nc, S, "n0")
            split_phase(nc, S, "s0", 0)
            attention_phase(nc, S, "a0", False)
            project_phase(nc, S, "p0", S.wot[:, 0, :], S.b_row[:, 0, :])
            moe_phase(nc, S, "m0", 1, S.gate_w[:, 0, :], S.gate_b[:, 0, :], S.w1_0, S.b1[:, 0:4 * EXPERTS],
                      S.w2_0, S.b2_0[:])
        if 1 in layers:
            norm_phase(nc, S, "n1")
            split_phase(nc, S, "s1", 1)
            attention_phase(nc, S, "a1", True)
            project_phase(nc, S, "p1", S.wp1[:], S.b_row[:, 1, :])
            moe_phase(nc, S, "m1", 2, S.gate_w[:, 1, :], S.gate_b[:, 1, :], S.w1_1,
                      S.b1[:, 4 * EXPERTS:5 * EXPERTS], S.w2_1, S.b2_1[:])
        first_half.close()
        if 2 in layers:
            norm_phase(nc, S, "n2")
            with nc.sbuf_tensor("q2T", [P, TOK], F32) as qT, nc.sbuf_tensor("state", [P, BATCH, P + HEADS], F32) as st:
                linear_phase(nc, S, "l2", qT, st)
                project_phase(nc, S, "p2", S.wot4[:], S.b_row[:, 5, :], linear=(qT, st))
            fp4_phase(nc, S, "f2")
        if 3 in layers:
            norm_phase(nc, S, "n3")
            renorm_phase(nc, S, "r3")
            gau_phase(nc, S, "g3")
        with nc.semaphore("written") as written, nc.Block() as block:
            @block.sync
            def _(sp):
                sp.dma_start(out.rearrange("b (t p) c -> p (b t) c", p=P), S.x[:]).then_inc(written, 16)
                sp.wait_ge(written, 16)


LAYERS = (0, 1, 2, 3)


def kernel(**inputs):
    import concourse.bacc as bacc
    from concourse.bass_utils import run_bass_kernel_spmd

    nc = bacc.Bacc("TRN2", target_bir_lowering=False, num_devices=1)
    arrays, args = {}, {}
    given = dict(inputs)
    given.pop("L3_ffn_attn_mask")
    given["ident"] = np.eye(P, dtype=np.float32)
    given["anti"] = np.ascontiguousarray(np.eye(P, dtype=np.float32)[::-1])
    given["buckets"] = buckets()
    given["buckets3"] = buckets3()
    given["quad_mask"], given["lin_mask"] = group_masks()
    given["head_of"] = np.ascontiguousarray(np.repeat(np.eye(HEADS, dtype=np.float32), HD, axis=0))
    given["same_head"] = np.ascontiguousarray(np.kron(np.eye(HEADS), np.ones((HD, HD))).astype(np.float32))
    for name, value in given.items():
        a = np.ascontiguousarray(value)
        arrays[f"in_{name}"] = a
        args[name] = nc.dram_tensor(f"in_{name}", a.shape, mybir.dt.from_np(a.dtype), kind="ExternalInput").ap()
    out = nc.dram_tensor("out_x", (BATCH, SEQ, P), F32, kind="ExternalOutput").ap()
    network(nc, args, out, LAYERS)
    r = run_bass_kernel_spmd(nc, [arrays], core_ids=[0])
    return r.results[0]["out_x"]
```
